# Optimizing a Trainium2 kernel written in Bass

```python
import numpy as np
import jax
import jax.numpy as jnp

def _softmax(x, axis=-1):
    return jax.nn.softmax(x, axis=axis)

def _gelu(x):
    return jax.nn.gelu(x, approximate=True)

def _silu(x):
    return jax.nn.silu(x)

def _sigmoid(x):
    return jax.nn.sigmoid(x)

def _layernorm(x, axis=-1, eps=1e-05):
    m = jnp.mean(x, axis=axis, keepdims=True)
    v = jnp.var(x, axis=axis, keepdims=True)
    return (x - m) / jnp.sqrt(v + eps)

def _scatter_add(tgt, idx, src, axis=0):
    return tgt.at[idx].add(src)

def _segment_sum(src, seg, n):
    return jax.ops.segment_sum(src, seg, n)
kernel_name = 'mk_decoder_postln_d1_seqx_r2_bb03a1'

def setup_inputs(seed: int=0):
    np.random.seed(seed)
    _w = jnp.asarray

    def _rec_inputs():
        import jax
        import jax.numpy as jnp
        _rk = jax.random.key(seed)
        x = -0.0002928 + 1 * jax.random.normal(jax.random.fold_in(_rk, 1), (4, 1024, 512), jnp.float32)
        _lenS = 1024 - jax.random.randint(jax.random.fold_in(_rk, 7), (4,), 0, max(1, 1024 // 4) + 1, jnp.int32)
        _lenS2 = 1024 - jax.random.randint(jax.random.fold_in(_rk, 8), (4,), 0, max(1, 1024 // 4) + 1, jnp.int32)
        _ctx_1024P = jax.random.normal(jax.random.fold_in(_rk, 11), (4, 16, 512), jnp.float32)
        _ctx_1024c = jax.random.dirichlet(jax.random.fold_in(_rk, 511), 0.3 * jnp.ones((16,), jnp.float32), (4, 1024))
        _ctx_1024t = jnp.einsum('bsk,bkd->bsd', _ctx_1024c, _ctx_1024P)
        _ctx_1024t = _ctx_1024t * jax.lax.rsqrt(jnp.mean(jnp.square(_ctx_1024t)) + 1e-12) * 0.953939
        ctx_1024 = -1.39393e-06 + 0.999914 * (_ctx_1024t + 0.3 * jax.random.normal(jax.random.fold_in(_rk, 611), (4, 1024, 512), jnp.float32))
        _validS = jnp.arange(1024)[None, :] < _lenS[:, None]
        _validS2 = jnp.arange(1024)[None, :] < _lenS2[:, None]
        _causal = jnp.tril(jnp.ones((1024, 1024), dtype=bool))
        mask_Bx1xSxS2_ik1 = jnp.where(jnp.broadcast_to(_validS2[:, None, None, :], (4, 1, 1024, 1024)), 1, 0).astype(jnp.int32)
        return (x, ctx_1024, mask_Bx1xSxS2_ik1)
    x, ctx_1024, mask_Bx1xSxS2_ik1 = _rec_inputs()

    def _L0_attn_setup():
        import jax, jax.numpy as jnp
        import numpy as np
        NUM_HEADS = 16
        D_MODEL = 512
        HEAD_DIM = D_MODEL // NUM_HEADS
        NEG_INF = -1000000000.0

        def alibi_bidirectional_bias(num_heads, seq_len, dtype=jnp.float32):
            half = num_heads // 2
            base = 24.0 ** (1.0 / half)
            slopes = (1.0 / base ** jnp.arange(1, half + 1, dtype=dtype))[:, None, None]
            pos = jnp.arange(seq_len)
            rel = (pos[None, :] - pos[:, None]).astype(dtype)
            neg = jnp.full((seq_len, seq_len), NEG_INF, dtype=dtype)
            fwd = slopes * jnp.tril(rel) + jnp.triu(neg, 1)
            bwd = slopes * jnp.triu(-rel) + jnp.tril(neg, -1)
            return jnp.concatenate([fwd, bwd], axis=0)
        key = jax.random.key(seed)
        ks = jax.random.split(key, 9)
        B, S, D = (2, 1024, D_MODEL)
        sc = 1.0 / np.sqrt(D)
        inp = {'x': jax.random.normal(ks[0], (B, S, D), dtype=jnp.float32)}
        inp['Wq'] = jax.random.normal(ks[1], (D, D), dtype=jnp.float32) * sc
        inp['bq'] = jnp.zeros((D,), dtype=jnp.float32)
        inp['Wk'] = jax.random.normal(ks[2], (D, D), dtype=jnp.float32) * sc
        inp['bk'] = jnp.zeros((D,), dtype=jnp.float32)
        inp['Wv'] = jax.random.normal(ks[3], (D, D), dtype=jnp.float32) * sc
        inp['bv'] = jnp.zeros((D,), dtype=jnp.float32)
        inp['Wf'] = jax.random.normal(ks[4], (D, D), dtype=jnp.float32) * sc
        inp['bf'] = jnp.zeros((D,), dtype=jnp.float32)
        return inp
    _L0_attn_all = _L0_attn_setup()
    _L0_attn_in = {k: v for k, v in _L0_attn_all.items() if k in ('Wq', 'bq', 'Wk', 'bk', 'Wv', 'bv', 'Wf', 'bf')}
    del _L0_attn_all

    def _L0_xattn_setup():
        import jax, jax.numpy as jnp
        import numpy as np
        B, N, C, H = (2, 1024, 512, 16)
        HD = C // H
        key = jax.random.key(seed)
        kq, kk, kv, km = jax.random.split(key, 4)
        q = jax.random.normal(kq, (B, N, C), dtype=jnp.float32)
        k = jax.random.normal(kk, (B, N, C), dtype=jnp.float32)
        v = jax.random.normal(kv, (B, N, C), dtype=jnp.float32)
        mask = jax.random.randint(km, (B, 1, N, N), 0, 2, dtype=jnp.int32)
        return {'q': q, 'k': k, 'v': v, 'mask': mask}
    _L0_xattn_all = _L0_xattn_setup()
    _L0_xattn_in = {k: v for k, v in _L0_xattn_all.items() if k in ()}
    del _L0_xattn_all

    def _L0_ffn_setup():
        import jax, jax.numpy as jnp
        import numpy as np
        BLOCK = 32
        W_BITS = 4
        ACT_BITS = 16

        def act_qdq(x):
            qmax = 2.0 ** (ACT_BITS - 1) - 1.0
            scale = jnp.maximum(jnp.max(jnp.abs(x)) / qmax, 1e-12)
            return jnp.clip(jnp.round(x / scale), -qmax - 1.0, qmax) * scale

        def fixed_qdq_u16(x):
            scale = 1.0 / 65536.0
            return jnp.clip(jnp.round(x / scale), 0.0, 65535.0) * scale

        def lpbq_dequant(w):
            O, I = w.shape
            qmax = 2.0 ** (W_BITS - 1) - 1.0
            wb = w.reshape(O, I // BLOCK, BLOCK)
            s = jnp.maximum(jnp.max(jnp.abs(wb), axis=-1, keepdims=True) / qmax, 1e-12)
            wq = jnp.clip(jnp.round(wb / s), -qmax - 1.0, qmax) * s
            return wq.reshape(O, I)
        key = jax.random.key(seed)
        k1, k2, k3, k4 = jax.random.split(key, 4)
        B, S, H, I = (2, 2048, 512, 1536)
        x = jax.random.normal(k1, (B, S, H), jnp.float32)
        w_gate = jax.random.normal(k2, (I, H), jnp.float32) * 0.02
        w_up = jax.random.normal(k3, (I, H), jnp.float32) * 0.02
        w_down = jax.random.normal(k4, (H, I), jnp.float32) * 0.02
        return {'x': x, 'w_gate': w_gate, 'w_up': w_up, 'w_down': w_down}
    _L0_ffn_all = _L0_ffn_setup()
    _L0_ffn_in = {k: v for k, v in _L0_ffn_all.items() if k in ('w_gate', 'w_up', 'w_down')}
    del _L0_ffn_all
    return {'x': x, 'ctx_1024': ctx_1024, 'mask_Bx1xSxS2_ik1': mask_Bx1xSxS2_ik1, 'L0_attn_Wq': _L0_attn_in['Wq'], 'L0_attn_bq': _L0_attn_in['bq'], 'L0_attn_Wk': _L0_attn_in['Wk'], 'L0_attn_bk': _L0_attn_in['bk'], 'L0_attn_Wv': _L0_attn_in['Wv'], 'L0_attn_bv': _L0_attn_in['bv'], 'L0_attn_Wf': _L0_attn_in['Wf'], 'L0_attn_bf': _L0_attn_in['bf'], 'L0_ffn_w_gate': _L0_ffn_in['w_gate'], 'L0_ffn_w_up': _L0_ffn_in['w_up'], 'L0_ffn_w_down': _L0_ffn_in['w_down']}

def reference(x, ctx_1024, mask_Bx1xSxS2_ik1, L0_attn_Wq, L0_attn_bq, L0_attn_Wk, L0_attn_bk, L0_attn_Wv, L0_attn_bv, L0_attn_Wf, L0_attn_bf, L0_ffn_w_gate, L0_ffn_w_up, L0_ffn_w_down):
    import jax
    import jax.numpy as jnp

    def _L0_attn_ref(x, Wq, bq, Wk, bk, Wv, bv, Wf, bf):
        import jax, jax.numpy as jnp
        import numpy as np
        NUM_HEADS = 16
        D_MODEL = 512
        HEAD_DIM = D_MODEL // NUM_HEADS
        NEG_INF = -1000000000.0

        def alibi_bidirectional_bias(num_heads, seq_len, dtype=jnp.float32):
            half = num_heads // 2
            base = 24.0 ** (1.0 / half)
            slopes = (1.0 / base ** jnp.arange(1, half + 1, dtype=dtype))[:, None, None]
            pos = jnp.arange(seq_len)
            rel = (pos[None, :] - pos[:, None]).astype(dtype)
            neg = jnp.full((seq_len, seq_len), NEG_INF, dtype=dtype)
            fwd = slopes * jnp.tril(rel) + jnp.triu(neg, 1)
            bwd = slopes * jnp.triu(-rel) + jnp.tril(neg, -1)
            return jnp.concatenate([fwd, bwd], axis=0)
        B, S, D = x.shape
        H, hd = (NUM_HEADS, HEAD_DIM)

        def heads(y):
            return y.reshape(B, S, H, hd).transpose(0, 2, 1, 3)
        q = heads(x @ Wq + bq)
        k = heads(x @ Wk + bk)
        v = heads(x @ Wv + bv)
        bias = alibi_bidirectional_bias(H, S, x.dtype)
        scores = jnp.einsum('bhqd,bhkd->bhqk', q, k) * (1.0 / np.sqrt(hd)) + bias[None]
        attn = jax.nn.softmax(scores, axis=-1)
        out = jnp.einsum('bhqk,bhkd->bhqd', attn, v)
        out = out.transpose(0, 2, 1, 3).reshape(B, S, D)
        return out @ Wf + bf

    def _L0_xattn_ref(q, k, v, mask):
        import jax, jax.numpy as jnp
        import numpy as np
        B, N, C, H = (2, 1024, 512, 16)
        HD = C // H
        b, n, c = q.shape
        qh = q.reshape(b, n, H, HD).transpose(0, 2, 1, 3)
        kh = k.reshape(b, n, H, HD).transpose(0, 2, 1, 3)
        vh = v.reshape(b, n, H, HD).transpose(0, 2, 1, 3)
        scale = 1.0 / jnp.sqrt(jnp.float32(HD))
        scores = jnp.einsum('bhqd,bhkd->bhqk', qh, kh) * scale
        scores = jnp.where(mask == 0, jnp.float32(-1000000000.0), scores)
        probs = jax.nn.softmax(scores, axis=-1)
        atten = jnp.einsum('bhqk,bhkd->bhqd', probs, vh)
        return atten.transpose(0, 2, 1, 3).reshape(b, n, c)

    def _L0_ffn_ref(x, w_gate, w_up, w_down):
        import jax, jax.numpy as jnp
        import numpy as np
        BLOCK = 32
        W_BITS = 4
        ACT_BITS = 16

        def act_qdq(x):
            qmax = 2.0 ** (ACT_BITS - 1) - 1.0
            scale = jnp.maximum(jnp.max(jnp.abs(x)) / qmax, 1e-12)
            return jnp.clip(jnp.round(x / scale), -qmax - 1.0, qmax) * scale

        def fixed_qdq_u16(x):
            scale = 1.0 / 65536.0
            return jnp.clip(jnp.round(x / scale), 0.0, 65535.0) * scale

        def lpbq_dequant(w):
            O, I = w.shape
            qmax = 2.0 ** (W_BITS - 1) - 1.0
            wb = w.reshape(O, I // BLOCK, BLOCK)
            s = jnp.maximum(jnp.max(jnp.abs(wb), axis=-1, keepdims=True) / qmax, 1e-12)
            wq = jnp.clip(jnp.round(wb / s), -qmax - 1.0, qmax) * s
            return wq.reshape(O, I)
        x = act_qdq(x)
        up = act_qdq(x @ lpbq_dequant(w_up).T)
        gate = act_qdq(x @ lpbq_dequant(w_gate).T)
        sig = fixed_qdq_u16(jax.nn.sigmoid(gate))
        gate = act_qdq(gate * sig)
        o = act_qdq(gate * up)
        return o @ lpbq_dequant(w_down).T
    x = _layernorm(x + _L0_attn_ref(x, L0_attn_Wq, L0_attn_bq, L0_attn_Wk, L0_attn_bk, L0_attn_Wv, L0_attn_bv, L0_attn_Wf, L0_attn_bf), axis=-1)
    x = _layernorm(x + _L0_xattn_ref(x, ctx_1024, ctx_1024, mask_Bx1xSxS2_ik1), axis=-1)
    x = _layernorm(x + _L0_ffn_ref(x, L0_ffn_w_gate, L0_ffn_w_up, L0_ffn_w_down), axis=-1)
    return x

_drawn_inputs = setup_inputs


def setup_inputs(seed=0):
    import zlib

    import numpy as np

    out = dict(_drawn_inputs(seed))
    spreads = {'L0_attn_bq': (0.0, 0.322),
     'L0_attn_bk': (0.0, 0.8),
     'L0_attn_bv': (0.0, 0.1),
     'L0_attn_bf': (0.0, 0.1)}
    factors = {}
    for name, (base, spread) in spreads.items():
        noise = np.random.default_rng([zlib.crc32(name.encode()), seed]).standard_normal(out[name].shape)
        drawn = base * np.exp(spread * noise) if base else spread * noise
        out[name] = jnp.asarray(drawn.astype(out[name].dtype))
    for name, factor in factors.items():
        out[name] = (out[name] * factor).astype(out[name].dtype)
    return out
```

```python
from contextlib import ExitStack

import numpy as np

import concourse.bass as bass
from concourse import mybir

F32 = mybir.dt.float32
F16 = mybir.dt.float16
BF16 = mybir.dt.bfloat16
I32 = mybir.dt.int32
ALU = mybir.AluOpType
ACT = mybir.ActivationFunctionType
AX = mybir.AxisListType
RMAX = bass.bass_isa.ReduceOp.max
ds = bass.ds

P = 128
B, S, D = 4, 1024, 512
H, HD = 16, 32
F = 1536
T = B * S
KT = D // P
FT = F // P
ST = S // P
GT = 512
NG = T // GT
TG = GT // P
VW = 2 * HD + 1
WSCALE = 64.0
FSCALE = 1024.0
BIG = 32768.0
SM = float(1.0 / np.sqrt(HD))
MAGIC = 12582912.0
QMAX = 32767.0
EPS = 1e-5


class Kit:

    def __init__(self, nc, ctx):
        self.nc, self.ctx, self.sems = nc, ctx, []
        ctx.callback(self.clear)

    def clear(self):
        if self.sems:
            self.nc.clear_and_free_semaphores(self.sems)
            self.nc.all_engine_barrier()

    def sb(self, name, shape, dt):
        return self.ctx.enter_context(self.nc.sbuf_tensor(name, shape, dt))

    def ps(self, name, shape, dt=F32):
        return self.ctx.enter_context(self.nc.psum_tensor(name, shape, dt))

    def sem(self, name):
        self.sems.append(self.nc.alloc_semaphore(name=name))
        return self.sems[-1]


def make_identities(nc, kit):
    c = {}
    c["idf"] = kit.sb("idf", [P, P], F32)
    c["idh"] = kit.sb("idh", [P, P], F16)
    c["idbig"] = kit.sb("idbig", [P, P], F16)
    made = kit.sem("id_made")
    with nc.Block() as block:
        @block.gpsimd
        def _(pool):
            for t in ("idf", "idh", "idbig"):
                nc.gpsimd.memset(c[t][:], 0.0).then_inc(made, 1)
            pool.wait_ge(made, 3)
            for t, v in (("idf", 1.0), ("idh", 1.0), ("idbig", BIG)):
                nc.gpsimd.affine_select(out=c[t][:], in_=c[t][:], compare_op=ALU.not_equal, fill=v, base=0,
                                        pattern=[[-1, P]], channel_multiplier=1).then_inc(made, 1)
            pool.wait_ge(made, 6)
    return c


def token_group(x, g):
    return x[ds(g * GT, GT), :].rearrange("(t p) n -> p t n", p=P)


class Turner:

    def __init__(self, kit, name, c):
        self.bank = [kit.ps(f"{name}_t{i}", [P, GT]) for i in range(2)]
        self.turned, self.hi_done, self.lo_done = kit.sem(f"{name}_turned"), kit.sem(f"{name}_hi"), kit.sem(f"{name}_lo")
        self.c = c

    def prime(self, dve):
        dve.sem_inc(self.lo_done, 2)

    def turn(self, nc, pe, n, d, src):
        pe.wait_ge(self.lo_done, n + 1)
        for tt in range(TG):
            mm = nc.tensor.transpose(self.bank[d % 2][:, tt * P:(tt + 1) * P], src[:, tt, d * P:(d + 1) * P], self.c["idf"][:])
        mm.then_inc(self.turned, 1)

    def hi(self, nc, act, n, d, hi):
        act.wait_ge(self.turned, n + 1)
        nc.scalar.copy(hi[:, d, :], self.bank[d % 2][:]).then_inc(self.hi_done, 1)

    def lo(self, nc, dve, n, d, hi, lo):
        dve.wait_ge(self.hi_done, n + 1)
        nc.vector.tensor_tensor(lo[:, d, :], self.bank[d % 2][:], hi[:, d, :], ALU.subtract).then_inc(self.lo_done, 1)


def split_matmuls(nc, out, terms):
    for n, (a, b) in enumerate(terms):
        mm = nc.tensor.matmul(out, a, b, start=(n == 0), stop=(n == len(terms) - 1))
    return mm


WT = 9
ORDER = "o0 u0 o1 m0 o2 w0 c0 o3 c1 m1 u1 o4 c2 w1 o5 c3 m2 u2 o6 w2 x0 o7 x1 m3 o8 x2 w3 o9 x3 u3 o10 w4 o11".split()
AHEAD = {0: "m0 w0", 1: "m1", 2: "w1", 3: "m2", 4: "w2", 5: "m3", 6: "w3", 7: "w4"}


def preparation_phase(nc, c, x, Wq, bq, Wk, bk, Wv, bv, qk_dram, v_dram, context, k2_dram, v2_dram,
                      mask, mb_dram, nm_dram, mlp, w_dram):
    NB = D // 32
    NO = 12
    NW = 3
    with ExitStack() as ctx:
        kit = Kit(nc, ctx)
        sb, sem = kit.sb, kit.sem
        w32 = [sb(f"w32_{j}", [P, KT, D], F32) for j in range(2)]
        wh = [sb(f"wh_{n}", [P, KT, D], F16) for n in "qkv"]
        wl = [sb(f"wl_{n}", [P, KT, D], F16) for n in "qkv"]
        bias = sb("qk_bias", [P, 2, KT], F32)
        bvr, bvb = sb("bv_row", [1, D], F32), sb("bv_all", [P, D], F32)
        xs = [sb(f"xs{v}", [P, TG, D], F32) for v in range(2)]
        xh = [sb(f"xh{v}", [P, KT, GT], F16) for v in range(2)]
        xl = [sb(f"xl{v}", [P, KT, GT], F16) for v in range(2)]
        y32 = sb("y32", [P, 4, GT], F32)
        qk = sb("qk_out", [P, 2, 2, KT, GT], F16)
        v65 = sb("v65", [P, H, TG, VW], F16)
        cs = [sb(f"cs{v}", [P, TG, D], F32) for v in range(2)]
        ch, cl = sb("ch", [P, KT, GT], F16), sb("cl", [P, KT, GT], F16)
        u65 = sb("u65", [P, H, TG, VW], F16)
        m32 = [sb(f"m32_{j}", [P, S], I32) for j in range(2)]
        mb = [sb(f"mb_tile{j}", [P, S], BF16) for j in range(2)]
        nq = [sb(f"nq_tile{j}", [P, S], F16) for j in range(2)]
        nk = sb("nk_tiles", [P, ST, TG, P], F16)
        w = [sb(f"g_w{j}", [P, D], F32) for j in range(NW)]
        wq = [sb(f"g_wq{j}", [P, D], F32) for j in range(NW)]
        wr = sb("g_r", [P, D], F32)
        wscale, winv = sb("g_s", [P, NB], F32), sb("g_i", [P, NB], F32)
        gh = [sb(f"g_hi{j}", [P, KT, P], F16) for j in range(NW)]
        gl = [sb(f"g_lo{j}", [P, KT, P], F16) for j in range(NW)]

        tr = Turner(kit, "prep", c)
        acc = [kit.ps(f"qkv_acc{i}", [P, GT]) for i in range(4)]
        mask_t = kit.ps("mask_t", [P, ST, P], F16)
        w_t = kit.ps("g_t", [P, KT, P])

        w_in, wsplit, x_in = [sem(f"w_in{j}") for j in range(3)], sem("w_split"), [sem(f"x_in{v}") for v in range(2)]
        b_in, b_all, one = sem("b_in"), sem("b_all"), sem("ones_set")
        summed, y_done, h_done, l_done = sem("summed"), sem("y_done"), sem("h_done"), sem("l_done")
        q_out, k_out, v_out = sem("q_out"), sem("k_out"), sem("v_out")
        c_in, uh_done, ul_done = [sem(f"c_in{v}") for v in range(2)], sem("uh_done"), sem("ul_done")
        c_out, u_out = sem("c_out"), sem("u_out")
        m_in, mb_out, nk_out = [sem(f"m_in{j}") for j in range(2)], [sem(f"mb_out{j}") for j in range(2)], sem("nk_out")
        m_made, m_turned, m_copied = sem("m_made"), sem("m_turned"), sem("m_copied")
        g_in, g_out = [sem(f"g_in{j}") for j in range(NW)], [sem(f"g_out{j}") for j in range(NW)]
        g_steps, g_quant, g_turned, g_hi, g_lo = (sem(f"g_{n}") for n in ("steps", "quant", "turned", "hi_done", "lo_done"))

        blocks = lambda t: t[:].rearrange("p (b e) -> p b e", e=32)
        spread = lambda t: t[:].unsqueeze(2).to_broadcast([P, NB, 32])
        by_head = lambda t: t.rearrange("p (h e) -> p h e", e=HD)

        def ctx_bank(g, d):
            return g * (2 * KT) + KT + d

        def x_bank(g, d):
            return g * (2 * KT) + 2 * KT + d

        def weight_tile(v, n):
            k = n + 5 * v
            return k if k < WT else None

        with nc.Block() as block:
            @block.sync
            def _(sp):
                def load_mask(t, j):
                    sp.dma_start(m32[j][:], mask[ds(t % (B * ST) * P, P), :]).then_inc(m_in[j], 16)

                def load_weight(i, k):
                    m, r = k // 3, k % 3
                    src = mlp[m][ds(i * (3 * P) + r * P, P), :] if m < 2 else mlp[m][ds(i * P, P), r * D:(r + 1) * D]
                    sp.dma_start(w[k % NW][:], src).then_inc(g_in[k % NW], 16)

                def rows(dram, i, v):
                    return dram[ds(i * H, H), :, v * TG:(v + 1) * TG, :].rearrange("h p t w -> p h (t w)")

                for k in range(KT):
                    sp.dma_start(w32[0][:, k], Wq[k * P:(k + 1) * P, :]).then_inc(w_in[0], 16)
                sp.dma_start(xs[0][:], token_group(x, 0)).then_inc(x_in[0], 16)
                for k in range(KT):
                    sp.dma_start(w32[1][:, k], Wk[k * P:(k + 1) * P, :]).then_inc(w_in[1], 16)
                for j, b in enumerate((bq, bk)):
                    for r in range(2):
                        for n in range(H // 2):
                            s = 2 * n + r
                            sp.dma_start(bias[s % 4 * HD:s % 4 * HD + HD, j, s // 4:s // 4 + 1],
                                         b.rearrange("(h e o) -> h e o", e=HD, o=1)[r * (H // 2) + n]).then_inc(b_in, 16)
                for r in range(2):
                    sp.dma_start(bvr[:].rearrange("p (n r e) -> p r n e", r=2, e=HD)[:, r],
                                 bv.rearrange("(o r n e) -> o r n e", o=1, r=2, e=HD)[:, r]).then_inc(b_in, 16)
                sp.dma_start(xs[1][:], token_group(x, 1)).then_inc(x_in[1], 16)
                sp.wait_ge(wsplit, 1)
                for k in range(KT):
                    sp.dma_start(w32[0][:, k], Wv[k * P:(k + 1) * P, :]).then_inc(w_in[2], 16)
                for v in range(2):
                    sp.dma_start(cs[v][:], token_group(context, v)).then_inc(c_in[v], 16)
                for j in range(2):
                    load_mask(j, j)
                for k in range(NW):
                    load_weight(0, k)
                with sp.Fori(0, NG // 2) as i:
                    for v in range(2):
                        g = i * 2 + v
                        sp.wait_ge(tr.turned, x_bank(g - 1, KT))
                        sp.dma_start(xs[v][:], token_group(x, (g + 2) % NG)).then_inc(x_in[v], 16)
                        for e in ORDER:
                            kind, n = e[0], int(e[1:])
                            if kind == "o" and n in (3, 7):
                                sp.wait_ge(l_done, g * NO + n + 1 + 4)
                                for j in range(2):
                                    sp.dma_start(qk_dram[n // 4 * 2 + j][i, :, v * GT:(v + 1) * GT].rearrange("(k p) t -> p k t", p=P),
                                                 qk[:, n // 4, j]).then_inc((q_out, k_out)[n // 4], 16)
                            if kind == "o" and n == NO - 1:
                                sp.wait_ge(l_done, g * NO + NO + 4)
                                sp.dma_start(rows(v_dram, i, v), v65[:].rearrange("p h t w -> p h (t w)")).then_inc(v_out, 16)
                            if kind == "u" and n == TG - 1:
                                sp.wait_ge(ul_done, g * TG + TG)
                                sp.dma_start(rows(v2_dram, i, v), u65[:].rearrange("p h t w -> p h (t w)")).then_inc(u_out, 16)
                                sp.dma_start(cs[v][:], token_group(context, (g + 2) % NG)).then_inc(c_in[v], 16)
                            if kind == "c" and n == KT - 1:
                                sp.wait_ge(tr.lo_done, ctx_bank(g, KT) + 2)
                                for j, src in enumerate((ch, cl)):
                                    sp.dma_start(k2_dram[j][i, :, v * GT:(v + 1) * GT].rearrange("(k p) t -> p k t", p=P),
                                                 src[:]).then_inc(c_out, 16)
                            if kind == "m":
                                t, j = g * TG + n, n % 2
                                sp.wait_ge(m_made, t * 2 + 2)
                                load_mask(t + 2, j)
                                sp.dma_start(mb_dram[ds(t * P, P), :], mb[j][:]).then_inc(mb_out[j], 16)
                                if n == TG - 1:
                                    sp.wait_ge(m_copied, t + 1)
                                    sp.dma_start(nm_dram[i, :, v * GT:(v + 1) * GT].rearrange("(k p) q -> p k q", p=P),
                                                 nk[:].rearrange("p k t q -> p k (t q)")).then_inc(nk_out, 16)
                            if kind == "w" and weight_tile(v, n) is not None:
                                k = weight_tile(v, n)
                                sp.wait_ge(g_quant, i * WT + k + 1)
                                load_weight((i + (k + NW) // WT) % (NG // 2), (k + NW) % WT)
                                sp.wait_ge(g_lo, i * WT + k + 1)
                                for j, src in enumerate((gh, gl)):
                                    sp.dma_start(w_dram[j][ds(i * 3 + (k // 3 * FT + k % 3), 1)].rearrange("o p n -> (o p) n"),
                                                 src[k % NW][:].rearrange("p k q -> p (k q)")).then_inc(g_out[k % NW], 16)
                sp.wait_ge(q_out, 32 * NG)
                sp.wait_ge(k_out, 32 * NG)
                sp.wait_ge(c_out, 32 * NG)
                for s in (v_out, u_out, nk_out):
                    sp.wait_ge(s, 16 * NG)
                for v in range(2):
                    sp.wait_ge(mb_out[v], 16 * 2 * NG)
                    sp.wait_ge(m_in[v], 16 * (2 * NG + 1))
                    sp.wait_ge(x_in[v], 16 * (NG // 2 + 1))
                    sp.wait_ge(c_in[v], 16 * (NG // 2 + 1))
                for j in range(NW):
                    sp.wait_ge(g_out[j], 32 * FT)
                    sp.wait_ge(g_in[j], 16 * (FT + 1))

            @block.tensor
            def _(pe):
                pe.wait_ge(x_in[0], 16)
                for d in range(KT):
                    tr.turn(nc, pe, d, d, xs[0])
                with pe.Fori(0, NG // 2) as i:
                    for v in range(2):
                        g = i * 2 + v
                        pe.wait_ge(tr.lo_done, x_bank(g - 1, KT) + 2)
                        for e in ORDER:
                            kind, n = e[0], int(e[1:])
                            if kind == "o":
                                if n % 4 == 0:
                                    pe.wait_ge(wsplit, n // 4 + 1)
                                pe.wait_ge(y_done, g * NO + n + 1)
                                if n < 8:
                                    m, j = slice(n % 4 * P, n % 4 * P + P), n // 4
                                    terms = [(a[:, k, m], b[:, k, :]) for k in range(KT)
                                             for a, b in ((wh[j], xh[v]), (wh[j], xl[v]), (wl[j], xh[v]))]
                                else:
                                    t = slice((n - 8) * P, (n - 8) * P + P)
                                    terms = [(a[:, k, t], b[:, k, :]) for k in range(KT)
                                             for a, b in ((xh[v], wh[2]), (xh[v], wl[2]), (xl[v], wh[2]))]
                                split_matmuls(nc, acc[n % 4][:], terms).then_inc(summed, 1)
                            if kind == "c":
                                pe.wait_ge(c_in[v], i * 16 + 16)
                                tr.turn(nc, pe, ctx_bank(g, n), n, cs[v])
                            if kind == "x":
                                pe.wait_ge(x_in[1 - v], (i + v) * 16 + 16)
                                tr.turn(nc, pe, x_bank(g, n), n, xs[1 - v])
                            if kind == "m":
                                pe.wait_ge(m_made, (g * TG + n) * 2 + 2)
                                pe.wait_ge(m_copied, g * TG + n)
                                for k in range(ST):
                                    mm = nc.tensor.transpose(mask_t[:, k, :], nq[n % 2][:, k * P:(k + 1) * P], c["idh"][:])
                                mm.then_inc(m_turned, 1)
                            if kind == "w" and weight_tile(v, n) is not None:
                                k = weight_tile(v, n)
                                pe.wait_ge(g_quant, i * WT + k + 1)
                                pe.wait_ge(g_lo, i * WT + k)
                                for d in range(KT):
                                    mm = nc.tensor.transpose(w_t[:, d, :], wq[k % NW][:, d * P:(d + 1) * P], c["idf"][:])
                                mm.then_inc(g_turned, 1)

            @block.scalar
            def _(act):
                for d in range(KT):
                    tr.hi(nc, act, d, d, xh[0])
                act.wait_ge(b_in, 16 * (2 * H + 2))
                with act.Fori(0, NG // 2) as i:
                    for v in range(2):
                        g = i * 2 + v
                        for e in ORDER:
                            kind, n = e[0], int(e[1:])
                            if kind == "o" and n < 8:
                                act.wait_ge(summed, g * NO + n + 1)
                                act.wait_ge(l_done, g * NO + max(n + 1, 4))
                                nc.scalar.activation(y32[:, n % 4], acc[n % 4][:], ACT.Identity, scale=1.0 / WSCALE,
                                                     bias=bias[:, n // 4, n % 4:n % 4 + 1]).then_inc(y_done, 1)
                            if kind == "u":
                                act.wait_ge(c_in[v], i * 16 + 16)
                                if n == 0:
                                    act.wait_ge(u_out, g * 16)
                                nc.scalar.copy(u65[:, :, n, 0:HD], by_head(cs[v][:, n])).then_inc(uh_done, 1)
                            if kind == "c":
                                if n == 0:
                                    act.wait_ge(c_out, g * 32)
                                tr.hi(nc, act, ctx_bank(g, n), n, ch)
                            if kind == "x":
                                tr.hi(nc, act, x_bank(g, n), n, xh[1 - v])
                            if kind == "m":
                                act.wait_ge(m_turned, g * TG + n + 1)
                                if n == 0:
                                    act.wait_ge(nk_out, g * 16)
                                nc.scalar.copy(nk[:, :, n, :], mask_t[:]).then_inc(m_copied, 1)
                            if kind == "w" and weight_tile(v, n) is not None:
                                k = weight_tile(v, n)
                                act.wait_ge(g_turned, i * WT + k + 1)
                                act.wait_ge(g_out[k % NW], i * 96 + k // 3 * 32)
                                nc.scalar.mul(gh[k % NW][:], w_t[:], FSCALE).then_inc(g_hi, 1)

            @block.vector
            def _(dve):
                dve.sem_inc(y_done, 4)
                dve.sem_inc(l_done, 4)
                tr.prime(dve)

                def split_projection(j):
                    src = w32[j % 2]
                    dve.wait_ge(w_in[j], 16 * KT)
                    nc.vector.tensor_scalar(src[:], src[:], WSCALE, None, ALU.mult).then_inc(one, 1)
                    dve.wait_ge(one, 2 * TG + j * 5 + 1)
                    order = lambda t, k: t[:, k, :].rearrange("p (n r e) -> p r n e", r=2, e=HD)
                    given = lambda k: src[:, k, :].rearrange("p (r n e) -> p r n e", r=2, e=HD)
                    for k in range(KT):
                        nc.vector.tensor_copy(order(wh[j], k), given(k)).then_inc(one, 1)
                    for k in range(KT):
                        dve.wait_ge(one, 2 * TG + j * 5 + 2 + k)
                        mm = nc.vector.tensor_tensor(order(wl[j], k), given(k), order(wh[j], k), ALU.subtract)
                    mm.then_inc(wsplit, 1)

                def quantise(i, k):
                    n = i * WT + k
                    dve.wait_ge(g_in[k % NW], i * 48 + (k // NW * 16 + 16))
                    dve.wait_ge(g_quant, n)
                    nc.vector.tensor_reduce(wscale[:], blocks(w[k % NW]), AX.X, ALU.max, apply_absolute_value=True).then_inc(g_steps, 1)
                    dve.wait_ge(g_steps, n * 5 + 1)
                    nc.vector.tensor_scalar(wscale[:], wscale[:], 1.0 / 7.0, 1e-12, ALU.mult, ALU.max).then_inc(g_steps, 1)
                    dve.wait_ge(g_steps, n * 5 + 2)
                    nc.vector.reciprocal(winv[:], wscale[:]).then_inc(g_steps, 1)
                    dve.wait_ge(g_steps, n * 5 + 3)
                    nc.vector.tensor_tensor(blocks(wr), blocks(w[k % NW]), spread(winv), ALU.mult).then_inc(g_steps, 1)
                    dve.wait_ge(g_steps, n * 5 + 4)
                    nc.vector.tensor_scalar(wr[:], wr[:], MAGIC, -MAGIC, ALU.add, ALU.add).then_inc(g_steps, 1)
                    dve.wait_ge(g_steps, n * 5 + 5)
                    nc.vector.tensor_tensor(blocks(wq[k % NW]), blocks(wr), spread(wscale), ALU.mult).then_inc(g_quant, 1)

                def mask_inputs(g, v, n):
                    j = n % 2
                    dve.wait_ge(m_in[j], g * 32 + (n // 2 * 16 + 16))
                    dve.wait_ge(mb_out[j], g * 32 + n // 2 * 16)
                    dve.wait_ge(m_turned, g * TG + max(n - 1, 0))
                    nc.vector.tensor_scalar(mb[j][:], m32[j][:], 0.0, -BIG * BIG, ALU.is_equal, ALU.mult).then_inc(m_made, 1)
                    nc.vector.tensor_scalar(nq[j][:], m32[j][:], 0.0, -BIG, ALU.is_equal, ALU.mult).then_inc(m_made, 1)

                for t in (v65, u65):
                    for tt in range(TG):
                        nc.vector.memset(t[:, :, tt, HD:HD + 1], 1.0).then_inc(one, 1)
                split_projection(0)
                for d in range(KT):
                    tr.lo(nc, dve, d, d, xh[0], xl[0])
                split_projection(1)
                split_projection(2)
                with dve.Fori(0, NG // 2) as i:
                    for v in range(2):
                        g = i * 2 + v
                        for e in ORDER:
                            kind, n = e[0], int(e[1:])
                            if kind == "o":
                                for a in AHEAD.get(n, "").split():
                                    if a[0] == "m":
                                        mask_inputs(g, v, int(a[1:]))
                                    elif weight_tile(v, int(a[1:])) is not None:
                                        quantise(i, weight_tile(v, int(a[1:])))
                                if n in (0, 4):
                                    dve.wait_ge((q_out, k_out)[n // 4], g * 32)
                                if n < 8:
                                    dve.wait_ge(y_done, g * NO + n + 5)
                                    nc.vector.tensor_copy(qk[:, n // 4, 0, n % 4], y32[:, n % 4]).then_inc(h_done, 1)
                                else:
                                    tt = n - 8
                                    if n == 8:
                                        dve.wait_ge(b_all, 1)
                                    dve.wait_ge(summed, g * NO + n + 1)
                                    dve.wait_ge(l_done, g * NO + n + 1)
                                    nc.vector.scalar_tensor_tensor(out=y32[:, tt], in0=acc[n % 4][:], scalar=1.0 / WSCALE, in1=bvb[:],
                                                                   op0=ALU.mult, op1=ALU.add).then_inc(y_done, 1)
                                    dve.wait_ge(y_done, g * NO + n + 5)
                                    dve.wait_ge(v_out, g * 16)
                                    nc.vector.tensor_copy(v65[:, :, tt, 0:HD], by_head(y32[:, tt])).then_inc(h_done, 1)
                            if kind == "c":
                                tr.lo(nc, dve, ctx_bank(g, n), n, ch, cl)
                            if kind == "x":
                                tr.lo(nc, dve, x_bank(g, n), n, xh[1 - v], xl[1 - v])
                            if kind == "w" and weight_tile(v, n) is not None:
                                k = weight_tile(v, n)
                                dve.wait_ge(g_hi, i * WT + k + 1)
                                nc.vector.scalar_tensor_tensor(out=gl[k % NW][:], in0=w_t[:], scalar=FSCALE, in1=gh[k % NW][:],
                                                               op0=ALU.mult, op1=ALU.subtract).then_inc(g_lo, 1)

            @block.gpsimd
            def _(pool):
                pool.wait_ge(b_in, 16 * (2 * H + 2))
                nc.gpsimd.partition_broadcast(bvb[:], bvr[:]).then_inc(b_all, 1)
                with pool.Fori(0, NG // 2) as i:
                    for v in range(2):
                        g = i * 2 + v
                        for e in ORDER:
                            kind, n = e[0], int(e[1:])
                            if kind == "o":
                                pool.wait_ge(h_done, g * NO + n + 1)
                                if n < 8:
                                    nc.gpsimd.tensor_tensor(qk[:, n // 4, 1, n % 4], y32[:, n % 4], qk[:, n // 4, 0, n % 4],
                                                            ALU.subtract).then_inc(l_done, 1)
                                else:
                                    tt = n - 8
                                    nc.gpsimd.tensor_tensor(v65[:, :, tt, HD + 1:VW], by_head(y32[:, tt]),
                                                            v65[:, :, tt, 0:HD], ALU.subtract).then_inc(l_done, 1)
                            if kind == "u":
                                pool.wait_ge(uh_done, g * TG + n + 1)
                                nc.gpsimd.tensor_tensor(u65[:, :, n, HD + 1:VW], by_head(cs[v][:, n]),
                                                        u65[:, :, n, 0:HD], ALU.subtract).then_inc(ul_done, 1)


SLEAD = 18
ELEAD = 3
NQK = 4
NPR = 4
UH = ST
HB = 4
NI = B * H // HB
SLOTS = B * H * (UH + 1)
PRIME = 3 * UH


def slot_of_scores(u):
    return u + max(0, (u - 2) // UH)


def slot_of_max(n):
    return min((UH + 1) * n + UH + 2, SLOTS - 1)


def attention_phase(nc, c, name, causal, q_dram, k_dram, v_dram, out_dram, mb_dram=None, nm_dram=None):
    with ExitStack() as ctx:
        kit = Kit(nc, ctx)
        sem = lambda n: kit.sem(f"{name}_{n}")
        sb = lambda n, s, d: kit.sb(f"{name}_{n}", s, d)
        qa = [sb(f"qa{j}", [P, S], F16) for j in range(NQK)]
        ka = [sb(f"ka{j}", [P, S], F16) for j in range(NQK)]
        vh = [sb(f"vh{j}", [P, ST, VW], F16) for j in range(NQK)]
        p32 = [sb(f"p32_{j}", [P, S], F32) for j in range(NPR)]
        plo = [sb(f"plo{j}", [P, S], F16) for j in range(NPR)]
        junk = [sb(f"junk{j}", [P, S], BF16) for j in range(2)]
        qmax = [sb(f"qmax{j}", [P, ST], F32) for j in range(2)]
        mneg = [sb(f"mneg{j}", [P, ST], F32) for j in range(2)]
        mrow = [sb(f"mrow{j}", [ST, P], F16) for j in range(NQK)]
        oraw = [sb(f"oraw{j}", [P, ST, VW], F32) for j in range(2)]
        osum = [sb(f"osum{j}", [P, ST, HD], F32) for j in range(2)]
        rden = [sb(f"rden{j}", [P, ST], F32) for j in range(2)]
        ost = sb("ost", [P, ST, HB * HD], F32)
        sc = [kit.ps(f"{name}_sc{j}", [P, S]) for j in range(2)]
        stp = [kit.ps(f"{name}_st{j}", [P, GT]) for j in range(2)]
        ob = [kit.ps(f"{name}_o{j}", [P, ST // 2, VW]) for j in range(2)]

        qk_in = [sem(f"qk_in{j}") for j in range(NQK)]
        mrow_in = [sem(f"mrow_in{j}") for j in range(NQK)]
        v_in = [sem(f"v_in{j}") for j in range(NQK)]
        scored, taken = sem("scored"), sem("taken")
        negated = sem("negated")
        chunked = sem("chunked")
        expd = sem("expd")
        lo_v, lo_g = sem("lo_v"), sem("lo_g")
        pv_done = sem("pv_done")
        o_read = sem("o_read")
        o_recip, o_added, o_scaled = sem("o_recip"), sem("o_added"), sem("o_scaled")
        o_out = sem("o_out")
        ready = sem("ready")
        stood = sem("stood")
        if causal:
            kc = sb("kc", [P, ST], F32)
            slopes = sb("slopes", [P, H], F32)
            tab = sb("tab", [P, H, 2 * ST + 1], F32)
            cur = [sb(f"cur{j}", [P, 2 * ST + 1], F32) for j in range(NQK)]
            ramp = [sb(f"ramp{j}", [P, S], F32) for j in range(2)]
            tri = [sb(f"tri{j}", [P, P], F16) for j in range(2)]
            strip = [sb(f"strip{j}", [P, S], F32) for j in range(2)]
            made, cur_in, strip_in = sem("made"), sem("cur_in"), sem("strip_in")
        else:
            mb = [sb(f"mb{j}", [P, S], BF16) for j in range(ST)]
            nm = [sb(f"nm{j}", [P, S], F16) for j in range(ST)]
            mb_in, nm_in = [sem(f"mb_in{j}") for j in range(ST)], [sem(f"nm_in{j}") for j in range(ST)]

        def key_range(n, qt):
            if not causal:
                return 0, S
            return (0, (qt + 1) * P) if n % 2 == 0 else (qt * P, S)

        def query_range(n, kt):
            if not causal:
                return 0, S
            return (kt * P, S) if n % 2 == 0 else (0, (kt + 1) * P)

        def chunks(n, kt):
            a, b = query_range(n, kt)
            return [(max(a, x), min(b, x + GT)) for x in range(0, S, GT) if x < b and x + GT > a]

        def chunks_before(u):
            return sum(len(chunks(m // UH, m % UH)) for m in range(u))

        CS = chunks_before(HB * UH)

        def share(n, kt):
            a, b = query_range(n, kt)
            k0, k1 = key_range(n, kt)
            return a + min(max(32, int((2.03 * (b - a) - 1.04 * (k1 - k0) - 200) / 3.07) // 32 * 32), b - a - 32)

        def steps(eng, prologue, step):
            prologue()
            with eng.Fori(0, NI - 1) as i:
                for t in range(HB * UH):
                    step(i, t, False)
            for t in range(HB * UH):
                step(NI - 1, t, True)

        def max_slot(i, n):
            return slot_of_max(n) if not isinstance(i, int) else slot_of_max(n + i * HB) - (UH + 1) * HB * i

        def within(last, u):
            return not last or u < HB * UH

        with nc.Block() as block:
            @block.sync
            def _(sp):
                def load_head(i, n):
                    j, row = n % NQK, (i * HB + n) % (B * H) * HD
                    for dst, src, part in ((qa, q_dram[0], 0), (qa, q_dram[0], 1), (qa, q_dram[1], 2),
                                           (ka, k_dram[0], 0), (ka, k_dram[1], 1), (ka, k_dram[0], 2)):
                        sp.dma_start(dst[j][part * HD:(part + 1) * HD, :],
                                     src.rearrange("b r t -> (b r) t")[ds(row, HD), :]).then_inc(qk_in[j], 16)

                def load_values(i, n):
                    sp.dma_start(vh[n % NQK][:], v_dram[ds((i * HB + n) % (B * H), 1)].rearrange("o p t w -> (o p) t w")).then_inc(v_in[n % NQK], 16)

                def load_max(i, n):
                    sp.wait_ge(taken, i * (HB * (UH + 1)) + max_slot(i, n) + 3)
                    sp.dma_start(qa[n % NQK][3 * HD:3 * HD + 1, :].rearrange("o (a c) -> o a c", a=ST),
                                 mrow[n % NQK][:]).then_inc(mrow_in[n % NQK], 16)

                def load_mb(b, qt):
                    sp.dma_start(mb[qt][:], mb_dram[ds(b * S + qt * P, P), :]).then_inc(mb_in[qt], 16)

                def load_nm(b, kt):
                    sp.dma_start(nm[kt][:], nm_dram.rearrange("b k q -> (b k) q")[ds(b * S + kt * P, P), :]).then_inc(nm_in[kt], 16)

                def step(i, t, last, next_batch=None):
                    n, k = divmod(t, UH)
                    if k == 0 and within(last, (n + 1) * UH):
                        load_max(i, n + 1)
                    if k == 1 and n > 0 or t == 1:
                        sp.wait_ge(pv_done, i * (HB * UH) + n * UH + PRIME)
                        load_values(i, n - 1 + NQK)
                    if k == UH - 3:
                        sp.wait_ge(chunked, i * CS + chunks_before((n + 1) * UH))
                        load_head(i, n + NQK)
                    if next_batch is not None:
                        q = t + SLEAD - 2 - 3 * UH
                        if 0 <= q < UH:
                            sp.wait_ge(taken, i * (HB * (UH + 1)) + slot_of_scores(3 * UH + q) + 3)
                            load_mb(next_batch, q)
                        q = t + ELEAD - 2 - 3 * UH
                        if 0 <= q < UH and t < HB * UH - 1:
                            sp.wait_ge(chunked, i * CS + chunks_before(3 * UH + q + 1))
                            load_nm(next_batch, q)
                        if t == HB * UH - 1:
                            for q in range(t + ELEAD - 2 - 3 * UH, UH):
                                sp.wait_ge(chunked, i * CS + chunks_before(3 * UH + q + 1))
                                load_nm(next_batch, q)
                    if t == HB * UH - 1:
                        sp.wait_ge(o_scaled, i * HB + HB + 1)
                        sp.dma_start(out_dram[ds(i // (H // HB) * S, S), ds(i % (H // HB) * (HB * HD), HB * HD)].rearrange("(t p) n -> p t n", p=P),
                                     ost[:]).then_inc(o_out, 16)

                sp.wait_ge(ready, NQK)
                for n in range(NQK):
                    load_head(0, n)
                    if n < NQK - 1:
                        load_values(0, n)
                    if n == 0 and not causal:
                        for q in range(UH):
                            load_mb(0, q)
                if not causal:
                    for q in range(UH):
                        load_nm(0, q)
                load_max(0, 0)
                NB = H // HB
                with sp.Fori(0, B - 1) as b:
                    with sp.Fori(0, NB - 1) as g:
                        for t in range(HB * UH):
                            step(b * NB + g, t, False)
                    for t in range(HB * UH):
                        step(b * NB + (NB - 1), t, False, None if causal else b + 1)
                with sp.Fori(NI - NB, NI - 1) as i:
                    for t in range(HB * UH):
                        step(i, t, False)
                for t in range(HB * UH):
                    step(NI - 1, t, True)
                sp.wait_ge(o_out, 16 * NI)
                for j in range(NQK):
                    sp.wait_ge(qk_in[j], 96 * (NI + 1))
                    sp.wait_ge(v_in[j], 16 * (NI + 1 if j < NQK - 1 else NI))

            @block.tensor
            def _(pe):
                def scores(i, u):
                    n, qt = divmod(u, UH)
                    j, slot = n % NQK, slot_of_scores(u)
                    if qt == 0:
                        pe.wait_ge(qk_in[j], (i + n // NQK + 1) * 96)
                    pe.wait_ge(taken, i * (HB * (UH + 1)) + slot + 1)
                    k0, k1 = key_range(n, qt)
                    for k in range(k0, k1, GT):
                        w = min(GT, k1 - k)
                        mm = nc.tensor.matmul(sc[slot % 2][:, k - k0:k - k0 + w], qa[j][0:3 * HD, qt * P:(qt + 1) * P],
                                              ka[j][0:3 * HD, k:k + w], start=True, stop=True)
                    mm.then_inc(scored, 1)

                def turn_max(i, n, slot):
                    pe.wait_ge(taken, i * (HB * (UH + 1)) + slot + 1)
                    pe.wait_ge(negated, i * HB + n + 1 + 2)
                    nc.tensor.transpose(sc[slot % 2][0:ST, 0:P], mneg[n % 2][:], c["idf"][:]).then_inc(scored, 1)

                def ahead(i, u, last):
                    if within(last, u):
                        scores(i, u)
                    if u >= UH + 1 and u % UH == 1:
                        n = u // UH - 1
                        if within(last, n * UH):
                            turn_max(i, n, max_slot(i, n))

                def key_scores(i, u):
                    n, kt = divmod(u, UH)
                    j = n % NQK
                    if kt == 0:
                        pe.wait_ge(mrow_in[j], (i + n // NQK + 1) * 16)
                    if not causal and n % HB == 0:
                        pe.wait_ge(nm_in[kt], (i + n // HB) // (H // HB) * 16 + 16)
                    cc = chunks_before(u)
                    for q0, q1 in chunks(n, kt):
                        pe.wait_ge(expd, i * CS + cc + 1)
                        w, out = q1 - q0, stp[cc % 2]
                        lhs = ka[j][0:3 * HD + 1, kt * P:(kt + 1) * P]
                        diag = causal and q0 <= kt * P < q1
                        mm = nc.tensor.matmul(out[:, 0:w], lhs, qa[j][0:3 * HD + 1, q0:q1], start=True, stop=causal)
                        if diag:
                            d = kt * P - q0
                            mm = nc.tensor.matmul(out[:, d:d + P], c["idbig"][:], tri[n % 2][:], start=False, stop=True, skip_group_check=True)
                        if not causal:
                            mm = nc.tensor.matmul(out[:, 0:w], c["idbig"][:], nm[kt][:, q0:q1], start=False, stop=True)
                        mm.then_inc(chunked, 1)
                        cc += 1

                def values(i, u):
                    n, kt = divmod(u, UH)
                    unit = i * (HB * UH) + u
                    if kt == 0:
                        pe.wait_ge(v_in[n % NQK], i * 16 + 16)
                        pe.wait_ge(o_read, (i * HB + n) * 2 + 2)
                    pe.wait_ge(expd, i * CS + chunks_before(u + 1) + 2)
                    pe.wait_ge(lo_v, unit + 1)
                    pe.wait_ge(lo_g, unit + 1)
                    a, z = query_range(n, kt)
                    high = p32[u % NPR][:].bitcast(BF16).rearrange("p (q h) -> p q h", h=2)[:, :, 1]
                    for qt in range(a // P, z // P):
                        q = slice(qt * P, (qt + 1) * P)
                        out = ob[qt // 4]
                        first = (kt == 0 and qt % 4 == 0) or (causal and n % 2 == 1 and kt == qt == 4)
                        last_kt = kt == (qt if causal and n % 2 == 0 else ST - 1)
                        nc.tensor.matmul(out[:, qt % 4, :], high[:, q], vh[n % NQK][:, kt, :], start=first, stop=False, skip_group_check=True)
                        mm = nc.tensor.matmul(out[:, qt % 4, 0:HD + 1], plo[u % NPR][:, q], vh[n % NQK][:, kt, 0:HD + 1],
                                              start=False, stop=last_kt, skip_group_check=True)
                    mm.then_inc(pv_done, 1)
                    return mm

                if causal:
                    pe.wait_ge(made, 9 + H)
                pe.wait_ge(ready, NQK)

                def prologue():
                    for u in range(SLEAD):
                        ahead(0, u, False)
                    for u in range(ELEAD):
                        key_scores(0, u)

                def step(i, t, last):
                    ahead(i, t + SLEAD, last)
                    if within(last, t + ELEAD):
                        key_scores(i, t + ELEAD)
                    values(i, t)

                steps(pe, prologue, step)

            @block.scalar
            def _(act):
                act.sem_inc(expd, 2)
                act.sem_inc(o_read, 2)

                def exps(i, u):
                    n, kt = divmod(u, UH)
                    act.wait_ge(pv_done, i * (HB * UH) + u - NPR + 1 + PRIME)
                    if causal and kt == 0:
                        act.wait_ge(cur_in, i * HB + n + 1)
                    cc = chunks_before(u)
                    for q0, q1 in chunks(n, kt):
                        act.wait_ge(chunked, i * CS + cc + 1)
                        bias = cur[n % NQK][:, kt:kt + 1] if causal else 0.0
                        nc.scalar.activation(p32[u % NPR][:, q0:q1], stp[cc % 2][:, 0:q1 - q0], ACT.Exp,
                                             bias=bias, scale=SM).then_inc(expd, 1)
                        cc += 1

                def prologue():
                    for u in range(ELEAD):
                        exps(0, u)

                def step(i, t, last):
                    if within(last, t + ELEAD):
                        exps(i, t + ELEAD)
                    if t % UH == UH - 1:
                        n = t // UH
                        head = i * HB + n
                        act.wait_ge(pv_done, i * (HB * UH) + t + 1 + PRIME)
                        act.wait_ge(o_scaled, head)
                        for j in range(2):
                            nc.scalar.copy(oraw[n % 2][:, 4 * j:4 * j + 4, :], ob[j][:]).then_inc(o_read, 1)

                steps(act, prologue, step)

            @block.vector
            def _(dve):
                dve.sem_inc(taken, 2)
                dve.sem_inc(pv_done, PRIME)
                dve.sem_inc(negated, 2)
                dve.sem_inc(o_scaled, 1)
                for j in range(NQK):
                    nc.vector.memset(ka[j][3 * HD:3 * HD + 1, :], BIG).then_inc(ready, 1)
                if causal:
                    dve.wait_ge(made, 9 + H)
                    for n in range(H):
                        nc.vector.tensor_scalar(tab[:, n, 0:ST], kc[:], slopes[:, n:n + 1], SM, ALU.mult, ALU.mult).then_inc(ready, 1)
                        nc.vector.tensor_scalar(tab[:, n, ST:2 * ST], kc[:], slopes[:, n:n + 1], -1.0 / BIG, ALU.mult, ALU.mult).then_inc(ready, 1)
                        nc.vector.tensor_copy(tab[:, n, 2 * ST:2 * ST + 1], slopes[:, n:n + 1]).then_inc(ready, 1)
                    dve.wait_ge(ready, NQK + 3 * H)

                def constants(i, n):
                    dve.wait_ge(pv_done, i * (HB * UH) + (n - NQK + 1) * UH + PRIME)
                    slot = (i * HB + n) % H
                    nc.vector.tensor_copy(cur[n % NQK][:], tab[:].rearrange("p n w -> p (n w)")[:, ds(slot * (2 * ST + 1), 2 * ST + 1)]).then_inc(cur_in, 1)

                def maxima(i, u):
                    n, qt = divmod(u, UH)
                    slot = slot_of_scores(u)
                    k0, k1 = key_range(n, qt)
                    w = k1 - k0
                    done = i * (HB * (UH + 1)) + slot
                    dve.wait_ge(scored, done + 1)
                    dve.wait_ge(taken, done + 1)
                    if qt == 0:
                        dve.wait_ge(negated, i * HB + n + 1)
                    if causal:
                        if qt == 0:
                            dve.wait_ge(strip_in, i * HB + n + 1)
                        bias = strip[n % 2][:, S - w:S] if n % 2 == 0 else strip[n % 2][:, 0:w]
                    else:
                        if n % HB == 0:
                            dve.wait_ge(mb_in[qt], (i + n // HB) // (H // HB) * 16 + 16)
                        bias = mb[qt][:]
                    dve.sem_inc(stood, 1)
                    nc.vector.tensor_tensor_reduce(junk[slot % 2][:, 0:w], sc[slot % 2][:, 0:w], bias, 1.0, -3e38,
                                                   ALU.add, ALU.max, qmax[n % 2][:, qt:qt + 1]).then_inc(taken, 1)
                    if qt == UH - 1:
                        dve.wait_ge(taken, done + 3)
                        if causal:
                            nc.vector.scalar_tensor_tensor(out=mneg[n % 2][:], in0=qmax[n % 2][:], scalar=-1.0 / BIG,
                                                           in1=cur[n % NQK][:, ST:2 * ST], op0=ALU.mult, op1=ALU.add).then_inc(negated, 1)
                        else:
                            nc.vector.tensor_scalar(mneg[n % 2][:], qmax[n % 2][:], -1.0 / BIG, None, ALU.mult).then_inc(negated, 1)

                def max_row(i, n, slot):
                    dve.wait_ge(scored, i * (HB * (UH + 1)) + slot + 1)
                    dve.wait_ge(mrow_in[n % NQK], (i + n // NQK) * 16)
                    nc.vector.tensor_copy(mrow[n % NQK][:], sc[slot % 2][0:ST, 0:P]).then_inc(taken, 1)

                def ahead(i, u, last):
                    if causal and u % UH == 0 and within(last, u):
                        constants(i, u // UH)
                    if within(last, u):
                        maxima(i, u)
                    if u >= UH + 1 and u % UH == 1:
                        n = u // UH - 1
                        if within(last, n * UH):
                            max_row(i, n, max_slot(i, n))

                def low(i, u):
                    n, kt = divmod(u, UH)
                    dve.wait_ge(expd, i * CS + chunks_before(u + 1) + 2)
                    q = slice(query_range(n, kt)[0], share(n, kt))
                    high = p32[u % NPR][:].bitcast(BF16).rearrange("p (q h) -> p q h", h=2)[:, :, 1]
                    nc.vector.tensor_tensor(plo[u % NPR][:, q], p32[u % NPR][:, q], high[:, q], ALU.subtract).then_inc(lo_v, 1)

                def prologue():
                    for u in range(SLEAD):
                        ahead(0, u, False)
                    for u in range(ELEAD - 1):
                        low(0, u)

                def step(i, t, last):
                    ahead(i, t + SLEAD, last)
                    if within(last, t + ELEAD - 1):
                        low(i, t + ELEAD - 1)
                    n, k = divmod(t, UH)
                    if k == UH - 1:
                        head = i * HB + n
                        dve.wait_ge(o_read, head * 2 + 4)
                        nc.vector.reciprocal(rden[n % 2][:], oraw[n % 2][:, :, HD]).then_inc(o_recip, 1)
                        dve.wait_ge(o_recip, head + 1)
                        dve.wait_ge(o_added, head + 1)
                        if n == 0:
                            dve.wait_ge(o_out, i * 16)
                        nc.vector.tensor_tensor(ost[:, :, n * HD:(n + 1) * HD], osum[n % 2][:],
                                                rden[n % 2][:].unsqueeze(2).to_broadcast([P, ST, HD]), ALU.mult).then_inc(o_scaled, 1)

                steps(dve, prologue, step)

            @block.gpsimd
            def _(pool):
                if causal:
                    nc.gpsimd.iota(kc[:], pattern=[[P, ST]], base=-S // 2, channel_multiplier=1, allow_small_or_imprecise_dtypes=True).then_inc(made, 1)
                    for n in range(H):
                        s = 24.0 ** (-(n // 2 + 1) / (H // 2)) / SM
                        nc.gpsimd.memset(slopes[:, n:n + 1], s if n % 2 == 0 else -s).then_inc(made, 1)
                    for j in range(2):
                        nc.gpsimd.memset(tri[j][:], 0.0).then_inc(made, 1)
                        nc.gpsimd.iota(ramp[j][:], pattern=[[1, S]], base=(P - S, 0)[j], channel_multiplier=-1,
                                       allow_small_or_imprecise_dtypes=True).then_inc(made, 1)
                    pool.wait_ge(made, 5 + H)
                    for j, sign in enumerate((-1, 1)):
                        nc.gpsimd.affine_select(out=ramp[j][:], in_=ramp[j][:], compare_op=ALU.is_ge, fill=sign * 4.5e9,
                                                base=sign * (P - S, 0)[j], pattern=[[sign, S]], channel_multiplier=-sign).then_inc(made, 1)
                        nc.gpsimd.affine_select(out=tri[j][:], in_=tri[j][:], compare_op=ALU.is_ge, fill=-BIG,
                                                base=0, pattern=[[-sign, P]], channel_multiplier=sign).then_inc(made, 1)
                    pool.wait_ge(made, 9 + H)

                def strips(i, n):
                    pool.wait_ge(cur_in, i * HB + n + 1)
                    pool.wait_ge(negated, i * HB + n + 1)
                    pool.sem_inc(stood, 1)
                    nc.gpsimd.tensor_scalar(strip[n % 2][:], ramp[n % 2][:], cur[n % NQK][:, 2 * ST:2 * ST + 1], 1.0, ALU.mult, ALU.mult).then_inc(strip_in, 1)

                def low(i, u):
                    n, kt = divmod(u, UH)
                    pool.wait_ge(expd, i * CS + chunks_before(u + 1) + 2)
                    q = slice(share(n, kt), query_range(n, kt)[1])
                    high = p32[u % NPR][:].bitcast(BF16).rearrange("p (q h) -> p q h", h=2)[:, :, 1]
                    nc.gpsimd.tensor_tensor(plo[u % NPR][:, q], p32[u % NPR][:, q], high[:, q], ALU.subtract).then_inc(lo_g, 1)

                def ahead(i, u, last):
                    if causal and u % UH == 0 and within(last, u):
                        strips(i, u // UH)

                def prologue():
                    for u in range(SLEAD):
                        ahead(0, u, False)
                    for u in range(ELEAD - 1):
                        low(0, u)

                def step(i, t, last):
                    ahead(i, t + SLEAD, last)
                    if within(last, t + ELEAD - 1):
                        low(i, t + ELEAD - 1)
                    n, k = divmod(t, UH)
                    if k == UH - 1:
                        head = i * HB + n
                        pool.wait_ge(o_read, head * 2 + 4)
                        pool.wait_ge(o_scaled, head)
                        nc.gpsimd.tensor_tensor(osum[n % 2][:], oraw[n % 2][:, :, 0:HD], oraw[n % 2][:, :, HD + 1:VW],
                                                ALU.add).then_inc(o_added, 1)

                steps(pool, prologue, step)


class Norm:

    def __init__(self, kit, name):
        self.st = [kit.sb(f"{name}_bn{j}", [P, 6], F32) for j in range(2)]
        self.mv = [kit.sb(f"{name}_mv{j}", [P, 2], F32) for j in range(2)]
        self.sd = [kit.sb(f"{name}_sd{j}", [P, 1], F32) for j in range(2)]
        self.rs = [kit.sb(f"{name}_rs{j}", [P, 1], F32) for j in range(2)]
        self.steps = kit.sem(f"{name}_steps")
        self.root = kit.sem(f"{name}_root")
        self.recip = kit.sem(f"{name}_recip")
        self.stood = kit.sem(f"{name}_stood")

    def statistics(self, nc, dve, n, j, r):
        nc.vector.bn_stats(self.st[j][:], r).then_inc(self.steps, 1)
        dve.wait_ge(self.steps, n * 3 + 1)
        dve.sem_inc(self.stood, 1)
        nc.vector.bn_aggr(self.mv[j][:], self.st[j][:]).then_inc(self.steps, 1)
        dve.wait_ge(self.steps, n * 3 + 2)
        nc.vector.tensor_scalar(self.mv[j][:, 1:2], self.mv[j][:, 1:2], EPS, None, ALU.add).then_inc(self.steps, 1)

    def square_root(self, nc, act, n, j):
        act.wait_ge(self.steps, n * 3 + 3)
        nc.scalar.activation(self.sd[j][:], self.mv[j][:, 1:2], ACT.Sqrt).then_inc(self.root, 1)

    def scale(self, nc, dve, n, j, out, r):
        dve.wait_ge(self.root, n + 1)
        nc.vector.reciprocal(self.rs[j][:], self.sd[j][:]).then_inc(self.recip, 1)
        dve.wait_ge(self.recip, n + 1)
        return nc.vector.tensor_scalar(out, r, self.mv[j][:, 0:1], self.rs[j][:, 0:1], ALU.subtract, ALU.mult)


def projection_phase(nc, c, attn, x, Wf, bf, x1_dram, q_dram):
    with ExitStack() as ctx:
        kit = Kit(nc, ctx)
        w32 = kit.sb("wf32", [P, KT, D], F32)
        wh, wl = kit.sb("wfh", [P, KT, D], F16), kit.sb("wfl", [P, KT, D], F16)
        bfr, bfb = kit.sb("bf_row", [1, D], F32), kit.sb("bf_all", [P, D], F32)
        at = [kit.sb(f"at{v}", [P, TG, D], F32) for v in range(2)]
        xs = [kit.sb(f"px{v}", [P, TG, D], F32) for v in range(2)]
        x1 = [kit.sb(f"px1_{v}", [P, TG, D], F32) for v in range(2)]
        ah, al = [kit.sb(f"ah{v}", [P, KT, GT], F16) for v in range(2)], [kit.sb(f"al{v}", [P, KT, GT], F16) for v in range(2)]
        qh, ql = kit.sb("pqh", [P, KT, GT], F16), kit.sb("pql", [P, KT, GT], F16)
        res = [kit.sb(f"pres{j}", [P, D], F32) for j in range(2)]
        norm = Norm(kit, "n1")
        tr = Turner(kit, "proj", c)
        acc = [kit.ps(f"proj_acc{j}", [P, D]) for j in range(2)]
        w_in, wsplit, b_in, b_all = kit.sem("pw_in"), kit.sem("pw_split"), kit.sem("pb_in"), kit.sem("pb_all")
        a_in, x_in = [kit.sem(f"pa_in{v}") for v in range(2)], [kit.sem(f"px_in{v}") for v in range(2)]
        biased, summed, added, normed = kit.sem("p_biased"), kit.sem("p_summed"), kit.sem("p_added"), kit.sem("p_normed")
        x1_out, q_out = [kit.sem(f"px1_out{v}") for v in range(2)], kit.sem("pq_out")

        def next_bank(g, d):
            return g * (2 * KT) + KT + d

        def x1_bank(g, d):
            return g * (2 * KT) + 2 * KT + d

        with nc.Block() as block:
            @block.sync
            def _(sp):
                sp.dma_start(at[0][:], token_group(attn, 0)).then_inc(a_in[0], 16)
                for k in range(KT):
                    for s in range(4):
                        slot = 4 * k + s
                        head = (slot % 2) * (H // 2) + slot // 2
                        sp.dma_start(w32[s * HD:(s + 1) * HD, k, :], Wf[head * HD:(head + 1) * HD, :]).then_inc(w_in, 16)
                sp.dma_start(bfr[:], bf.rearrange("(o n) -> o n", o=1)).then_inc(b_in, 16)
                sp.dma_start(xs[0][:], token_group(x, 0)).then_inc(x_in[0], 16)
                sp.dma_start(at[1][:], token_group(attn, 1)).then_inc(a_in[1], 16)
                sp.dma_start(xs[1][:], token_group(x, 1)).then_inc(x_in[1], 16)
                sp.wait_ge(tr.turned, KT)
                with sp.Fori(0, NG // 2) as i:
                    for v in range(2):
                        g = i * 2 + v
                        sp.wait_ge(tr.turned, next_bank(g - 1, KT))
                        sp.dma_start(at[v][:], token_group(attn, (g + 2) % NG)).then_inc(a_in[v], 16)
                        sp.wait_ge(normed, g * TG + TG)
                        sp.dma_start(xs[v][:], token_group(x, (g + 2) % NG)).then_inc(x_in[v], 16)
                        sp.dma_start(token_group(x1_dram, g), x1[v][:]).then_inc(x1_out[v], 16)
                        sp.wait_ge(tr.lo_done, x1_bank(g, KT) + 2)
                        for j, src in enumerate((qh, ql)):
                            sp.dma_start(q_dram[j][i, :, v * GT:(v + 1) * GT].rearrange("(k p) t -> p k t", p=P),
                                         src[:]).then_inc(q_out, 16)
                sp.wait_ge(q_out, 32 * NG)
                for v in range(2):
                    sp.wait_ge(x1_out[v], 16 * (NG // 2))
                    sp.wait_ge(a_in[v], 16 * (NG // 2 + 1))
                    sp.wait_ge(x_in[v], 16 * (NG // 2 + 1))

            @block.gpsimd
            def _(pool):
                pool.wait_ge(b_in, 16)
                nc.gpsimd.partition_broadcast(bfb[:], bfr[:]).then_inc(b_all, 1)
                pool.wait_ge(b_all, 1)
                with pool.Fori(0, NG // 2) as i:
                    for v in range(2):
                        pool.wait_ge(x_in[v], i * 16 + 16)
                        for tt in range(TG):
                            nc.gpsimd.tensor_tensor(xs[v][:, tt, :], xs[v][:, tt, :], bfb[:], ALU.add).then_inc(biased, 1)

            @block.tensor
            def _(pe):
                pe.wait_ge(a_in[0], 16)
                for d in range(KT):
                    tr.turn(nc, pe, d, d, at[0])
                pe.wait_ge(wsplit, 2)
                pe.wait_ge(tr.lo_done, KT + 2)
                with pe.Fori(0, NG // 2) as i:
                    for v in range(2):
                        g = i * 2 + v
                        pe.wait_ge(tr.lo_done, next_bank(g - 1, KT) + 2)
                        for tt in range(TG):
                            pe.wait_ge(added, g * TG + tt + 1)
                            t = slice(tt * P, (tt + 1) * P)
                            split_matmuls(nc, acc[tt % 2][:], [(a[:, k, t], b[:, k, :]) for k in range(KT)
                                                               for a, b in ((ah[v], wh), (ah[v], wl), (al[v], wh))]).then_inc(summed, 1)
                        pe.wait_ge(a_in[1 - v], (i + v) * 16 + 16)
                        for d in range(KT):
                            tr.turn(nc, pe, next_bank(g, d), d, at[1 - v])
                        pe.wait_ge(normed, g * TG + TG)
                        for d in range(KT):
                            tr.turn(nc, pe, x1_bank(g, d), d, x1[v])

            @block.scalar
            def _(act):
                for d in range(KT):
                    tr.hi(nc, act, d, d, ah[0])
                with act.Fori(0, NG // 2) as i:
                    for v in range(2):
                        g = i * 2 + v
                        for tt in range(TG):
                            norm.square_root(nc, act, g * TG + tt, tt % 2)
                        for d in range(KT):
                            tr.hi(nc, act, next_bank(g, d), d, ah[1 - v])
                        act.wait_ge(q_out, g * 32)
                        for d in range(KT):
                            tr.hi(nc, act, x1_bank(g, d), d, qh)

            @block.vector
            def _(dve):
                tr.prime(dve)
                dve.sem_inc(added, 2)
                for d in range(KT):
                    tr.lo(nc, dve, d, d, ah[0], al[0])
                dve.wait_ge(w_in, 16 * 16)
                nc.vector.tensor_scalar(wh[:], w32[:], WSCALE, None, ALU.mult).then_inc(wsplit, 1)
                dve.wait_ge(wsplit, 1)
                nc.vector.scalar_tensor_tensor(out=wl[:].rearrange("p k n -> p (k n)"), in0=w32[:].rearrange("p k n -> p (k n)"), scalar=WSCALE,
                                               in1=wh[:].rearrange("p k n -> p (k n)"), op0=ALU.mult, op1=ALU.subtract).then_inc(wsplit, 1)
                with dve.Fori(0, NG // 2) as i:
                    for v in range(2):
                        g = i * 2 + v

                        def scale(tt):
                            norm.scale(nc, dve, g * TG + tt, tt % 2, x1[v][:, tt, :], res[tt % 2][:]).then_inc(normed, 1)

                        dve.wait_ge(x1_out[v], i * 16)
                        for tt in range(TG):
                            n, j = g * TG + tt, tt % 2
                            dve.wait_ge(summed, n + 1)
                            dve.wait_ge(biased, n + 1)
                            dve.wait_ge(normed, g * TG + max(tt - 1, 0))
                            nc.vector.scalar_tensor_tensor(out=res[j][:], in0=acc[j][:], scalar=1.0 / WSCALE, in1=xs[v][:, tt, :],
                                                           op0=ALU.mult, op1=ALU.add).then_inc(added, 1)
                            dve.wait_ge(added, n + 3)
                            norm.statistics(nc, dve, n, j, res[j][:])
                            if tt:
                                scale(tt - 1)
                        scale(TG - 1)
                        for d in range(KT):
                            tr.lo(nc, dve, next_bank(g, d), d, ah[1 - v], al[1 - v])
                        for d in range(KT):
                            tr.lo(nc, dve, x1_bank(g, d), d, qh, ql)


def second_norm_phase(nc, attn, x1_dram, x2, x2_dram, xmax, loads):
    NT = T // P
    with ExitStack() as ctx:
        kit = Kit(nc, ctx)
        NR = 4
        a = [kit.sb(f"sa{j}", [P, D], F32) for j in range(NR)]
        b = [kit.sb(f"sb{j}", [P, D], F32) for j in range(NR)]
        tmax = kit.sb("stmax", [P, NT], F32)
        norm = Norm(kit, "n2")
        t_in = [kit.sem(f"s_in{j}") for j in range(NR)]
        added, normed, maxed, done = kit.sem("s_added"), kit.sem("s_normed"), kit.sem("s_maxed"), kit.sem("s_done")
        x2_out, weights_in = kit.sem("s_x2_out"), kit.sem("s_weights")
        with nc.Block() as block:
            @block.sync
            def _(sp):
                with sp.Fori(0, NT // NR) as i:
                    for j in range(NR):
                        sp.wait_ge(normed, i * NR + j + 1)
                        for t, src in ((a, attn), (b, x1_dram)):
                            sp.dma_start(t[j][:], src[ds(i * (NR * P) + j * P, P), :]).then_inc(t_in[j], 16)

            @block.gpsimd
            def _(pool):
                with pool.Fori(0, NT // NR) as i:
                    for j in range(NR):
                        pool.wait_ge(t_in[j], i * 32 + 32)
                        nc.gpsimd.tensor_tensor(a[j][:], a[j][:], b[j][:], ALU.add).then_inc(added, 1)

            @block.scalar
            def _(act):
                for dst, src in loads:
                    act.dma_start(dst, src).then_inc(weights_in, 16)
                with act.Fori(0, NT // NR) as i:
                    for j in range(NR):
                        n = i * NR + j
                        norm.square_root(nc, act, n, j % 2)
                        if j:
                            act.wait_ge(normed, n + NR)
                            act.dma_start(x2_dram[ds(i * (NR * P) + (j - 1) * P, P), :], x2[:, ds((n - 1) * D, D)]).then_inc(x2_out, 16)
                    act.wait_ge(normed, i * NR + 2 * NR)
                    act.dma_start(x2_dram[ds(i * (NR * P) + (NR - 1) * P, P), :], x2[:, ds((i * NR + NR - 1) * D, D)]).then_inc(x2_out, 16)
                act.wait_ge(x2_out, 16 * NT)
                act.wait_ge(weights_in, 16 * len(loads))

            @block.vector
            def _(dve):
                dve.sem_inc(normed, NR)

                def statistics(i, j):
                    n = i * NR + j
                    dve.wait_ge(added, n + 1)
                    norm.statistics(nc, dve, n, j % 2, a[j][:])

                def scale(i, j):
                    n = i * NR + j
                    norm.scale(nc, dve, n, j % 2, x2[:, ds(n * D, D)], a[j][:]).then_inc(normed, 1)

                def maximum(i, j):
                    n = i * NR + j
                    dve.wait_ge(normed, n + NR + 1)
                    nc.vector.tensor_reduce(tmax[:, ds(n, 1)], x2[:, ds(n * D, D)], AX.X, ALU.max,
                                            apply_absolute_value=True).then_inc(maxed, 1)

                with dve.Fori(0, NT // NR) as i:
                    statistics(i, 0)
                    for j in range(NR):
                        if j < NR - 1:
                            statistics(i, j + 1)
                        scale(i, j)
                        maximum(i, j)
                dve.wait_ge(maxed, NT)
                nc.vector.tensor_reduce(xmax[:], tmax[:], AX.X, ALU.max).then_inc(done, 1)
                dve.wait_ge(done, 1)


def quantisers(nc, name, of):
    with ExitStack() as ctx:
        kit = Kit(nc, ctx)
        amax = [kit.sb(f"{name}_amax{j}", [P, 1], F32) for j in range(len(of))]
        reduced, steps = kit.sem(f"{name}_reduced"), kit.sem(f"{name}_steps")
        with nc.Block() as block:
            @block.gpsimd
            def _(pool):
                for j, (pmax, scale, inverse) in enumerate(of):
                    nc.gpsimd.partition_all_reduce(amax[j][:], pmax[:], P, RMAX).then_inc(reduced, 1)

            @block.vector
            def _(dve):
                for j, (pmax, scale, inverse) in enumerate(of):
                    dve.wait_ge(reduced, j + 1)
                    nc.vector.tensor_scalar(scale[:], amax[j][:], 1.0 / QMAX, 1e-12, ALU.mult, ALU.max).then_inc(steps, 1)
                    dve.wait_ge(steps, 2 * j + 1)
                    nc.vector.reciprocal(inverse[:], scale[:]).then_inc(steps, 1)
                    dve.wait_ge(steps, 2 * j + 2)


def gate_phase(nc, c, x2, scale, inverse, wts, y_dram, x_dram, gmax):
    with ExitStack() as ctx:
        kit = Kit(nc, ctx)
        xq = [kit.sb(f"gt_xq{v}", [P, TG, D], F32) for v in range(2)]
        xh = [kit.sb(f"gt_xh{v}", [P, KT, GT], F16) for v in range(2)]
        xl = [kit.sb(f"gt_xl{v}", [P, KT, GT], F16) for v in range(2)]
        y = [kit.sb(f"gt_y{j}", [P, GT], F32) for j in range(4)]
        tmax = kit.sb("gt_tmax", [P, NG * FT], F32)
        yscale = kit.sb("gt_ysc", [P, 1], F32)
        tr = Turner(kit, "gate", c)
        acc = [kit.ps(f"gt_acc{j}", [P, GT]) for j in range(4)]
        scaled, added, rounded = kit.sem("gt_scaled"), kit.sem("gt_added"), kit.sem("gt_rounded")
        summed, out_done, maxed = kit.sem("gt_summed"), kit.sem("gt_out"), kit.sem("gt_maxed")
        stored = [kit.sem(f"gt_stored{j}") for j in range(4)]
        x_out = [kit.sem(f"gt_x_out{v}") for v in range(2)]
        EARLY = {4: 0, 5: 1, 6: 2, 7: 3}
        hi, lo = wts
        with nc.Block() as block:
            @block.sync
            def _(sp):
                with sp.Fori(0, NG // 2) as i:
                    for v in range(2):
                        g = i * 2 + v
                        sp.wait_ge(tr.lo_done, g * KT + KT + 2)
                        for j, src in enumerate((xh, xl)):
                            sp.dma_start(x_dram[j][ds(g, 1)].rearrange("o p n -> (o p) n"), src[v][:].rearrange("p k t -> p (k t)")).then_inc(x_out[v], 16)
                        for o in range(FT):
                            sp.wait_ge(out_done, g * FT + o + 1)
                            sp.dma_start(y_dram[o, :, ds(g * GT, GT)], y[o % 4][:]).then_inc(stored[o % 4], 16)
                for j in range(4):
                    sp.wait_ge(stored[j], 16 * NG * FT // 4)
                for v in range(2):
                    sp.wait_ge(x_out[v], 32 * NG // 2)

            @block.tensor
            def _(pe):
                pe.wait_ge(rounded, 1)
                for d in range(KT):
                    tr.turn(nc, pe, d, d, xq[0])
                with pe.Fori(0, NG // 2) as i:
                    for v in range(2):
                        g = i * 2 + v
                        pe.wait_ge(tr.lo_done, g * KT + KT + 2)
                        for o in range(FT):
                            pe.wait_ge(maxed, g * FT + o + 1)
                            split_matmuls(nc, acc[o % 4][:], [(a[:, o, k, :], b[:, k, :]) for k in range(KT)
                                                              for a, b in ((hi, xh[v]), (hi, xl[v]), (lo, xh[v]))]).then_inc(summed, 1)
                            if o in EARLY:
                                pe.wait_ge(rounded, g + 2)
                                tr.turn(nc, pe, g * KT + KT + EARLY[o], EARLY[o], xq[1 - v])

            @block.scalar
            def _(act):
                for d in range(KT):
                    tr.hi(nc, act, d, d, xh[0])
                act.wait_ge(scaled, 1)
                with act.Fori(0, NG // 2) as i:
                    for v in range(2):
                        g = i * 2 + v
                        for o in range(FT):
                            act.wait_ge(summed, g * FT + o + 1)
                            act.wait_ge(maxed, g * FT + o + 1)
                            act.wait_ge(stored[o % 4], g * (16 * FT // 4) + o // 4 * 16)
                            nc.scalar.activation(y[o % 4][:], acc[o % 4][:], ACT.Copy, scale=yscale[:, 0:1]).then_inc(out_done, 1)
                            if o in EARLY:
                                if EARLY[o] == 0:
                                    act.wait_ge(x_out[1 - v], (i + v) * 32)
                                tr.hi(nc, act, g * KT + KT + EARLY[o], EARLY[o], xh[1 - v])

            @block.vector
            def _(dve):
                tr.prime(dve)
                dve.sem_inc(maxed, 4)
                nc.vector.tensor_scalar(yscale[:], scale[:], 1.0 / FSCALE, None, ALU.mult).then_inc(scaled, 1)

                def quantise(g, v):
                    nc.vector.tensor_scalar(xq[v][:].rearrange("p t n -> p (t n)"), x2[:, ds(g % NG * (TG * D), TG * D)], inverse[:, 0:1], MAGIC,
                                            ALU.mult, ALU.add).then_inc(added, 1)
                    dve.wait_ge(added, g + 1)
                    nc.vector.tensor_scalar(xq[v][:], xq[v][:], -MAGIC, None, ALU.add).then_inc(rounded, 1)

                quantise(0, 0)
                for d in range(KT):
                    tr.lo(nc, dve, d, d, xh[0], xl[0])
                with dve.Fori(0, NG // 2) as i:
                    for v in range(2):
                        g = i * 2 + v
                        for o in range(FT):
                            if o == 1:
                                quantise(g + 1, 1 - v)
                            dve.wait_ge(out_done, g * FT + o + 1)
                            nc.vector.tensor_reduce(tmax[:, ds(g * FT + o, 1)], y[o % 4][:], AX.X, ALU.max,
                                                    apply_absolute_value=True).then_inc(maxed, 1)
                            if o in EARLY:
                                tr.lo(nc, dve, g * KT + KT + EARLY[o], EARLY[o], xh[1 - v], xl[1 - v])
                dve.wait_ge(maxed, FT * NG + 4)
                nc.vector.tensor_reduce(gmax[:], tmax[:], AX.X, ALU.max).then_inc(scaled, 1)
                dve.wait_ge(scaled, 2)


def up_phase(nc, x_dram, scale, wts, gate_dram, sg, isg, y_dram, res, h_dram, ymax, hmax):
    NR = 4
    with ExitStack() as ctx:
        kit = Kit(nc, ctx)
        xh = [kit.sb(f"v_xh{v}", [P, KT * GT], F16) for v in range(2)]
        xl = [kit.sb(f"v_xl{v}", [P, KT * GT], F16) for v in range(2)]
        y = [kit.sb(f"v_y{j}", [P, GT], F32) for j in range(NR)]
        ga = [kit.sb(f"v_g{j}", [P, GT], F32) for j in range(NR)]
        ra = [kit.sb(f"v_r{j}", [P, GT], F32) for j in range(2)]
        qa = [kit.sb(f"v_q{j}", [P, GT], F32) for j in range(NR)]
        sa = [kit.sb(f"v_s{j}", [P, GT], F32) for j in range(2)]
        sq = [kit.sb(f"v_t{j}", [P, GT], F32) for j in range(2)]
        h = [kit.sb(f"v_h{j}", [P, GT], F32) for j in range(NR)]
        magic, yscale, gscale = kit.sb("v_magic", [P, 1], F32), kit.sb("v_ysc", [P, 1], F32), kit.sb("v_gsc", [P, 1], F32)
        ytmax, htmax = kit.sb("v_ytmax", [P, NG * FT], F32), kit.sb("v_htmax", [P, NG * FT], F32)
        acc = [kit.ps(f"v_acc{j}", [P, GT]) for j in range(4)]
        x_in = [kit.sem(f"v_x_in{v}") for v in range(2)]
        g_in = [kit.sem(f"v_g_in{j}") for j in range(NR)]
        y_out, h_out = [kit.sem(f"v_y_out{j}") for j in range(NR)], [kit.sem(f"v_h_out{j}") for j in range(NR)]
        ready, summed, evicted, ymaxed = (kit.sem(f"v_{n}") for n in ("ready", "summed", "evicted", "ymaxed"))
        added, deq, sig, inc, clipped, prod, hmaxed, done, stood = (kit.sem(f"v_{n}") for n in (
            "added", "deq", "sig", "in_units", "clipped", "prod", "hmaxed", "done", "stood"))
        hi, lo = wts
        RES = res.shape[1] // T

        def y_stores(o):
            return sum(1 for p in range(o) if p % NR == o % NR and p >= RES)

        with nc.Block() as block:
            @block.sync
            def _(sp):
                def load_x(g, v):
                    for j, dst in enumerate((xh, xl)):
                        sp.dma_start(dst[v][:], x_dram[j][ds(g % NG, 1)].rearrange("o p n -> (o p) n")).then_inc(x_in[v], 16)

                for v in range(2):
                    load_x(v, v)
                for o in range(NR):
                    sp.dma_start(ga[o][:], gate_dram[o, :, 0:GT]).then_inc(g_in[o], 16)
                with sp.Fori(0, NG // 2) as i:
                    for v in range(2):
                        g = i * 2 + v
                        for o in range(FT):
                            n = g * FT + o
                            sp.wait_ge(added, n + 1)
                            sp.dma_start(ga[o % NR][:], gate_dram[(o + NR) % FT, :, ds((g + (o + NR) // FT) % NG * GT, GT)]).then_inc(g_in[o % NR], 16)
                            if o >= RES:
                                sp.wait_ge(evicted, n + 5)
                                sp.dma_start(y_dram[o, :, ds(g * GT, GT)], y[o % NR][:]).then_inc(y_out[o % NR], 16)
                            sp.wait_ge(prod, n + 3)
                            sp.sem_inc(stood, 1)
                            sp.dma_start(h_dram[o, :, ds(g * GT, GT)], h[o % NR][:]).then_inc(h_out[o % NR], 16)
                        sp.wait_ge(summed, g * FT + FT)
                        load_x(g + 2, v)
                for j in range(NR):
                    sp.wait_ge(y_out[j], 16 * NG * sum(1 for o in range(RES, FT) if o % NR == j))
                    sp.wait_ge(h_out[j], 16 * NG * FT // NR)
                    sp.wait_ge(g_in[j], 16 * (NG * FT // NR + 1))
                for v in range(2):
                    sp.wait_ge(x_in[v], 32 * (NG // 2 + 1))

            @block.tensor
            def _(pe):
                with pe.Fori(0, NG // 2) as i:
                    for v in range(2):
                        g = i * 2 + v
                        pe.wait_ge(x_in[v], i * 32 + 32)
                        part = lambda t, k: t[v][:, k * GT:(k + 1) * GT]
                        for o in range(FT):
                            pe.wait_ge(evicted, g * FT + o + 1)
                            split_matmuls(nc, acc[o % 4][:], [(a[:, o, k, :], part(b, k)) for k in range(KT)
                                                              for a, b in ((hi, xh), (hi, xl), (lo, xh))]).then_inc(summed, 1)

            @block.scalar
            def _(act):
                act.sem_inc(evicted, 4)

                def front(n, o, i, v):
                    count = (i * 2 + v) * (16 * FT // NR) + o // NR * 16 + 16
                    act.wait_ge(g_in[o % NR], count)
                    act.wait_ge(deq, n + 1)
                    nc.scalar.activation(ra[o % 2][:], ga[o % NR][:], ACT.Identity, scale=isg[:, 0:1], bias=magic[:, 0:1]).then_inc(added, 1)

                act.wait_ge(ready, 3)
                front(0, 0, 0, 0)
                with act.Fori(0, NG // 2) as i:
                    for v in range(2):
                        g = i * 2 + v
                        for o in range(FT):
                            n = g * FT + o
                            front(n + 1, o + 1, i, v)
                            act.wait_ge(deq, n + 3)
                            act.wait_ge(inc, n + 1)
                            nc.scalar.activation(sa[o % 2][:], qa[o % NR][:], ACT.Sigmoid, scale=65536.0).then_inc(sig, 1)
                            act.wait_ge(summed, n + 1)
                            if o < RES:
                                out = res[:, ds(g * GT + o * T, GT)]
                            else:
                                act.wait_ge(ymaxed, n + 1)
                                act.wait_ge(y_out[o % NR], g * (16 * y_stores(FT + o % NR)) + 16 * y_stores(o))
                                out = y[o % NR][:]
                            nc.scalar.activation(out, acc[o % 4][:], ACT.Copy, scale=yscale[:, 0:1]).then_inc(evicted, 1)

            @block.gpsimd
            def _(pool):
                pool.sem_inc(inc, 2)
                pool.sem_inc(prod, 2)

                with pool.Fori(0, NG // 2) as i:
                    for v in range(2):
                        g = i * 2 + v
                        for o in range(FT):
                            n = g * FT + o
                            pool.wait_ge(sig, n + 1)
                            pool.wait_ge(prod, n + 1)
                            pool.sem_inc(stood, 1)
                            nc.gpsimd.tensor_scalar(sq[o % 2][:], sa[o % 2][:], 65536.0, MAGIC, ALU.mult, ALU.add).then_inc(inc, 1)
                            pool.wait_ge(clipped, n + 1)
                            pool.wait_ge(h_out[o % NR], g * (16 * FT // NR) + o // NR * 16)
                            pool.wait_ge(hmaxed, n + 1)
                            nc.gpsimd.tensor_tensor(h[o % NR][:], sq[o % 2][:], qa[o % NR][:], ALU.mult).then_inc(prod, 1)

            @block.vector
            def _(dve):
                dve.sem_inc(deq, 2)
                dve.sem_inc(ymaxed, 4)
                dve.sem_inc(hmaxed, 4)
                nc.vector.memset(magic[:], MAGIC).then_inc(ready, 1)
                nc.vector.tensor_scalar(yscale[:], scale[:], 1.0 / FSCALE, None, ALU.mult).then_inc(ready, 1)
                nc.vector.tensor_scalar(gscale[:], sg[:], 1.0 / 65536.0, None, ALU.mult).then_inc(ready, 1)
                dve.wait_ge(ready, 3)

                def front(n, o):
                    dve.wait_ge(added, n + 1)
                    nc.vector.tensor_scalar(qa[o % NR][:], ra[o % 2][:], -MAGIC, gscale[:, 0:1], ALU.add, ALU.mult).then_inc(deq, 1)

                def hreduce(n, o):
                    dve.wait_ge(prod, n + 3)
                    nc.vector.tensor_reduce(htmax[:, ds(n, 1)], h[o % NR][:], AX.X, ALU.max, apply_absolute_value=True).then_inc(hmaxed, 1)

                front(0, 0)
                with dve.Fori(0, NG // 2) as i:
                    for v in range(2):
                        g = i * 2 + v
                        for o in range(FT):
                            n = g * FT + o
                            front(n + 1, o + 1)
                            dve.wait_ge(inc, n + 3)
                            nc.vector.tensor_scalar(sq[o % 2][:], sq[o % 2][:], -MAGIC, 65535.0, ALU.add, ALU.min).then_inc(clipped, 1)
                            dve.wait_ge(evicted, n + 5)
                            out = res[:, ds(g * GT + o * T, GT)] if o < RES else y[o % NR][:]
                            nc.vector.tensor_reduce(ytmax[:, ds(n, 1)], out, AX.X, ALU.max, apply_absolute_value=True).then_inc(ymaxed, 1)
                            hreduce(n, o)
                dve.wait_ge(ymaxed, FT * NG + 4)
                nc.vector.tensor_reduce(ymax[:], ytmax[:], AX.X, ALU.max).then_inc(done, 1)
                dve.wait_ge(hmaxed, FT * NG + 4)
                nc.vector.tensor_reduce(hmax[:], htmax[:], AX.X, ALU.max).then_inc(done, 1)
                dve.wait_ge(done, 2)


def product_phase(nc, h_dram, y_dram, res, ish, isu, o_dram, omax):
    W, NR = 1024, 4
    TR = T // W
    flat = lambda t: t.rearrange("f p t -> (f p) t")
    with ExitStack() as ctx:
        kit = Kit(nc, ctx)
        h = [kit.sb(f"j_h{j}", [P, W], F32) for j in range(NR)]
        u = [kit.sb(f"j_u{j}", [P, W], F32) for j in range(NR)]
        o = [kit.sb(f"j_o{j}", [P, W], F32) for j in range(NR)]
        magic = kit.sb("j_magic", [P, 1], F32)
        tmax = kit.sb("j_tmax", [P, FT * TR], F32)
        h_in, u_in, stored = ([kit.sem(f"j_{n}{j}") for j in range(NR)] for n in ("h_in", "u_in", "out"))
        ready, added, cut, prod, maxed, done, stood = (kit.sem(f"j_{n}") for n in ("ready", "added", "cut", "prod", "maxed", "done", "stood"))
        RES = res.shape[1] // T
        with nc.Block() as block:
            @block.sync
            def _(sp):
                def load(f, j, up):
                    sp.dma_start(h[j][:], flat(h_dram)[ds(f * P, P), j * W:(j + 1) * W]).then_inc(h_in[j], 16)
                    if up:
                        sp.dma_start(u[j][:], flat(y_dram)[ds(f * P, P), j * W:(j + 1) * W]).then_inc(u_in[j], 16)

                for j in range(NR):
                    load(0, j, False)
                for f in range(RES):
                    for j in range(NR):
                        sp.wait_ge(prod, f * NR + j + 1)
                        load(f + 1, j, f + 1 >= RES)

                def store(f, last):
                    for j in range(NR):
                        sp.wait_ge(prod, f * NR + (j + 1))
                        if not last:
                            load(f + 1, j, True)
                        sp.dma_start(flat(o_dram)[ds(f * P, P), j * W:(j + 1) * W], o[j][:]).then_inc(stored[j], 16)

                with sp.Fori(RES, FT - 1) as f:
                    store(f, False)
                store(FT - 1, True)
                for j in range(NR):
                    sp.wait_ge(stored[j], 16 * (FT - RES))

            def over_rows(eng, body):
                for f in range(RES):
                    for j in range(TR):
                        body(f, j, True)
                with eng.Fori(RES, FT) as f:
                    for j in range(TR):
                        body(f, j, False)

            def up_tile(f, j, resident):
                return res[:, f * T + j * W:f * T + (j + 1) * W] if resident else u[j][:]

            @block.scalar
            def _(act):
                act.wait_ge(ready, 1)

                def body(f, j, resident):
                    act.wait_ge(h_in[j], f * 16 + 16)
                    nc.scalar.activation(h[j][:], h[j][:], ACT.Identity, scale=ish[:, 0:1], bias=magic[:, 0:1]).then_inc(added, 1)
                    if not resident:
                        act.wait_ge(u_in[j], (f - RES) * 16 + 16)
                    nc.scalar.activation(up_tile(f, j, resident), up_tile(f, j, resident), ACT.Identity,
                                         scale=isu[:, 0:1], bias=magic[:, 0:1]).then_inc(added, 1)
                over_rows(act, body)

            @block.gpsimd
            def _(pool):
                def body(f, j, resident):
                    pool.wait_ge(added, (f * TR + j) * 2 + 2)
                    pool.sem_inc(stood, 1)
                    nc.gpsimd.tensor_scalar(up_tile(f, j, resident), up_tile(f, j, resident), 1.0, -MAGIC, ALU.mult, ALU.add).then_inc(cut, 1)
                over_rows(pool, body)

            @block.vector
            def _(dve):
                nc.vector.memset(magic[:], MAGIC).then_inc(ready, 1)

                def body(f, j, resident):
                    n = f * TR + j
                    dve.wait_ge(cut, n + 1)
                    if resident:
                        out = up_tile(f, j, True)
                    else:
                        out = o[j][:]
                        dve.wait_ge(stored[j], (f - RES) * 16)
                    nc.vector.scalar_tensor_tensor(out=out, in0=h[j][:], scalar=-MAGIC, in1=up_tile(f, j, resident),
                                                   op0=ALU.add, op1=ALU.mult).then_inc(prod, 1)
                    dve.wait_ge(prod, n + 1)
                    nc.vector.tensor_reduce(tmax[:, ds(n, 1)], out, AX.X, ALU.max, apply_absolute_value=True).then_inc(maxed, 1)

                over_rows(dve, body)
                dve.wait_ge(maxed, FT * TR)
                nc.vector.tensor_reduce(omax[:], tmax[:], AX.X, ALU.max).then_inc(done, 1)
                dve.wait_ge(done, 1)


def product_quantiser(nc, omax, sh, su, so, iso):
    with ExitStack() as ctx:
        kit = Kit(nc, ctx)
        amax, unit, inv = (kit.sb(f"qo_{n}", [P, 1], F32) for n in ("amax", "unit", "inv"))
        reduced, steps = kit.sem("qo_reduced"), kit.sem("qo_steps")
        with nc.Block() as block:
            @block.gpsimd
            def _(pool):
                nc.gpsimd.partition_all_reduce(amax[:], omax[:], P, RMAX).then_inc(reduced, 1)

            @block.vector
            def _(dve):
                nc.vector.tensor_tensor(unit[:], sh[:], su[:], ALU.mult).then_inc(steps, 1)
                dve.wait_ge(reduced, 1)
                dve.wait_ge(steps, 1)
                nc.vector.tensor_tensor(amax[:], amax[:], unit[:], ALU.mult).then_inc(steps, 1)
                dve.wait_ge(steps, 2)
                nc.vector.tensor_scalar(so[:], amax[:], 1.0 / QMAX, 1e-12, ALU.mult, ALU.max).then_inc(steps, 1)
                dve.wait_ge(steps, 3)
                nc.vector.reciprocal(inv[:], so[:]).then_inc(steps, 1)
                dve.wait_ge(steps, 4)
                nc.vector.tensor_tensor(iso[:], inv[:], unit[:], ALU.mult).then_inc(steps, 1)
                dve.wait_ge(steps, 5)


def down_phase(nc, o_dram, res, so, iso, wd, x2_dram, out):
    with ExitStack() as ctx:
        kit = Kit(nc, ctx)
        RES = res.shape[1] // T
        o32 = [kit.sb(f"d_o{v}", [P, FT - RES, GT], F32) for v in range(2)]
        r32 = [kit.sb(f"d_t{j}", [P, GT], F32) for j in range(4)]
        oh = [kit.sb(f"d_oh{v}", [P, FT, GT], F16) for v in range(2)]
        ol = [kit.sb(f"d_ol{v}", [P, FT, GT], F16) for v in range(2)]
        xt = [kit.sb(f"d_x{j}", [P, D], F32) for j in range(4)]
        rs = [kit.sb(f"d_r{j}", [P, D], F32) for j in range(2)]
        fin = [kit.sb(f"d_f{j}", [P, D], F32) for j in range(2)]
        magic, ysc = kit.sb("d_magic", [P, 1], F32), kit.sb("d_ysc", [P, 1], F32)
        norm = Norm(kit, "n3")
        acc = [kit.ps(f"d_acc{j}", [P, D]) for j in range(2)]
        o_in = [kit.sem(f"d_in{v}") for v in range(2)]
        x_in = [kit.sem(f"d_x_in{j}") for j in range(4)]
        f_out = [kit.sem(f"d_out{j}") for j in range(2)]
        ready, rounded, hi_done, lo_done, summed, added, normed = (kit.sem(f"d_{n}") for n in (
            "ready", "rounded", "hi", "lo", "summed", "added", "normed"))
        wh, wl = wd
        with nc.Block() as block:
            @block.sync
            def _(sp):
                def load_o(g, v):
                    sp.dma_start(o32[v][:], o_dram[RES:FT, :, ds(g * GT, GT)].rearrange("f p t -> p f t")).then_inc(o_in[v], 16)

                for v in range(2):
                    load_o(v, v)
                for j in range(4):
                    sp.dma_start(xt[j][:], x2_dram[j * P:(j + 1) * P, :]).then_inc(x_in[j], 16)
                with sp.Fori(0, NG // 2) as i:
                    for v in range(2):
                        g = i * 2 + v
                        sp.wait_ge(rounded, g * FT + FT)
                        load_o((g + 2) % NG, v)
                        for tt in range(TG):
                            n = g * TG + tt
                            sp.wait_ge(added, n + 3)
                            sp.dma_start(xt[tt][:], x2_dram[ds((g + 1) % NG * GT + tt * P, P), :]).then_inc(x_in[tt], 16)
                            sp.wait_ge(normed, n + 1)
                            sp.dma_start(out[ds(n * P, P), :], fin[tt % 2][:]).then_inc(f_out[tt % 2], 16)
                for v in range(2):
                    sp.wait_ge(f_out[v], 16 * T // P // 2)
                    sp.wait_ge(o_in[v], 16 * (NG // 2 + 1))
                for j in range(4):
                    sp.wait_ge(x_in[j], 16 * (NG + 1))

            @block.tensor
            def _(pe):
                with pe.Fori(0, NG // 2) as i:
                    for v in range(2):
                        g = i * 2 + v
                        for tt in range(TG):
                            pe.wait_ge(added, g * TG + tt + 1)
                            t = slice(tt * P, (tt + 1) * P)
                            n = 0
                            for k in range(FT):
                                if tt == 0:
                                    pe.wait_ge(lo_done, g * FT + k + 1)
                                for a, b in ((oh[v], wh), (oh[v], wl), (ol[v], wh)):
                                    mm = nc.tensor.matmul(acc[tt % 2][:], a[:, k, t], b[:, k, :], start=(n == 0), stop=(n == 3 * FT - 1))
                                    n += 1
                            mm.then_inc(summed, 1)

            @block.scalar
            def _(act):
                act.wait_ge(ready, 2)

                def round_row(g, v, f):
                    act.wait_ge(lo_done, g * FT + max(f - 3, 0))
                    src = res[:, ds(g % NG * GT + f * T, GT)] if f < RES else o32[v][:, f - RES]
                    nc.scalar.activation(r32[f % 4][:], src, ACT.Identity, scale=iso[:, 0:1], bias=magic[:, 0:1]).then_inc(rounded, 1)

                act.wait_ge(o_in[0], 16)
                for f in range(FT):
                    round_row(0, 0, f)
                with act.Fori(0, NG // 2) as i:
                    for v in range(2):
                        g = i * 2 + v
                        act.wait_ge(o_in[1 - v], (i + v) * 16 + 16)
                        for tt in range(TG):
                            for f in range(tt * 3, tt * 3 + 3):
                                round_row(g + 1, 1 - v, f)
                            norm.square_root(nc, act, g * TG + tt, tt % 2)

            @block.vector
            def _(dve):
                dve.sem_inc(added, 2)
                nc.vector.memset(magic[:], MAGIC).then_inc(ready, 1)
                nc.vector.tensor_scalar(ysc[:], so[:], 1.0 / FSCALE, None, ALU.mult).then_inc(ready, 1)
                dve.wait_ge(ready, 2)

                def split(n0, v, f):
                    dve.wait_ge(rounded, n0 + f + 1)
                    nc.vector.tensor_scalar(oh[v][:, f], r32[f % 4][:], -MAGIC, None, ALU.add).then_inc(hi_done, 1)
                    dve.wait_ge(hi_done, n0 + f + 1)
                    nc.vector.scalar_tensor_tensor(out=ol[v][:, f], in0=r32[f % 4][:], scalar=-MAGIC, in1=oh[v][:, f],
                                                   op0=ALU.add, op1=ALU.subtract).then_inc(lo_done, 1)

                for f in range(FT):
                    split(0, 0, f)
                with dve.Fori(0, NG // 2) as i:
                    for v in range(2):
                        g = i * 2 + v
                        dve.wait_ge(summed, g * TG)
                        for tt in range(TG):
                            n, j = g * TG + tt, tt % 2
                            for f in range(tt * 3, tt * 3 + 3):
                                split((g + 1) * FT, 1 - v, f)
                            dve.wait_ge(summed, n + 1)
                            dve.wait_ge(normed, n)
                            dve.wait_ge(x_in[tt], g * 16 + 16)
                            nc.vector.scalar_tensor_tensor(out=rs[j][:], in0=acc[j][:], scalar=ysc[:, 0:1], in1=xt[tt][:],
                                                           op0=ALU.mult, op1=ALU.add).then_inc(added, 1)
                            dve.wait_ge(added, n + 3)
                            norm.statistics(nc, dve, n, j, rs[j][:])
                            dve.wait_ge(f_out[j], g * 32 + tt // 2 * 16)
                            norm.scale(nc, dve, n, j, fin[j][:], rs[j][:]).then_inc(normed, 1)


def feed_forward(nc, c, attn2, x1_dram, w_dram, scratch, out):
    x2_dram = scratch("scr_x2", [T, D], F32)
    x_dram = [scratch(f"scr_xq_{n}", [NG, P, KT * GT], F16) for n in ("hi", "lo")]
    gate_dram, up_dram, h_dram, o_dram = (scratch(f"scr_{n}", [FT, P, T], F32) for n in ("gate", "up", "h", "o"))
    with ExitStack() as ctx:
        kit = Kit(nc, ctx)
        names = ("x", "gate", "up", "h", "o")
        pmax, scale, inverse = ({n: kit.sb(f"{k}_{n}", [P, 1], F32) for n in names} for k in ("pmax", "scale", "inverse"))
        of = lambda n: (pmax[n], scale[n], inverse[n])
        wd = [kit.sb(f"wd_{n}", [P, FT, D], F16) for n in ("hi", "lo")]
        wu = [kit.sb(f"wu_{n}", [P, FT, KT, P], F16) for n in ("hi", "lo")]
        with ExitStack() as inner:
            k2 = Kit(nc, inner)
            wg = [k2.sb(f"wg_{n}", [P, FT, KT, P], F16) for n in ("hi", "lo")]
            x2 = k2.sb("x2", [P, T // P * D], F32)
            loads = [(w[j][:].rearrange("p t k n -> p t (k n)"), w_dram[j][m * FT:(m + 1) * FT].rearrange("t p n -> p t n"))
                     for m, w in enumerate((wg, wu)) for j in range(2)]
            loads += [(wd[j][:, k * KT:(k + 1) * KT, r * P:(r + 1) * P], w_dram[j][2 * FT + r * 3 + k].rearrange("p (q n) -> p q n", n=P))
                      for j in range(2) for r in range(KT) for k in range(3)]
            second_norm_phase(nc, attn2, x1_dram, x2, x2_dram, pmax["x"], loads)
            quantisers(nc, "qx", [of("x")])
            gate_phase(nc, c, x2, scale["x"], inverse["x"], wg, gate_dram, x_dram, pmax["gate"])
        res = kit.sb("up_rows", [P, 3 * T], F32)
        quantisers(nc, "qg", [of("gate")])
        up_phase(nc, x_dram, scale["x"], wu, gate_dram, scale["gate"], inverse["gate"], up_dram, res, h_dram,
                 pmax["up"], pmax["h"])
        quantisers(nc, "quh", [of("up"), of("h")])
        product_phase(nc, h_dram, up_dram, res, inverse["h"], inverse["up"], o_dram, pmax["o"])
        product_quantiser(nc, pmax["o"], scale["h"], scale["up"], scale["o"], inverse["o"])
        down_phase(nc, o_dram, res, scale["o"], inverse["o"], wd, x2_dram, out)


def decoder_layer(nc, x, context, mask, Wq, bq, Wk, bk, Wv, bv, Wf, bf, w_gate, w_up, w_down, out):
    x = x.rearrange("b s d -> (b s) d")
    context = context.rearrange("b s d -> (b s) d")
    mask = mask.rearrange("b o q k -> (b o q) k")
    out = out.rearrange("b s d -> (b s) d")

    def scratch(name, shape, dt):
        return nc.dram_tensor(name, shape, dt).ap()

    qk_dram = [scratch(f"scr_{n}", [B, D, S], F16) for n in ("q_hi", "q_lo", "k_hi", "k_lo")]
    q2_dram = [scratch(f"scr_q2_{n}", [B, D, S], F16) for n in ("hi", "lo")]
    k2_dram = [scratch(f"scr_k2_{n}", [B, D, S], F16) for n in ("hi", "lo")]
    v_dram, v2_dram = scratch("scr_v", [B * H, P, ST, VW], F16), scratch("scr_v2", [B * H, P, ST, VW], F16)
    mb_dram, nm_dram = scratch("scr_mb", [T, S], BF16), scratch("scr_nm", [B, S, S], F16)
    w_dram = [scratch(f"scr_w_{n}", [3 * FT, P, KT * P], F16) for n in ("hi", "lo")]
    attn, attn2, x1_dram = (scratch(n, [T, D], F32) for n in ("scr_attn", "scr_attn2", "scr_x1"))

    with ExitStack() as ctx:
        c = make_identities(nc, Kit(nc, ctx))
        preparation_phase(nc, c, x, Wq, bq, Wk, bk, Wv, bv, qk_dram, v_dram, context, k2_dram, v2_dram,
                          mask, mb_dram, nm_dram, (w_gate, w_up, w_down), w_dram)
        attention_phase(nc, c, "self", True, qk_dram[0:2], qk_dram[2:4], v_dram, attn)
        projection_phase(nc, c, attn, x, Wf, bf, x1_dram, q2_dram)
        attention_phase(nc, c, "cross", False, q2_dram, k2_dram, v2_dram, attn2, mb_dram, nm_dram)
        feed_forward(nc, c, attn2, x1_dram, w_dram, scratch, out)


_INS = ["x", "ctx_1024", "mask_Bx1xSxS2_ik1", "L0_attn_Wq", "L0_attn_bq", "L0_attn_Wk", "L0_attn_bk", "L0_attn_Wv",
        "L0_attn_bv", "L0_attn_Wf", "L0_attn_bf", "L0_ffn_w_gate", "L0_ffn_w_up", "L0_ffn_w_down"]


def kernel(**inputs):
    import concourse.bacc as bacc
    from concourse.bass_utils import run_bass_kernel_spmd

    nc = bacc.Bacc("TRN2", target_bir_lowering=False, num_devices=1)
    arrays, args = {}, []
    for name in _INS:
        a = np.ascontiguousarray(inputs[name])
        arrays[f"in_{name}"] = a
        args.append(nc.dram_tensor(f"in_{name}", a.shape, mybir.dt.from_np(a.dtype), kind="ExternalInput").ap())
    args.append(nc.dram_tensor("out_0", (B, S, D), F32, kind="ExternalOutput").ap())
    decoder_layer(nc, *args)
    r = run_bass_kernel_spmd(nc, [arrays], core_ids=[0])
    return r.results[0]["out_0"]
```

```python
from contextlib import ExitStack

import numpy as np

import concourse.bass as bass
from concourse import mybir

F32 = mybir.dt.float32
F16 = mybir.dt.float16
BF16 = mybir.dt.bfloat16
I32 = mybir.dt.int32
ALU = mybir.AluOpType
ACT = mybir.ActivationFunctionType
AX = mybir.AxisListType
RMAX = bass.bass_isa.ReduceOp.max
ds = bass.ds

P = 128
B, S, D = 4, 1024, 512
H, HD = 16, 32
F = 1536
T = B * S
KT = D // P
FT = F // P
ST = S // P
GT = 512
NG = T // GT
TG = GT // P
VW = 2 * HD + 1
WSCALE = 64.0
FSCALE = 1024.0
BIG = 32768.0
SM = float(1.0 / np.sqrt(HD))
MAGIC = 12582912.0
QMAX = 32767.0
EPS = 1e-5
RES = 6


class Kit:

    def __init__(self, nc, ctx):
        self.nc, self.ctx, self.sems = nc, ctx, []
        ctx.callback(self.clear)

    def clear(self):
        if self.sems:
            self.nc.clear_and_free_semaphores(self.sems)
            self.nc.all_engine_barrier()

    def sb(self, name, shape, dt):
        return self.ctx.enter_context(self.nc.sbuf_tensor(name, shape, dt))

    def ps(self, name, shape, dt=F32):
        return self.ctx.enter_context(self.nc.psum_tensor(name, shape, dt))

    def sem(self, name):
        self.sems.append(self.nc.alloc_semaphore(name=name))
        return self.sems[-1]


def make_identities(nc, kit):
    c = {}
    c["idf"] = kit.sb("idf", [P, P], F32)
    c["idh"] = kit.sb("idh", [P, P], F16)
    c["idbig"] = kit.sb("idbig", [P, P], F16)
    made = kit.sem("id_made")
    with nc.Block() as block:
        @block.gpsimd
        def _(pool):
            for t in ("idf", "idh", "idbig"):
                nc.gpsimd.memset(c[t][:], 0.0).then_inc(made, 1)
            pool.wait_ge(made, 3)
            for t, v in (("idf", 1.0), ("idh", 1.0), ("idbig", BIG)):
                nc.gpsimd.affine_select(out=c[t][:], in_=c[t][:], compare_op=ALU.not_equal, fill=v, base=0,
                                        pattern=[[-1, P]], channel_multiplier=1).then_inc(made, 1)
            pool.wait_ge(made, 6)
    return c


def token_group(x, g):
    return x[ds(g * GT, GT), :].rearrange("(t p) n -> p t n", p=P)


class Turner:

    def __init__(self, kit, name, c):
        self.bank = [kit.ps(f"{name}_t{i}", [P, GT]) for i in range(2)]
        self.turned, self.hi_done, self.lo_done = kit.sem(f"{name}_turned"), kit.sem(f"{name}_hi"), kit.sem(f"{name}_lo")
        self.c = c

    def prime(self, dve):
        dve.sem_inc(self.lo_done, 2)

    def turn(self, nc, pe, n, d, src):
        pe.wait_ge(self.lo_done, n + 1)
        for tt in range(TG):
            mm = nc.tensor.transpose(self.bank[d % 2][:, tt * P:(tt + 1) * P], src[:, tt, d * P:(d + 1) * P], self.c["idf"][:])
        mm.then_inc(self.turned, 1)

    def hi(self, nc, act, n, d, hi):
        act.wait_ge(self.turned, n + 1)
        nc.scalar.copy(hi[:, d, :], self.bank[d % 2][:]).then_inc(self.hi_done, 1)

    def lo(self, nc, dve, n, d, hi, lo):
        dve.wait_ge(self.hi_done, n + 1)
        nc.vector.tensor_tensor(lo[:, d, :], self.bank[d % 2][:], hi[:, d, :], ALU.subtract).then_inc(self.lo_done, 1)


def split_matmuls(nc, out, terms):
    for n, (a, b) in enumerate(terms):
        mm = nc.tensor.matmul(out, a, b, start=(n == 0), stop=(n == len(terms) - 1))
    return mm


WT = 9
ORDER = "o0 u0 c0 o1 c1 o2 m0 u1 c2 o3 w0 c3 o4 m1 u2 o5 w1 x0 o6 m2 u3 x1 o7 w2 x2 o8 m3 x3 o9 w3 o10 o11 w4".split()
AHEAD = {0: "m0", 1: "w0", 2: "m1", 3: "w1", 4: "m2", 5: "w2", 6: "m3", 7: "w3", 9: "w4"}


def preparation_phase(nc, c, x, Wq, bq, Wk, bk, Wv, bv, qk_dram, v_dram, context, k2_dram, v2_dram,
                      mask, mb_dram, nm_dram, mlp, w_dram):
    NB = D // 32
    NO = 12
    NW = 3
    with ExitStack() as ctx:
        kit = Kit(nc, ctx)
        sb, sem = kit.sb, kit.sem
        w32 = [sb(f"w32_{n}", [P, KT, D], F32) for n in "qkv"]
        wh = [sb(f"wh_{n}", [P, KT, D], F16) for n in "qkv"]
        wl = [sb(f"wl_{n}", [P, KT, D], F16) for n in "qkv"]
        bias = sb("qk_bias", [P, 2, KT], F32)
        bvr, bvb = sb("bv_row", [1, D], F32), sb("bv_all", [P, D], F32)
        xs = [sb(f"xs{v}", [P, TG, D], F32) for v in range(2)]
        xh = [sb(f"xh{v}", [P, KT, GT], F16) for v in range(2)]
        xl = [sb(f"xl{v}", [P, KT, GT], F16) for v in range(2)]
        y32 = sb("y32", [P, 4, GT], F32)
        qk = sb("qk_out", [P, 2, 2, KT, GT], F16)
        v65 = sb("v65", [P, H, TG, VW], F16)
        cs = [sb(f"cs{v}", [P, TG, D], F32) for v in range(2)]
        ch, cl = sb("ch", [P, KT, GT], F16), sb("cl", [P, KT, GT], F16)
        u65 = sb("u65", [P, H, TG, VW], F16)
        m32 = [sb(f"m32_{j}", [P, S], I32) for j in range(2)]
        mb = [sb(f"mb_tile{j}", [P, S], BF16) for j in range(2)]
        nq = [sb(f"nq_tile{j}", [P, S], F16) for j in range(2)]
        nk = sb("nk_tiles", [P, ST, TG, P], F16)
        w = [sb(f"g_w{j}", [P, D], F32) for j in range(NW)]
        wq = [sb(f"g_wq{j}", [P, D], F32) for j in range(NW)]
        wr = sb("g_r", [P, D], F32)
        wscale, winv = sb("g_s", [P, NB], F32), sb("g_i", [P, NB], F32)
        gh = [sb(f"g_hi{j}", [P, KT, P], F16) for j in range(NW)]
        gl = [sb(f"g_lo{j}", [P, KT, P], F16) for j in range(NW)]

        tr = Turner(kit, "prep", c)
        acc = [kit.ps(f"qkv_acc{i}", [P, GT]) for i in range(4)]
        mask_t = kit.ps("mask_t", [P, ST, P], F16)
        w_t = kit.ps("g_t", [P, KT, P])

        w_in, wsplit, x_in = [sem(f"w_in{j}") for j in range(3)], sem("w_split"), [sem(f"x_in{v}") for v in range(2)]
        b_in, b_all, one = sem("b_in"), sem("b_all"), sem("ones_set")
        summed, y_done, h_done, l_done = sem("summed"), sem("y_done"), sem("h_done"), sem("l_done")
        q_out, k_out, v_out = sem("q_out"), sem("k_out"), sem("v_out")
        c_in, uh_done, ul_done = [sem(f"c_in{v}") for v in range(2)], sem("uh_done"), sem("ul_done")
        c_out, u_out = sem("c_out"), sem("u_out")
        m_in, mb_out, nk_out = [sem(f"m_in{j}") for j in range(2)], [sem(f"mb_out{j}") for j in range(2)], sem("nk_out")
        m_made, m_turned, m_copied = sem("m_made"), sem("m_turned"), sem("m_copied")
        g_in, g_out = [sem(f"g_in{j}") for j in range(NW)], [sem(f"g_out{j}") for j in range(NW)]
        g_steps, g_quant, g_turned, g_hi, g_lo = (sem(f"g_{n}") for n in ("steps", "quant", "turned", "hi_done", "lo_done"))

        blocks = lambda t: t[:].rearrange("p (b e) -> p b e", e=32)
        spread = lambda t: t[:].unsqueeze(2).to_broadcast([P, NB, 32])
        by_head = lambda t: t.rearrange("p (h e) -> p h e", e=HD)

        def ctx_bank(g, d):
            return g * (2 * KT) + KT + d

        def x_bank(g, d):
            return g * (2 * KT) + 2 * KT + d

        def weight_tile(v, n):
            k = n + 5 * v
            return k if k < WT else None

        with nc.Block() as block:
            @block.sync
            def _(sp):
                def load_mask(t, j):
                    sp.dma_start(m32[j][:], mask[ds(t % (B * ST) * P, P), :]).then_inc(m_in[j], 16)

                def load_weight(i, k):
                    m, r = k // 3, k % 3
                    src = mlp[m][ds(i * (3 * P) + r * P, P), :] if m < 2 else mlp[m][ds(i * P, P), r * D:(r + 1) * D]
                    sp.dma_start(w[k % NW][:], src).then_inc(g_in[k % NW], 16)

                def rows(dram, i, v):
                    return dram[ds(i * H, H), :, v * TG:(v + 1) * TG, :].rearrange("h p t w -> p h (t w)")

                for k in range(KT):
                    sp.dma_start(w32[0][:, k], Wq[k * P:(k + 1) * P, :]).then_inc(w_in[0], 16)
                sp.dma_start(xs[0][:], token_group(x, 0)).then_inc(x_in[0], 16)
                for k in range(KT):
                    sp.dma_start(w32[1][:, k], Wk[k * P:(k + 1) * P, :]).then_inc(w_in[1], 16)
                sp.dma_start(xs[1][:], token_group(x, 1)).then_inc(x_in[1], 16)
                for k in range(KT):
                    sp.dma_start(w32[2][:, k], Wv[k * P:(k + 1) * P, :]).then_inc(w_in[2], 16)
                for v in range(2):
                    sp.dma_start(cs[v][:], token_group(context, v)).then_inc(c_in[v], 16)
                for j in range(2):
                    load_mask(j, j)
                for k in range(NW):
                    load_weight(0, k)
                with sp.Fori(0, NG // 2) as i:
                    for v in range(2):
                        g = i * 2 + v
                        sp.wait_ge(tr.turned, x_bank(g - 1, KT))
                        sp.dma_start(xs[v][:], token_group(x, (g + 2) % NG)).then_inc(x_in[v], 16)
                        for e in ORDER:
                            kind, n = e[0], int(e[1:])
                            if kind == "o" and n in (3, 7):
                                sp.wait_ge(l_done, g * NO + n + 1 + 4)
                                for j in range(2):
                                    sp.dma_start(qk_dram[n // 4 * 2 + j][i, :, v * GT:(v + 1) * GT].rearrange("(k p) t -> p k t", p=P),
                                                 qk[:, n // 4, j]).then_inc((q_out, k_out)[n // 4], 16)
                            if kind == "o" and n == NO - 1:
                                sp.wait_ge(l_done, g * NO + NO + 4)
                                sp.dma_start(rows(v_dram, i, v), v65[:].rearrange("p h t w -> p h (t w)")).then_inc(v_out, 16)
                            if kind == "u" and n == TG - 1:
                                sp.wait_ge(ul_done, g * TG + TG)
                                sp.dma_start(rows(v2_dram, i, v), u65[:].rearrange("p h t w -> p h (t w)")).then_inc(u_out, 16)
                                sp.dma_start(cs[v][:], token_group(context, (g + 2) % NG)).then_inc(c_in[v], 16)
                            if kind == "c" and n == KT - 1:
                                sp.wait_ge(tr.lo_done, ctx_bank(g, KT) + 2)
                                for j, src in enumerate((ch, cl)):
                                    sp.dma_start(k2_dram[j][i, :, v * GT:(v + 1) * GT].rearrange("(k p) t -> p k t", p=P),
                                                 src[:]).then_inc(c_out, 16)
                            if kind == "m":
                                t, j = g * TG + n, n % 2
                                sp.wait_ge(m_made, t * 2 + 2)
                                load_mask(t + 2, j)
                                sp.dma_start(mb_dram[ds(t * P, P), :], mb[j][:]).then_inc(mb_out[j], 16)
                                if n == TG - 1:
                                    sp.wait_ge(m_copied, t + 1)
                                    sp.dma_start(nm_dram[i, :, v * GT:(v + 1) * GT].rearrange("(k p) q -> p k q", p=P),
                                                 nk[:].rearrange("p k t q -> p k (t q)")).then_inc(nk_out, 16)
                            if kind == "w" and weight_tile(v, n) is not None:
                                k = weight_tile(v, n)
                                sp.wait_ge(g_quant, i * WT + k + 1)
                                load_weight((i + (k + NW) // WT) % (NG // 2), (k + NW) % WT)
                                sp.wait_ge(g_lo, i * WT + k + 1)
                                for j, src in enumerate((gh, gl)):
                                    sp.dma_start(w_dram[j][ds(i * 3 + (k // 3 * FT + k % 3), 1)].rearrange("o p n -> (o p) n"),
                                                 src[k % NW][:].rearrange("p k q -> p (k q)")).then_inc(g_out[k % NW], 16)
                sp.wait_ge(q_out, 32 * NG)
                sp.wait_ge(k_out, 32 * NG)
                sp.wait_ge(c_out, 32 * NG)
                for s in (v_out, u_out, nk_out):
                    sp.wait_ge(s, 16 * NG)
                for v in range(2):
                    sp.wait_ge(mb_out[v], 16 * 2 * NG)
                    sp.wait_ge(m_in[v], 16 * (2 * NG + 1))
                    sp.wait_ge(x_in[v], 16 * (NG // 2 + 1))
                    sp.wait_ge(c_in[v], 16 * (NG // 2 + 1))
                for j in range(NW):
                    sp.wait_ge(g_out[j], 32 * FT)
                    sp.wait_ge(g_in[j], 16 * (FT + 1))

            @block.tensor
            def _(pe):
                pe.wait_ge(x_in[0], 16)
                for d in range(KT):
                    tr.turn(nc, pe, d, d, xs[0])
                with pe.Fori(0, NG // 2) as i:
                    for v in range(2):
                        g = i * 2 + v
                        pe.wait_ge(tr.lo_done, x_bank(g - 1, KT) + 2)
                        for e in ORDER:
                            kind, n = e[0], int(e[1:])
                            if kind == "o":
                                if n % 4 == 0:
                                    pe.wait_ge(wsplit, n // 4 + 1)
                                pe.wait_ge(y_done, g * NO + n + 1)
                                if n < 8:
                                    m, j = slice(n % 4 * P, n % 4 * P + P), n // 4
                                    terms = [(a[:, k, m], b[:, k, :]) for k in range(KT)
                                             for a, b in ((wh[j], xh[v]), (wh[j], xl[v]), (wl[j], xh[v]))]
                                else:
                                    t = slice((n - 8) * P, (n - 8) * P + P)
                                    terms = [(a[:, k, t], b[:, k, :]) for k in range(KT)
                                             for a, b in ((xh[v], wh[2]), (xh[v], wl[2]), (xl[v], wh[2]))]
                                split_matmuls(nc, acc[n % 4][:], terms).then_inc(summed, 1)
                            if kind == "c":
                                pe.wait_ge(c_in[v], i * 16 + 16)
                                tr.turn(nc, pe, ctx_bank(g, n), n, cs[v])
                            if kind == "x":
                                pe.wait_ge(x_in[1 - v], (i + v) * 16 + 16)
                                tr.turn(nc, pe, x_bank(g, n), n, xs[1 - v])
                            if kind == "m":
                                pe.wait_ge(m_made, (g * TG + n) * 2 + 2)
                                pe.wait_ge(m_copied, g * TG + n)
                                for k in range(ST):
                                    mm = nc.tensor.transpose(mask_t[:, k, :], nq[n % 2][:, k * P:(k + 1) * P], c["idh"][:])
                                mm.then_inc(m_turned, 1)
                            if kind == "w" and weight_tile(v, n) is not None:
                                k = weight_tile(v, n)
                                pe.wait_ge(g_quant, i * WT + k + 1)
                                pe.wait_ge(g_lo, i * WT + k)
                                for d in range(KT):
                                    mm = nc.tensor.transpose(w_t[:, d, :], wq[k % NW][:, d * P:(d + 1) * P], c["idf"][:])
                                mm.then_inc(g_turned, 1)

            @block.scalar
            def _(act):
                for j, b in enumerate((bq, bk)):
                    for s in range(4):
                        act.dma_start(bias[s * HD:(s + 1) * HD, j, :],
                                      b.rearrange("(r k m e) -> r m e k", r=2, m=2, e=HD)[s % 2, s // 2],
                                      allow_slow_non_contiguous=True).then_inc(b_in, 16)
                for r in range(2):
                    act.dma_start(bvr[:].rearrange("p (n r e) -> p r n e", r=2, e=HD)[:, r],
                                 bv.rearrange("(o r n e) -> o r n e", o=1, r=2, e=HD)[:, r]).then_inc(b_in, 16)
                for d in range(KT):
                    tr.hi(nc, act, d, d, xh[0])
                act.wait_ge(b_in, 16 * 10)
                with act.Fori(0, NG // 2) as i:
                    for v in range(2):
                        g = i * 2 + v
                        for e in ORDER:
                            kind, n = e[0], int(e[1:])
                            if kind == "o" and n < 8:
                                act.wait_ge(summed, g * NO + n + 1)
                                act.wait_ge(l_done, g * NO + max(n + 1, 4))
                                nc.scalar.activation(y32[:, n % 4], acc[n % 4][:], ACT.Identity, scale=1.0 / WSCALE,
                                                     bias=bias[:, n // 4, n % 4:n % 4 + 1]).then_inc(y_done, 1)
                            if kind == "u":
                                act.wait_ge(c_in[v], i * 16 + 16)
                                if n == 0:
                                    act.wait_ge(u_out, g * 16)
                                nc.scalar.copy(u65[:, :, n, 0:HD], by_head(cs[v][:, n])).then_inc(uh_done, 1)
                            if kind == "c":
                                if n == 0:
                                    act.wait_ge(c_out, g * 32)
                                tr.hi(nc, act, ctx_bank(g, n), n, ch)
                            if kind == "x":
                                tr.hi(nc, act, x_bank(g, n), n, xh[1 - v])
                            if kind == "m":
                                act.wait_ge(m_turned, g * TG + n + 1)
                                if n == 0:
                                    act.wait_ge(nk_out, g * 16)
                                nc.scalar.copy(nk[:, :, n, :], mask_t[:]).then_inc(m_copied, 1)
                            if kind == "w" and weight_tile(v, n) is not None:
                                k = weight_tile(v, n)
                                act.wait_ge(g_turned, i * WT + k + 1)
                                act.wait_ge(g_out[k % NW], i * 96 + k // 3 * 32)
                                nc.scalar.mul(gh[k % NW][:], w_t[:], FSCALE).then_inc(g_hi, 1)

            @block.vector
            def _(dve):
                dve.sem_inc(y_done, 4)
                dve.sem_inc(l_done, 4)
                tr.prime(dve)

                def split_projection(j):
                    src = w32[j]
                    dve.wait_ge(w_in[j], 16 * KT)
                    nc.vector.tensor_scalar(src[:], src[:], WSCALE, None, ALU.mult).then_inc(one, 1)
                    dve.wait_ge(one, 2 * TG + j * 5 + 1)
                    order = lambda t, k: t[:, k, :].rearrange("p (n r e) -> p r n e", r=2, e=HD)
                    given = lambda k: src[:, k, :].rearrange("p (r n e) -> p r n e", r=2, e=HD)
                    for k in range(KT):
                        nc.vector.tensor_copy(order(wh[j], k), given(k)).then_inc(one, 1)
                    for k in range(KT):
                        dve.wait_ge(one, 2 * TG + j * 5 + 2 + k)
                        mm = nc.vector.tensor_tensor(order(wl[j], k), given(k), order(wh[j], k), ALU.subtract)
                    mm.then_inc(wsplit, 1)

                def quantise(i, k):
                    n = i * WT + k
                    dve.wait_ge(g_in[k % NW], i * 48 + (k // NW * 16 + 16))
                    dve.wait_ge(g_quant, n)
                    nc.vector.tensor_reduce(wscale[:], blocks(w[k % NW]), AX.X, ALU.max, apply_absolute_value=True).then_inc(g_steps, 1)
                    dve.wait_ge(g_steps, n * 5 + 1)
                    nc.vector.tensor_scalar(wscale[:], wscale[:], 1.0 / 7.0, 1e-12, ALU.mult, ALU.max).then_inc(g_steps, 1)
                    dve.wait_ge(g_steps, n * 5 + 2)
                    nc.vector.reciprocal(winv[:], wscale[:]).then_inc(g_steps, 1)
                    dve.wait_ge(g_steps, n * 5 + 3)
                    nc.vector.tensor_tensor(blocks(wr), blocks(w[k % NW]), spread(winv), ALU.mult).then_inc(g_steps, 1)
                    dve.wait_ge(g_steps, n * 5 + 4)
                    nc.vector.tensor_scalar(wr[:], wr[:], MAGIC, -MAGIC, ALU.add, ALU.add).then_inc(g_steps, 1)
                    dve.wait_ge(g_steps, n * 5 + 5)
                    nc.vector.tensor_tensor(blocks(wq[k % NW]), blocks(wr), spread(wscale), ALU.mult).then_inc(g_quant, 1)

                def mask_inputs(g, n):
                    j = n % 2
                    dve.wait_ge(m_in[j], g * 32 + (n // 2 * 16 + 16))
                    dve.wait_ge(mb_out[j], g * 32 + n // 2 * 16)
                    dve.wait_ge(m_turned, g * TG + max(n - 1, 0))
                    nc.vector.tensor_scalar(mb[j][:], m32[j][:], 0.0, -BIG * BIG, ALU.is_equal, ALU.mult).then_inc(m_made, 1)
                    nc.vector.tensor_scalar(nq[j][:], m32[j][:], 0.0, -BIG, ALU.is_equal, ALU.mult).then_inc(m_made, 1)

                for t in (v65, u65):
                    for tt in range(TG):
                        nc.vector.memset(t[:, :, tt, HD:HD + 1], 1.0).then_inc(one, 1)
                split_projection(0)
                for d in range(KT):
                    tr.lo(nc, dve, d, d, xh[0], xl[0])
                split_projection(1)
                split_projection(2)
                with dve.Fori(0, NG // 2) as i:
                    for v in range(2):
                        g = i * 2 + v
                        for e in ORDER:
                            kind, n = e[0], int(e[1:])
                            if kind == "o":
                                for a in AHEAD.get(n, "").split():
                                    if a[0] == "m":
                                        mask_inputs(g, int(a[1:]))
                                    elif weight_tile(v, int(a[1:])) is not None:
                                        quantise(i, weight_tile(v, int(a[1:])))
                                if n in (0, 4):
                                    dve.wait_ge((q_out, k_out)[n // 4], g * 32)
                                if n < 8:
                                    dve.wait_ge(y_done, g * NO + n + 5)
                                    nc.vector.tensor_copy(qk[:, n // 4, 0, n % 4], y32[:, n % 4]).then_inc(h_done, 1)
                                else:
                                    tt = n - 8
                                    if n == 8:
                                        dve.wait_ge(b_all, 1)
                                    dve.wait_ge(summed, g * NO + n + 1)
                                    dve.wait_ge(l_done, g * NO + n + 1)
                                    nc.vector.scalar_tensor_tensor(out=y32[:, tt], in0=acc[n % 4][:], scalar=1.0 / WSCALE, in1=bvb[:],
                                                                   op0=ALU.mult, op1=ALU.add).then_inc(y_done, 1)
                                    dve.wait_ge(y_done, g * NO + n + 5)
                                    dve.wait_ge(v_out, g * 16)
                                    nc.vector.tensor_copy(v65[:, :, tt, 0:HD], by_head(y32[:, tt])).then_inc(h_done, 1)
                            if kind == "c":
                                tr.lo(nc, dve, ctx_bank(g, n), n, ch, cl)
                            if kind == "x":
                                tr.lo(nc, dve, x_bank(g, n), n, xh[1 - v], xl[1 - v])
                            if kind == "w" and weight_tile(v, n) is not None:
                                k = weight_tile(v, n)
                                dve.wait_ge(g_hi, i * WT + k + 1)
                                nc.vector.scalar_tensor_tensor(out=gl[k % NW][:], in0=w_t[:], scalar=FSCALE, in1=gh[k % NW][:],
                                                               op0=ALU.mult, op1=ALU.subtract).then_inc(g_lo, 1)

            @block.gpsimd
            def _(pool):
                pool.wait_ge(b_in, 16 * 10)
                nc.gpsimd.partition_broadcast(bvb[:], bvr[:]).then_inc(b_all, 1)
                with pool.Fori(0, NG // 2) as i:
                    for v in range(2):
                        g = i * 2 + v
                        for e in ORDER:
                            kind, n = e[0], int(e[1:])
                            if kind == "o":
                                pool.wait_ge(h_done, g * NO + n + 1)
                                if n < 8:
                                    nc.gpsimd.tensor_tensor(qk[:, n // 4, 1, n % 4], y32[:, n % 4], qk[:, n // 4, 0, n % 4],
                                                            ALU.subtract).then_inc(l_done, 1)
                                else:
                                    tt = n - 8
                                    nc.gpsimd.tensor_tensor(v65[:, :, tt, HD + 1:VW], by_head(y32[:, tt]),
                                                            v65[:, :, tt, 0:HD], ALU.subtract).then_inc(l_done, 1)
                            if kind == "u":
                                pool.wait_ge(uh_done, g * TG + n + 1)
                                nc.gpsimd.tensor_tensor(u65[:, :, n, HD + 1:VW], by_head(cs[v][:, n]),
                                                        u65[:, :, n, 0:HD], ALU.subtract).then_inc(ul_done, 1)


SLEAD = 15
ELEAD = 3
FINISH = 3
NQK = 4
NPR = 4
UH = ST
HB = 4
NI = B * H // HB
SLOTS = B * H * (UH + 1)
PRIME = 3 * UH


def slot_of_scores(u):
    return u + max(0, (u - 2) // UH)


def slot_of_max(n):
    return min((UH + 1) * n + UH + 2, SLOTS - 1)


def attention_phase(nc, c, name, causal, q_dram, k_dram, v_dram, out_dram, mb_dram=None, nm_dram=None):
    with ExitStack() as ctx:
        kit = Kit(nc, ctx)
        sem = lambda n: kit.sem(f"{name}_{n}")
        sb = lambda n, s, d: kit.sb(f"{name}_{n}", s, d)
        qa = [sb(f"qa{j}", [P, S], F16) for j in range(NQK)]
        ka = [sb(f"ka{j}", [P, S], F16) for j in range(NQK)]
        vh = [sb(f"vh{j}", [P, ST, VW], F16) for j in range(NQK)]
        p32 = [sb(f"p32_{j}", [P, S], F32) for j in range(NPR)]
        plo = [sb(f"plo{j}", [P, S], F16) for j in range(NPR)]
        junk = [sb(f"junk{j}", [P, S], BF16) for j in range(2)]
        qmax = [sb(f"qmax{j}", [P, ST], F32) for j in range(2)]
        mneg = [sb(f"mneg{j}", [P, ST], F32) for j in range(2)]
        mrow = [sb(f"mrow{j}", [ST, P], F16) for j in range(NQK)]
        oraw = [sb(f"oraw{j}", [P, ST, VW], F32) for j in range(2)]
        osum = [sb(f"osum{j}", [P, ST, HD], F32) for j in range(2)]
        rden = [sb(f"rden{j}", [P, ST], F32) for j in range(2)]
        ost = sb("ost", [P, ST, HB * HD], F32)
        sc = [kit.ps(f"{name}_sc{j}", [P, S]) for j in range(2)]
        stp = [kit.ps(f"{name}_st{j}", [P, GT]) for j in range(2)]
        ob = [kit.ps(f"{name}_o{j}", [P, ST // 2, VW]) for j in range(2)]

        qk_in = [sem(f"qk_in{j}") for j in range(NQK)]
        mrow_in = [sem(f"mrow_in{j}") for j in range(NQK)]
        v_in = [sem(f"v_in{j}") for j in range(NQK)]
        scored, taken = sem("scored"), sem("taken")
        negated = sem("negated")
        chunked = sem("chunked")
        expd = sem("expd")
        lo_v, lo_g = sem("lo_v"), sem("lo_g")
        pv_done = sem("pv_done")
        o_read = sem("o_read")
        o_recip, o_added, o_scaled = sem("o_recip"), sem("o_added"), sem("o_scaled")
        o_out = sem("o_out")
        ready = sem("ready")
        stood = sem("stood")
        if causal:
            kc = sb("kc", [P, ST], F32)
            slopes = sb("slopes", [P, H], F32)
            tab = sb("tab", [P, H, 2 * ST + 1], F32)
            cur = [sb(f"cur{j}", [P, 2 * ST + 1], F32) for j in range(NQK)]
            ramp = [sb(f"ramp{j}", [P, S], F32) for j in range(2)]
            tri = [sb(f"tri{j}", [P, P], F16) for j in range(2)]
            strip = [sb(f"strip{j}", [P, S], F32) for j in range(2)]
            made, cur_in, strip_in = sem("made"), sem("cur_in"), sem("strip_in")
        else:
            mb = [sb(f"mb{j}", [P, S], BF16) for j in range(ST)]
            nm = [sb(f"nm{j}", [P, S], F16) for j in range(ST)]
            mb_in, nm_in = [sem(f"mb_in{j}") for j in range(ST)], [sem(f"nm_in{j}") for j in range(ST)]

        def key_range(n, qt):
            if not causal:
                return 0, S
            return (0, (qt + 1) * P) if n % 2 == 0 else (qt * P, S)

        def query_range(n, kt):
            if not causal:
                return 0, S
            return (kt * P, S) if n % 2 == 0 else (0, (kt + 1) * P)

        def chunks(n, kt):
            a, b = query_range(n, kt)
            return [(max(a, x), min(b, x + GT)) for x in range(0, S, GT) if x < b and x + GT > a]

        def chunks_before(u):
            return sum(len(chunks(m // UH, m % UH)) for m in range(u))

        CS = chunks_before(HB * UH)

        def share(n, kt):
            a, b = query_range(n, kt)
            k0, k1 = key_range(*divmod(n * UH + kt + SLEAD - ELEAD + 1, UH))
            return a + min(max(32, int((2.03 * (b - a) - 1.04 * (k1 - k0) + (100 if causal else 50)) / 3.07) // 32 * 32), b - a - 32)

        def steps(eng, prologue, step):
            prologue()
            for t in range(HB * UH):
                step(0, t, False)
            with eng.Fori(1, NI - 1) as i:
                for t in range(HB * UH):
                    step(i, t, False)
            for t in range(HB * UH):
                step(NI - 1, t, True)

        def to_finish(i, t, late):
            n, k = divmod(t, UH)
            return n - 1 if k == late - 1 and (n > 0 or not isinstance(i, int) or i > 0) else None

        def max_slot(i, n):
            return slot_of_max(n) if not isinstance(i, int) else slot_of_max(n + i * HB) - (UH + 1) * HB * i

        def within(last, u):
            return not last or u < HB * UH

        with nc.Block() as block:
            @block.sync
            def _(sp):
                def load_head(i, n):
                    j, row = n % NQK, (i * HB + n) % (B * H) * HD
                    for dst, src, part in ((qa, q_dram[0], 0), (qa, q_dram[0], 1), (qa, q_dram[1], 2),
                                           (ka, k_dram[0], 0), (ka, k_dram[1], 1), (ka, k_dram[0], 2)):
                        sp.dma_start(dst[j][part * HD:(part + 1) * HD, :],
                                     src.rearrange("b r t -> (b r) t")[ds(row, HD), :]).then_inc(qk_in[j], 16)

                def load_values(i, n):
                    sp.dma_start(vh[n % NQK][:], v_dram[ds((i * HB + n) % (B * H), 1)].rearrange("o p t w -> (o p) t w")).then_inc(v_in[n % NQK], 16)

                def load_max(i, n):
                    sp.wait_ge(taken, i * (HB * (UH + 1)) + max_slot(i, n) + 3)
                    sp.dma_start(qa[n % NQK][3 * HD:3 * HD + 1, :].rearrange("o (a c) -> o a c", a=ST),
                                 mrow[n % NQK][:]).then_inc(mrow_in[n % NQK], 16)

                def load_mb(b, qt):
                    sp.dma_start(mb[qt][:], mb_dram[ds(b * S + qt * P, P), :]).then_inc(mb_in[qt], 16)

                def load_nm(b, kt):
                    sp.dma_start(nm[kt][:], nm_dram.rearrange("b k q -> (b k) q")[ds(b * S + kt * P, P), :]).then_inc(nm_in[kt], 16)

                def step(i, t, last, next_batch=None):
                    n, k = divmod(t, UH)
                    if k == 0 and within(last, (n + 1) * UH):
                        load_max(i, n + 1)
                    if k == 1 and n > 0 or t == 1:
                        sp.wait_ge(pv_done, i * (HB * UH) + n * UH + PRIME)
                        load_values(i, n - 1 + NQK)
                    if k == UH - 3:
                        sp.wait_ge(chunked, i * CS + chunks_before((n + 1) * UH))
                        load_head(i, n + NQK)
                    if next_batch is not None:
                        q = t + SLEAD - 2 - 3 * UH
                        if 0 <= q < UH:
                            sp.wait_ge(taken, i * (HB * (UH + 1)) + slot_of_scores(3 * UH + q) + 3)
                            load_mb(next_batch, q)
                        q = t + ELEAD - 2 - 3 * UH
                        if 0 <= q < UH and t < HB * UH - 1:
                            sp.wait_ge(chunked, i * CS + chunks_before(3 * UH + q + 1))
                            load_nm(next_batch, q)
                        if t == HB * UH - 1:
                            for q in range(t + ELEAD - 2 - 3 * UH, UH):
                                sp.wait_ge(chunked, i * CS + chunks_before(3 * UH + q + 1))
                                load_nm(next_batch, q)

                sp.wait_ge(ready, NQK)
                for n in range(NQK):
                    load_head(0, n)
                    if n < NQK - 1:
                        load_values(0, n)
                    if n == 0 and not causal:
                        for q in range(UH):
                            load_mb(0, q)
                if not causal:
                    for q in range(UH):
                        load_nm(0, q)
                load_max(0, 0)
                NB = H // HB
                with sp.Fori(0, B - 1) as b:
                    with sp.Fori(0, NB - 1) as g:
                        for t in range(HB * UH):
                            step(b * NB + g, t, False)
                    for t in range(HB * UH):
                        step(b * NB + (NB - 1), t, False, None if causal else b + 1)
                with sp.Fori(NI - NB, NI - 1) as i:
                    for t in range(HB * UH):
                        step(i, t, False)
                for t in range(HB * UH):
                    step(NI - 1, t, True)
                for j in range(NQK):
                    sp.wait_ge(qk_in[j], 96 * (NI + 1))
                    sp.wait_ge(v_in[j], 16 * (NI + 1 if j < NQK - 1 else NI))

            @block.tensor
            def _(pe):
                def scores(i, u):
                    n, qt = divmod(u, UH)
                    j, slot = n % NQK, slot_of_scores(u)
                    if qt == 0:
                        pe.wait_ge(qk_in[j], (i + n // NQK + 1) * 96)
                    pe.wait_ge(taken, i * (HB * (UH + 1)) + slot + 1)
                    k0, k1 = key_range(n, qt)
                    for k in range(k0, k1, GT):
                        w = min(GT, k1 - k)
                        mm = nc.tensor.matmul(sc[slot % 2][:, k - k0:k - k0 + w], qa[j][0:3 * HD, qt * P:(qt + 1) * P],
                                              ka[j][0:3 * HD, k:k + w], start=True, stop=True)
                    mm.then_inc(scored, 1)

                def turn_max(i, n, slot):
                    pe.wait_ge(taken, i * (HB * (UH + 1)) + slot + 1)
                    pe.wait_ge(negated, i * HB + n + 1 + 2)
                    nc.tensor.transpose(sc[slot % 2][0:ST, 0:P], mneg[n % 2][:], c["idf"][:]).then_inc(scored, 1)

                def ahead(i, u, last):
                    if within(last, u):
                        scores(i, u)
                    if u >= UH + 1 and u % UH == 1:
                        n = u // UH - 1
                        if within(last, n * UH):
                            turn_max(i, n, max_slot(i, n))

                def key_scores(i, u):
                    n, kt = divmod(u, UH)
                    j = n % NQK
                    if kt == 0:
                        pe.wait_ge(mrow_in[j], (i + n // NQK + 1) * 16)
                    if not causal and n % HB == 0:
                        pe.wait_ge(nm_in[kt], (i + n // HB) // (H // HB) * 16 + 16)
                    cc = chunks_before(u)
                    for q0, q1 in chunks(n, kt):
                        pe.wait_ge(expd, i * CS + cc + 1)
                        w, out = q1 - q0, stp[cc % 2]
                        lhs = ka[j][0:3 * HD + 1, kt * P:(kt + 1) * P]
                        diag = causal and q0 <= kt * P < q1
                        mm = nc.tensor.matmul(out[:, 0:w], lhs, qa[j][0:3 * HD + 1, q0:q1], start=True, stop=causal)
                        if diag:
                            d = kt * P - q0
                            mm = nc.tensor.matmul(out[:, d:d + P], c["idbig"][:], tri[n % 2][:], start=False, stop=True, skip_group_check=True)
                        if not causal:
                            mm = nc.tensor.matmul(out[:, 0:w], c["idbig"][:], nm[kt][:, q0:q1], start=False, stop=True)
                        mm.then_inc(chunked, 1)
                        cc += 1

                def values(i, u):
                    n, kt = divmod(u, UH)
                    unit = i * (HB * UH) + u
                    if kt == 0:
                        pe.wait_ge(v_in[n % NQK], i * 16 + 16)
                        pe.wait_ge(o_read, (i * HB + n) * 2 + 2)
                    pe.wait_ge(expd, i * CS + chunks_before(u + 1) + 2)
                    pe.wait_ge(lo_v, unit + 1)
                    pe.wait_ge(lo_g, unit + 1)
                    a, z = query_range(n, kt)
                    high = p32[u % NPR][:].bitcast(BF16).rearrange("p (q h) -> p q h", h=2)[:, :, 1]
                    for qt in range(a // P, z // P):
                        q = slice(qt * P, (qt + 1) * P)
                        out = ob[qt // 4]
                        first = (kt == 0 and qt % 4 == 0) or (causal and n % 2 == 1 and kt == qt == 4)
                        last_kt = kt == (qt if causal and n % 2 == 0 else ST - 1)
                        nc.tensor.matmul(out[:, qt % 4, :], high[:, q], vh[n % NQK][:, kt, :], start=first, stop=False, skip_group_check=True)
                        mm = nc.tensor.matmul(out[:, qt % 4, 0:HD + 1], plo[u % NPR][:, q], vh[n % NQK][:, kt, 0:HD + 1],
                                              start=False, stop=last_kt, skip_group_check=True)
                    mm.then_inc(pv_done, 1)
                    return mm

                if causal:
                    pe.wait_ge(made, 9 + H)
                pe.wait_ge(ready, NQK)

                def prologue():
                    for u in range(SLEAD):
                        ahead(0, u, False)
                    for u in range(ELEAD):
                        key_scores(0, u)

                def step(i, t, last):
                    ahead(i, t + SLEAD, last)
                    if within(last, t + ELEAD):
                        key_scores(i, t + ELEAD)
                    values(i, t)

                steps(pe, prologue, step)

            @block.scalar
            def _(act):
                act.sem_inc(expd, 2)
                act.sem_inc(o_read, 2)

                def exps(i, u):
                    n, kt = divmod(u, UH)
                    act.wait_ge(pv_done, i * (HB * UH) + u - NPR + 1 + PRIME)
                    if causal and kt == 0:
                        act.wait_ge(cur_in, i * HB + n + 1)
                    cc = chunks_before(u)
                    for q0, q1 in chunks(n, kt):
                        act.wait_ge(chunked, i * CS + cc + 1)
                        bias = cur[n % NQK][:, kt:kt + 1] if causal else 0.0
                        nc.scalar.activation(p32[u % NPR][:, q0:q1], stp[cc % 2][:, 0:q1 - q0], ACT.Exp,
                                             bias=bias, scale=SM).then_inc(expd, 1)
                        cc += 1

                def prologue():
                    for u in range(ELEAD):
                        exps(0, u)

                def store(i):
                    act.wait_ge(o_scaled, i * HB + HB + 1)
                    act.dma_start(out_dram[ds(i // (H // HB) * S, S), ds(i % (H // HB) * (HB * HD), HB * HD)].rearrange("(t p) n -> p t n", p=P),
                                  ost[:]).then_inc(o_out, 16)

                def step(i, t, last):
                    if to_finish(i, t, FINISH + 2) == -1:
                        store(i - 1)
                    if within(last, t + ELEAD):
                        exps(i, t + ELEAD)
                    if t % UH == UH - 1:
                        n = t // UH
                        head = i * HB + n
                        act.wait_ge(pv_done, i * (HB * UH) + t + 1 + PRIME)
                        act.wait_ge(o_scaled, head)
                        for j in range(2):
                            nc.scalar.copy(oraw[n % 2][:, 4 * j:4 * j + 4, :], ob[j][:]).then_inc(o_read, 1)

                steps(act, prologue, step)
                store(NI - 1)
                act.wait_ge(o_out, 16 * NI)

            @block.vector
            def _(dve):
                dve.sem_inc(taken, 2)
                dve.sem_inc(pv_done, PRIME)
                dve.sem_inc(negated, 2)
                dve.sem_inc(o_scaled, 1)
                for j in range(NQK):
                    nc.vector.memset(ka[j][3 * HD:3 * HD + 1, :], BIG).then_inc(ready, 1)
                if causal:
                    dve.wait_ge(made, 9 + H)
                    for n in range(H):
                        nc.vector.tensor_scalar(tab[:, n, 0:ST], kc[:], slopes[:, n:n + 1], SM, ALU.mult, ALU.mult).then_inc(ready, 1)
                        nc.vector.tensor_scalar(tab[:, n, ST:2 * ST], kc[:], slopes[:, n:n + 1], -1.0 / BIG, ALU.mult, ALU.mult).then_inc(ready, 1)
                        nc.vector.tensor_copy(tab[:, n, 2 * ST:2 * ST + 1], slopes[:, n:n + 1]).then_inc(ready, 1)
                    dve.wait_ge(ready, NQK + 3 * H)

                def constants(i, n):
                    dve.wait_ge(pv_done, i * (HB * UH) + (n - NQK + 1) * UH + PRIME)
                    slot = (i * HB + n) % H
                    nc.vector.tensor_copy(cur[n % NQK][:], tab[:].rearrange("p n w -> p (n w)")[:, ds(slot * (2 * ST + 1), 2 * ST + 1)]).then_inc(cur_in, 1)

                def maxima(i, u):
                    n, qt = divmod(u, UH)
                    slot = slot_of_scores(u)
                    k0, k1 = key_range(n, qt)
                    w = k1 - k0
                    done = i * (HB * (UH + 1)) + slot
                    dve.wait_ge(scored, done + 1)
                    dve.wait_ge(taken, done + 1)
                    if qt == 0:
                        dve.wait_ge(negated, i * HB + n + 1)
                    if causal:
                        if qt == 0:
                            dve.wait_ge(strip_in, i * HB + n + 1)
                        bias = strip[n % 2][:, S - w:S] if n % 2 == 0 else strip[n % 2][:, 0:w]
                    else:
                        if n % HB == 0:
                            dve.wait_ge(mb_in[qt], (i + n // HB) // (H // HB) * 16 + 16)
                        bias = mb[qt][:]
                    dve.sem_inc(stood, 1)
                    nc.vector.tensor_tensor_reduce(junk[slot % 2][:, 0:w], sc[slot % 2][:, 0:w], bias, 1.0, -3e38,
                                                   ALU.add, ALU.max, qmax[n % 2][:, qt:qt + 1]).then_inc(taken, 1)
                    if qt == UH - 1:
                        dve.wait_ge(taken, done + 3)
                        if causal:
                            nc.vector.scalar_tensor_tensor(out=mneg[n % 2][:], in0=qmax[n % 2][:], scalar=-1.0 / BIG,
                                                           in1=cur[n % NQK][:, ST:2 * ST], op0=ALU.mult, op1=ALU.add).then_inc(negated, 1)
                        else:
                            nc.vector.tensor_scalar(mneg[n % 2][:], qmax[n % 2][:], -1.0 / BIG, None, ALU.mult).then_inc(negated, 1)

                def max_row(i, n, slot):
                    dve.wait_ge(scored, i * (HB * (UH + 1)) + slot + 1)
                    dve.wait_ge(mrow_in[n % NQK], (i + n // NQK) * 16)
                    nc.vector.tensor_copy(mrow[n % NQK][:], sc[slot % 2][0:ST, 0:P]).then_inc(taken, 1)

                def ahead(i, u, last):
                    if causal and u % UH == 2 and within(last, u - 2 + UH):
                        constants(i, u // UH + 1)
                    if within(last, u):
                        maxima(i, u)
                    if u >= UH + 1 and u % UH == 1:
                        n = u // UH - 1
                        if within(last, n * UH):
                            max_row(i, n, max_slot(i, n))

                def low(i, u):
                    n, kt = divmod(u, UH)
                    dve.wait_ge(expd, i * CS + chunks_before(u + 1) + 2)
                    q = slice(query_range(n, kt)[0], share(n, kt))
                    high = p32[u % NPR][:].bitcast(BF16).rearrange("p (q h) -> p q h", h=2)[:, :, 1]
                    nc.vector.tensor_tensor(plo[u % NPR][:, q], p32[u % NPR][:, q], high[:, q], ALU.subtract).then_inc(lo_v, 1)

                def finish(i, n):
                    head, m = i * HB + n, n % HB
                    dve.wait_ge(o_read, head * 2 + 4)
                    nc.vector.reciprocal(rden[n % 2][:], oraw[n % 2][:, :, HD]).then_inc(o_recip, 1)
                    dve.wait_ge(o_recip, head + 1)
                    dve.wait_ge(o_added, head + 1)
                    if m == 0:
                        dve.wait_ge(o_out, i * 16)
                    nc.vector.tensor_tensor(ost[:, :, m * HD:(m + 1) * HD], osum[n % 2][:],
                                            rden[n % 2][:].unsqueeze(2).to_broadcast([P, ST, HD]), ALU.mult).then_inc(o_scaled, 1)

                def prologue():
                    if causal:
                        constants(0, 0)
                    for u in range(SLEAD):
                        ahead(0, u, False)
                    for u in range(ELEAD - 1):
                        low(0, u)

                def step(i, t, last):
                    ahead(i, t + SLEAD, last)
                    if within(last, t + ELEAD - 1):
                        low(i, t + ELEAD - 1)
                    n = to_finish(i, t, FINISH + 1)
                    if n is not None:
                        finish(i, n)

                steps(dve, prologue, step)
                finish(NI - 1, HB - 1)

            @block.gpsimd
            def _(pool):
                if causal:
                    nc.gpsimd.iota(kc[:], pattern=[[P, ST]], base=-S // 2, channel_multiplier=1, allow_small_or_imprecise_dtypes=True).then_inc(made, 1)
                    for n in range(H):
                        s = 24.0 ** (-(n // 2 + 1) / (H // 2)) / SM
                        nc.gpsimd.memset(slopes[:, n:n + 1], s if n % 2 == 0 else -s).then_inc(made, 1)
                    for j in range(2):
                        nc.gpsimd.memset(tri[j][:], 0.0).then_inc(made, 1)
                        nc.gpsimd.iota(ramp[j][:], pattern=[[1, S]], base=(P - S, 0)[j], channel_multiplier=-1,
                                       allow_small_or_imprecise_dtypes=True).then_inc(made, 1)
                    pool.wait_ge(made, 5 + H)
                    for j, sign in enumerate((-1, 1)):
                        nc.gpsimd.affine_select(out=ramp[j][:], in_=ramp[j][:], compare_op=ALU.is_ge, fill=sign * 4.5e9,
                                                base=sign * (P - S, 0)[j], pattern=[[sign, S]], channel_multiplier=-sign).then_inc(made, 1)
                        nc.gpsimd.affine_select(out=tri[j][:], in_=tri[j][:], compare_op=ALU.is_ge, fill=-BIG,
                                                base=0, pattern=[[-sign, P]], channel_multiplier=sign).then_inc(made, 1)
                    pool.wait_ge(made, 9 + H)

                def strips(i, n):
                    pool.wait_ge(cur_in, i * HB + n + 1)
                    pool.wait_ge(negated, i * HB + n + 1)
                    pool.sem_inc(stood, 1)
                    nc.gpsimd.tensor_scalar(strip[n % 2][:], ramp[n % 2][:], cur[n % NQK][:, 2 * ST:2 * ST + 1], 1.0, ALU.mult, ALU.mult).then_inc(strip_in, 1)

                def low(i, u):
                    n, kt = divmod(u, UH)
                    pool.wait_ge(expd, i * CS + chunks_before(u + 1) + 2)
                    q = slice(share(n, kt), query_range(n, kt)[1])
                    high = p32[u % NPR][:].bitcast(BF16).rearrange("p (q h) -> p q h", h=2)[:, :, 1]
                    nc.gpsimd.tensor_tensor(plo[u % NPR][:, q], p32[u % NPR][:, q], high[:, q], ALU.subtract).then_inc(lo_g, 1)

                def ahead(i, u, last):
                    if causal and u % UH == 2 and within(last, u - 2 + UH):
                        strips(i, u // UH + 1)

                def finish(i, n):
                    head = i * HB + n
                    pool.wait_ge(o_read, head * 2 + 4)
                    pool.wait_ge(o_scaled, head)
                    nc.gpsimd.tensor_tensor(osum[n % 2][:], oraw[n % 2][:, :, 0:HD], oraw[n % 2][:, :, HD + 1:VW],
                                            ALU.add).then_inc(o_added, 1)

                def prologue():
                    if causal:
                        strips(0, 0)
                    for u in range(SLEAD):
                        ahead(0, u, False)
                    for u in range(ELEAD - 1):
                        low(0, u)

                def step(i, t, last):
                    ahead(i, t + SLEAD, last)
                    if within(last, t + ELEAD - 1):
                        low(i, t + ELEAD - 1)
                    n = to_finish(i, t, FINISH)
                    if n is not None:
                        finish(i, n)

                steps(pool, prologue, step)
                finish(NI - 1, HB - 1)


class Norm:

    def __init__(self, kit, name):
        self.st = [kit.sb(f"{name}_bn{j}", [P, 6], F32) for j in range(2)]
        self.mv = [kit.sb(f"{name}_mv{j}", [P, 2], F32) for j in range(2)]
        self.sd = [kit.sb(f"{name}_sd{j}", [P, 1], F32) for j in range(2)]
        self.rs = [kit.sb(f"{name}_rs{j}", [P, 1], F32) for j in range(2)]
        self.steps = kit.sem(f"{name}_steps")
        self.root = kit.sem(f"{name}_root")
        self.recip = kit.sem(f"{name}_recip")
        self.stood = kit.sem(f"{name}_stood")

    def statistics(self, nc, dve, n, j, r):
        nc.vector.bn_stats(self.st[j][:], r).then_inc(self.steps, 1)
        dve.wait_ge(self.steps, n * 3 + 1)
        dve.sem_inc(self.stood, 1)
        nc.vector.bn_aggr(self.mv[j][:], self.st[j][:]).then_inc(self.steps, 1)
        dve.wait_ge(self.steps, n * 3 + 2)
        nc.vector.tensor_scalar(self.mv[j][:, 1:2], self.mv[j][:, 1:2], EPS, None, ALU.add).then_inc(self.steps, 1)

    def square_root(self, nc, act, n, j):
        act.wait_ge(self.steps, n * 3 + 3)
        nc.scalar.activation(self.sd[j][:], self.mv[j][:, 1:2], ACT.Sqrt).then_inc(self.root, 1)

    def scale(self, nc, dve, n, j, out, r):
        dve.wait_ge(self.root, n + 1)
        nc.vector.reciprocal(self.rs[j][:], self.sd[j][:]).then_inc(self.recip, 1)
        dve.wait_ge(self.recip, n + 1)
        return nc.vector.tensor_scalar(out, r, self.mv[j][:, 0:1], self.rs[j][:, 0:1], ALU.subtract, ALU.mult)


def projection_phase(nc, c, attn, x, Wf, bf, x1_dram, q_dram):
    with ExitStack() as ctx:
        kit = Kit(nc, ctx)
        w32 = kit.sb("wf32", [P, KT, D], F32)
        wh, wl = kit.sb("wfh", [P, KT, D], F16), kit.sb("wfl", [P, KT, D], F16)
        bfr, bfb = kit.sb("bf_row", [1, D], F32), kit.sb("bf_all", [P, D], F32)
        at = [kit.sb(f"at{v}", [P, TG, D], F32) for v in range(2)]
        xs = [kit.sb(f"px{v}", [P, TG, D], F32) for v in range(2)]
        x1 = [kit.sb(f"px1_{v}", [P, TG, D], F32) for v in range(2)]
        ah, al = [kit.sb(f"ah{v}", [P, KT, GT], F16) for v in range(2)], [kit.sb(f"al{v}", [P, KT, GT], F16) for v in range(2)]
        qh, ql = kit.sb("pqh", [P, KT, GT], F16), kit.sb("pql", [P, KT, GT], F16)
        res = [kit.sb(f"pres{j}", [P, D], F32) for j in range(2)]
        norm = Norm(kit, "n1")
        tr = Turner(kit, "proj", c)
        acc = [kit.ps(f"proj_acc{j}", [P, D]) for j in range(2)]
        w_in, wsplit, b_in, b_all = kit.sem("pw_in"), kit.sem("pw_split"), kit.sem("pb_in"), kit.sem("pb_all")
        a_in, x_in = [kit.sem(f"pa_in{v}") for v in range(2)], [kit.sem(f"px_in{v}") for v in range(2)]
        biased, summed, added, normed = kit.sem("p_biased"), kit.sem("p_summed"), kit.sem("p_added"), kit.sem("p_normed")
        x1_out, q_out = [kit.sem(f"px1_out{v}") for v in range(2)], kit.sem("pq_out")

        xt = kit.ps("x1_t", [P, KT, P])
        x_turned, xh_done, xl_done = kit.sem("x1_turned"), kit.sem("x1_hi"), kit.sem("x1_lo")

        with nc.Block() as block:
            @block.sync
            def _(sp):
                sp.dma_start(at[0][:], token_group(attn, 0)).then_inc(a_in[0], 16)
                for s in range(4):
                    sp.dma_start(w32[s * HD:(s + 1) * HD, :, :],
                                 Wf.rearrange("(r k m e) n -> r m e k n", r=2, m=2, e=HD)[s % 2, s // 2]).then_inc(w_in, 16)
                sp.dma_start(bfr[:], bf.rearrange("(o n) -> o n", o=1)).then_inc(b_in, 16)
                sp.dma_start(xs[0][:], token_group(x, 0)).then_inc(x_in[0], 16)
                sp.dma_start(at[1][:], token_group(attn, 1)).then_inc(a_in[1], 16)
                sp.dma_start(xs[1][:], token_group(x, 1)).then_inc(x_in[1], 16)
                def step(i, last):
                    for v in range(2):
                        g = i * 2 + v
                        sp.wait_ge(tr.turned, g * KT + KT)
                        if not last or v == 0:
                            sp.dma_start(at[v][:], token_group(attn, (g + 2) % NG)).then_inc(a_in[v], 16)
                        sp.wait_ge(normed, g * TG + TG)
                        if not last:
                            sp.dma_start(xs[v][:], token_group(x, g + 2)).then_inc(x_in[v], 16)
                        sp.dma_start(token_group(x1_dram, g), x1[v][:]).then_inc(x1_out[v], 16)
                        sp.wait_ge(xl_done, g * TG + TG)
                        for j, src in enumerate((qh, ql)):
                            sp.dma_start(q_dram[j][i, :, v * GT:(v + 1) * GT].rearrange("(k p) t -> p k t", p=P),
                                         src[:]).then_inc(q_out, 16)

                with sp.Fori(0, NG // 2 - 1) as i:
                    step(i, False)
                step(NG // 2 - 1, True)
                sp.wait_ge(q_out, 32 * NG)
                for v in range(2):
                    sp.wait_ge(x1_out[v], 16 * (NG // 2))

            @block.gpsimd
            def _(pool):
                pool.wait_ge(b_in, 16)
                nc.gpsimd.partition_broadcast(bfb[:], bfr[:]).then_inc(b_all, 1)
                pool.wait_ge(b_all, 1)
                with pool.Fori(0, NG // 2) as i:
                    for v in range(2):
                        pool.wait_ge(x_in[v], i * 16 + 16)
                        for tt in range(TG):
                            nc.gpsimd.tensor_tensor(xs[v][:, tt, :], xs[v][:, tt, :], bfb[:], ALU.add).then_inc(biased, 1)

            @block.tensor
            def _(pe):
                pe.wait_ge(a_in[0], 16)
                for d in range(KT):
                    tr.turn(nc, pe, d, d, at[0])
                pe.wait_ge(wsplit, 2)

                def turn_x1(g, v, tt):
                    n = g * TG + tt
                    pe.wait_ge(normed, n + 1)
                    pe.wait_ge(xl_done, n)
                    for d in range(KT):
                        mm = nc.tensor.transpose(xt[:, d, :], x1[v][:, tt, d * P:(d + 1) * P], c["idf"][:])
                    mm.then_inc(x_turned, 1)

                with pe.Fori(0, NG // 2) as i:
                    for v in range(2):
                        g = i * 2 + v
                        pe.wait_ge(tr.lo_done, g * KT + KT + 2)
                        pe.wait_ge(a_in[1 - v], (i + v) * 16 + 16)
                        for tt in range(TG):
                            pe.wait_ge(added, g * TG + tt + 1)
                            t = slice(tt * P, (tt + 1) * P)
                            split_matmuls(nc, acc[tt % 2][:], [(a[:, k, t], b[:, k, :]) for k in range(KT)
                                                               for a, b in ((ah[v], wh), (ah[v], wl), (al[v], wh))]).then_inc(summed, 1)
                            tr.turn(nc, pe, g * KT + KT + tt, tt, at[1 - v])
                            if tt >= 2:
                                turn_x1(g, v, tt - 2)
                        turn_x1(g, v, TG - 2)
                        turn_x1(g, v, TG - 1)

            @block.scalar
            def _(act):
                for d in range(KT):
                    tr.hi(nc, act, d, d, ah[0])
                with act.Fori(0, NG // 2) as i:
                    for v in range(2):
                        g = i * 2 + v
                        def x1_hi(tt):
                            act.wait_ge(x_turned, g * TG + tt + 1)
                            nc.scalar.copy(qh[:, :, tt * P:(tt + 1) * P], xt[:]).then_inc(xh_done, 1)

                        for tt in range(TG):
                            tr.hi(nc, act, g * KT + KT + tt, tt, ah[1 - v])
                            norm.square_root(nc, act, g * TG + tt, tt % 2)
                            if tt == 2:
                                act.wait_ge(q_out, g * 32)
                            if tt >= 2:
                                x1_hi(tt - 2)
                        x1_hi(TG - 2)
                        x1_hi(TG - 1)

            @block.vector
            def _(dve):
                tr.prime(dve)
                dve.sem_inc(added, 2)
                for d in range(KT):
                    tr.lo(nc, dve, d, d, ah[0], al[0])
                dve.wait_ge(w_in, 16 * 4)
                nc.vector.tensor_scalar(wh[:], w32[:], WSCALE, None, ALU.mult).then_inc(wsplit, 1)
                dve.wait_ge(wsplit, 1)
                nc.vector.scalar_tensor_tensor(out=wl[:].rearrange("p k n -> p (k n)"), in0=w32[:].rearrange("p k n -> p (k n)"), scalar=WSCALE,
                                               in1=wh[:].rearrange("p k n -> p (k n)"), op0=ALU.mult, op1=ALU.subtract).then_inc(wsplit, 1)
                with dve.Fori(0, NG // 2) as i:
                    for v in range(2):
                        g = i * 2 + v

                        def scale(tt):
                            norm.scale(nc, dve, g * TG + tt, tt % 2, x1[v][:, tt, :], res[tt % 2][:]).then_inc(normed, 1)

                        def x1_lo(tt):
                            dve.wait_ge(xh_done, g * TG + tt + 1)
                            nc.vector.tensor_tensor(ql[:, :, tt * P:(tt + 1) * P], xt[:], qh[:, :, tt * P:(tt + 1) * P],
                                                    ALU.subtract).then_inc(xl_done, 1)

                        dve.wait_ge(x1_out[v], i * 16)
                        for tt in range(TG):
                            n, j = g * TG + tt, tt % 2
                            dve.wait_ge(summed, n + 1)
                            dve.wait_ge(biased, n + 1)
                            dve.wait_ge(normed, g * TG + max(tt - 1, 0))
                            nc.vector.scalar_tensor_tensor(out=res[j][:], in0=acc[j][:], scalar=1.0 / WSCALE, in1=xs[v][:, tt, :],
                                                           op0=ALU.mult, op1=ALU.add).then_inc(added, 1)
                            dve.wait_ge(added, n + 3)
                            norm.statistics(nc, dve, n, j, res[j][:])
                            tr.lo(nc, dve, g * KT + KT + tt, tt, ah[1 - v], al[1 - v])
                            scale(tt)
                            if tt >= 2:
                                x1_lo(tt - 2)
                        x1_lo(TG - 2)
                        x1_lo(TG - 1)


def second_norm_phase(nc, attn, x1_dram, x2, x2_dram, xmax, loads):
    TQ, NR = 2, 4
    NQ = T // (TQ * P)

    def tokens(x, g):
        return x[ds(g * (TQ * P), TQ * P), :].rearrange("(t p) n -> p t n", p=P)

    with ExitStack() as ctx:
        kit = Kit(nc, ctx)
        a = [kit.sb(f"sa{v}", [P, TQ, D], F32) for v in range(NR)]
        b = [kit.sb(f"sb{v}", [P, TQ, D], F32) for v in range(NR)]
        st = [kit.sb(f"s_st{v}", [P, TQ, 6], F32) for v in range(NR)]
        mv = [kit.sb(f"s_mv{v}", [P, TQ, 2], F32) for v in range(NR)]
        sd, rs = ([kit.sb(f"s_{n}{v}", [P, TQ], F32) for v in range(NR)] for n in ("sd", "rs"))
        tmax = kit.sb("s_tmax", [P, NQ], F32)
        t_in = [kit.sem(f"s_in{v}") for v in range(NR)]
        added, stats, aggregated, root, recip, scaled, maxed, done, stood = (kit.sem(f"s_{n}") for n in (
            "added", "stats", "aggregated", "root", "recip", "scaled", "maxed", "done", "stood"))
        x2_out, weights_in = kit.sem("s_x2_out"), kit.sem("s_weights")
        with nc.Block() as block:
            @block.sync
            def _(sp):
                def load(g, v):
                    for t, src in ((a, attn), (b, x1_dram)):
                        sp.dma_start(t[v][:], tokens(src, g)).then_inc(t_in[v], 16)

                for v in range(NR):
                    load(v, v)
                with sp.Fori(0, NQ // NR - 1) as i:
                    for v in range(NR):
                        sp.wait_ge(scaled, i * (NR * TQ) + (v + 1) * TQ)
                        load(i * NR + v + NR, v)

            @block.gpsimd
            def _(pool):
                for dst, src in loads:
                    pool.dma_start(dst, src).then_inc(weights_in, 16)
                with pool.Fori(0, NQ // NR) as i:
                    for v in range(NR):
                        pool.wait_ge(t_in[v], i * 32 + 32)
                        for tt in range(TQ):
                            nc.gpsimd.tensor_tensor(a[v][:, tt], a[v][:, tt], b[v][:, tt], ALU.add).then_inc(added, 1)
                pool.wait_ge(weights_in, 16 * len(loads))

            @block.scalar
            def _(act):
                def store(g):
                    act.wait_ge(scaled, g * TQ + TQ)
                    act.dma_start(tokens(x2_dram, g), x2[:, ds(g * (TQ * D), TQ * D)].rearrange("p (t n) -> p t n", n=D)).then_inc(x2_out, 16)

                with act.Fori(0, NQ // NR) as i:
                    for v in range(NR):
                        g = i * NR + v
                        act.wait_ge(aggregated, g * (TQ + 1) + TQ + 1)
                        nc.scalar.activation(sd[v][:], mv[v][:, :, 1], ACT.Sqrt).then_inc(root, 1)
                        if v:
                            store(g - 1)
                    store(i * NR + (NR - 1))
                act.wait_ge(x2_out, 16 * NQ)

            @block.vector
            def _(dve):
                def statistics(g, v):
                    for tt in range(TQ):
                        dve.wait_ge(added, g * TQ + tt + 1)
                        nc.vector.bn_stats(st[v][:, tt], a[v][:, tt]).then_inc(stats, 1)
                    for tt in range(TQ):
                        dve.wait_ge(stats, g * TQ + tt + 1)
                        dve.sem_inc(stood, 1)
                        nc.vector.bn_aggr(mv[v][:, tt], st[v][:, tt]).then_inc(aggregated, 1)
                    dve.wait_ge(aggregated, g * (TQ + 1) + TQ)
                    nc.vector.tensor_scalar(mv[v][:, :, 1], mv[v][:, :, 1], EPS, None, ALU.add).then_inc(aggregated, 1)

                def scale(g, v):
                    dve.wait_ge(root, g + 1)
                    nc.vector.reciprocal(rs[v][:], sd[v][:]).then_inc(recip, 1)
                    dve.wait_ge(recip, g + 1)
                    for tt in range(TQ):
                        nc.vector.tensor_scalar(x2[:, ds(g * (TQ * D) + tt * D, D)], a[v][:, tt], mv[v][:, tt, 0:1], rs[v][:, tt:tt + 1],
                                                ALU.subtract, ALU.mult).then_inc(scaled, 1)
                    dve.wait_ge(scaled, g * TQ + TQ)
                    nc.vector.tensor_reduce(tmax[:, ds(g, 1)], x2[:, ds(g * (TQ * D), TQ * D)], AX.X, ALU.max,
                                            apply_absolute_value=True).then_inc(maxed, 1)

                with dve.Fori(0, NQ // NR) as i:
                    statistics(i * NR, 0)
                    for v in range(NR):
                        if v < NR - 1:
                            statistics(i * NR + v + 1, v + 1)
                        scale(i * NR + v, v)
                dve.wait_ge(maxed, NQ)
                nc.vector.tensor_reduce(xmax[:], tmax[:], AX.X, ALU.max).then_inc(done, 1)
                dve.wait_ge(done, 1)


def quantisers(nc, name, of):
    with ExitStack() as ctx:
        kit = Kit(nc, ctx)
        amax = [kit.sb(f"{name}_amax{j}", [P, 1], F32) for j in range(len(of))]
        reduced, steps = kit.sem(f"{name}_reduced"), kit.sem(f"{name}_steps")
        with nc.Block() as block:
            @block.gpsimd
            def _(pool):
                for j, (pmax, scale, inverse) in enumerate(of):
                    nc.gpsimd.partition_all_reduce(amax[j][:], pmax[:], P, RMAX).then_inc(reduced, 1)

            @block.vector
            def _(dve):
                for j, (pmax, scale, inverse) in enumerate(of):
                    dve.wait_ge(reduced, j + 1)
                    nc.vector.tensor_scalar(scale[:], amax[j][:], 1.0 / QMAX, 1e-12, ALU.mult, ALU.max).then_inc(steps, 1)
                    dve.wait_ge(steps, 2 * j + 1)
                    nc.vector.reciprocal(inverse[:], scale[:]).then_inc(steps, 1)
                    dve.wait_ge(steps, 2 * j + 2)


def gate_phase(nc, c, x2, scale, inverse, wts, y_dram, x_dram, gmax, loads):
    NY = 3
    with ExitStack() as ctx:
        kit = Kit(nc, ctx)
        xq = kit.sb("gt_xq", [P, TG, D], F32)
        xh = [kit.sb(f"gt_xh{v}", [P, KT, GT], F16) for v in range(2)]
        xl = [kit.sb(f"gt_xl{v}", [P, KT, GT], F16) for v in range(2)]
        y = [kit.sb(f"gt_y{j}", [P, GT], F32) for j in range(NY)]
        tmax = kit.sb("gt_tmax", [P, NG * FT], F32)
        yscale = kit.sb("gt_ysc", [P, 1], F32)
        tr = Turner(kit, "gate", c)
        acc = [kit.ps(f"gt_acc{j}", [P, GT]) for j in range(4)]
        weights_in = kit.sem("gt_weights")
        scaled, added, rounded = kit.sem("gt_scaled"), kit.sem("gt_added"), kit.sem("gt_rounded")
        summed, out_done, maxed = kit.sem("gt_summed"), kit.sem("gt_out"), kit.sem("gt_maxed")
        stored = [kit.sem(f"gt_stored{j}") for j in range(NY)]
        x_out = [kit.sem(f"gt_x_out{v}") for v in range(2)]
        EARLY = {4: 0, 5: 1, 6: 2, 7: 3}
        hi, lo = wts
        with nc.Block() as block:
            @block.sync
            def _(sp):
                with sp.Fori(0, NG // 2) as i:
                    for v in range(2):
                        g = i * 2 + v
                        sp.wait_ge(tr.lo_done, g * KT + KT + 2)
                        for j, src in enumerate((xh, xl)):
                            sp.dma_start(x_dram[j][ds(g, 1)].rearrange("o p n -> (o p) n"), src[v][:].rearrange("p k t -> p (k t)")).then_inc(x_out[v], 16)
                        for o in range(FT):
                            sp.wait_ge(out_done, g * FT + o + 1)
                            sp.dma_start(y_dram[o, :, ds(g * GT, GT)], y[o % NY][:]).then_inc(stored[o % NY], 16)
                for j in range(NY):
                    sp.wait_ge(stored[j], 16 * NG * FT // NY)
                for v in range(2):
                    sp.wait_ge(x_out[v], 32 * NG // 2)

            @block.tensor
            def _(pe):
                pe.wait_ge(rounded, 1)
                for d in range(KT):
                    tr.turn(nc, pe, d, d, xq)
                with pe.Fori(0, NG // 2) as i:
                    for v in range(2):
                        g = i * 2 + v
                        pe.wait_ge(tr.lo_done, g * KT + KT + 2)
                        for o in range(FT):
                            pe.wait_ge(maxed, g * FT + o + 1)
                            split_matmuls(nc, acc[o % 4][:], [(a[:, o, k, :], b[:, k, :]) for k in range(KT)
                                                              for a, b in ((hi, xh[v]), (hi, xl[v]), (lo, xh[v]))]).then_inc(summed, 1)
                            if o in EARLY:
                                pe.wait_ge(rounded, g + 2)
                                tr.turn(nc, pe, g * KT + KT + EARLY[o], EARLY[o], xq)

            @block.scalar
            def _(act):
                for d in range(KT):
                    tr.hi(nc, act, d, d, xh[0])
                act.wait_ge(scaled, 1)
                with act.Fori(0, NG // 2) as i:
                    for v in range(2):
                        g = i * 2 + v
                        for o in range(FT):
                            act.wait_ge(summed, g * FT + o + 1)
                            act.wait_ge(maxed, g * FT + o + 1)
                            act.wait_ge(stored[o % NY], g * (16 * FT // NY) + o // NY * 16)
                            nc.scalar.activation(y[o % NY][:], acc[o % 4][:], ACT.Copy, scale=yscale[:, 0:1]).then_inc(out_done, 1)
                            if o in EARLY:
                                if EARLY[o] == 0:
                                    act.wait_ge(x_out[1 - v], (i + v) * 32)
                                tr.hi(nc, act, g * KT + KT + EARLY[o], EARLY[o], xh[1 - v])

            @block.gpsimd
            def _(pool):
                for dst, src in loads:
                    pool.dma_start(dst, src).then_inc(weights_in, 16)
                pool.wait_ge(weights_in, 16 * len(loads))

            @block.vector
            def _(dve):
                tr.prime(dve)
                dve.sem_inc(maxed, NY)
                nc.vector.tensor_scalar(yscale[:], scale[:], 1.0 / FSCALE, None, ALU.mult).then_inc(scaled, 1)

                def quantise(g):
                    nc.vector.tensor_scalar(xq[:].rearrange("p t n -> p (t n)"), x2[:, ds(g % NG * (TG * D), TG * D)], inverse[:, 0:1], MAGIC,
                                            ALU.mult, ALU.add).then_inc(added, 1)
                    dve.wait_ge(added, g + 1)
                    nc.vector.tensor_scalar(xq[:], xq[:], -MAGIC, None, ALU.add).then_inc(rounded, 1)

                quantise(0)
                for d in range(KT):
                    tr.lo(nc, dve, d, d, xh[0], xl[0])
                with dve.Fori(0, NG // 2) as i:
                    for v in range(2):
                        g = i * 2 + v
                        for o in range(FT):
                            if o == 1:
                                quantise(g + 1)
                            dve.wait_ge(out_done, g * FT + o + 1)
                            nc.vector.tensor_reduce(tmax[:, ds(g * FT + o, 1)], y[o % NY][:], AX.X, ALU.max,
                                                    apply_absolute_value=True).then_inc(maxed, 1)
                            if o in EARLY:
                                tr.lo(nc, dve, g * KT + KT + EARLY[o], EARLY[o], xh[1 - v], xl[1 - v])
                dve.wait_ge(maxed, FT * NG + NY)
                nc.vector.tensor_reduce(gmax[:], tmax[:], AX.X, ALU.max).then_inc(scaled, 1)
                dve.wait_ge(scaled, 2)


def up_phase(nc, x_dram, scale, wts, gate_dram, sg, isg, y_dram, res, h_dram, ymax, hmax):
    NR = 4
    with ExitStack() as ctx:
        kit = Kit(nc, ctx)
        xh = [kit.sb(f"v_xh{v}", [P, KT * GT], F16) for v in range(2)]
        xl = [kit.sb(f"v_xl{v}", [P, KT * GT], F16) for v in range(2)]
        y = [kit.sb(f"v_y{j}", [P, GT], F32) for j in range(NR)]
        ga = [kit.sb(f"v_g{j}", [P, GT], F32) for j in range(NR)]
        ra = [kit.sb(f"v_r{j}", [P, GT], F32) for j in range(2)]
        qa = [kit.sb(f"v_q{j}", [P, GT], F32) for j in range(NR)]
        sa = [kit.sb(f"v_s{j}", [P, GT], F32) for j in range(2)]
        sq = [kit.sb(f"v_t{j}", [P, GT], F32) for j in range(2)]
        h = [kit.sb(f"v_h{j}", [P, GT], F32) for j in range(NR)]
        magic, yscale, gscale = kit.sb("v_magic", [P, 1], F32), kit.sb("v_ysc", [P, 1], F32), kit.sb("v_gsc", [P, 1], F32)
        ytmax, htmax = kit.sb("v_ytmax", [P, NG * FT], F32), kit.sb("v_htmax", [P, NG * FT], F32)
        acc = [kit.ps(f"v_acc{j}", [P, GT]) for j in range(4)]
        x_in = [kit.sem(f"v_x_in{v}") for v in range(2)]
        g_in = [kit.sem(f"v_g_in{j}") for j in range(NR)]
        y_out, h_out = [kit.sem(f"v_y_out{j}") for j in range(NR)], [kit.sem(f"v_h_out{j}") for j in range(NR)]
        ready, summed, evicted, ymaxed = (kit.sem(f"v_{n}") for n in ("ready", "summed", "evicted", "ymaxed"))
        added, deq, sig, inc, clipped, prod, hmaxed, done, stood = (kit.sem(f"v_{n}") for n in (
            "added", "deq", "sig", "in_units", "clipped", "prod", "hmaxed", "done", "stood"))
        hi, lo = wts

        def y_stores(o):
            return sum(1 for p in range(o) if p % NR == o % NR and p >= RES)

        with nc.Block() as block:
            @block.sync
            def _(sp):
                def load_x(g, v):
                    for j, dst in enumerate((xh, xl)):
                        sp.dma_start(dst[v][:], x_dram[j][ds(g % NG, 1)].rearrange("o p n -> (o p) n")).then_inc(x_in[v], 16)

                for v in range(2):
                    load_x(v, v)
                for o in range(NR):
                    sp.dma_start(ga[o][:], gate_dram[o, :, 0:GT]).then_inc(g_in[o], 16)
                def step(i, last):
                    for v in range(2):
                        g = i * 2 + v
                        for o in range(FT):
                            n = g * FT + o
                            sp.wait_ge(added, n + 1)
                            if not last or v == 0 or o <= FT - NR:
                                sp.dma_start(ga[o % NR][:], gate_dram[(o + NR) % FT, :, ds((g + (o + NR) // FT) % NG * GT, GT)]).then_inc(g_in[o % NR], 16)
                            if o >= RES:
                                sp.wait_ge(evicted, n + 5)
                                sp.dma_start(y_dram[o, :, ds(g * GT, GT)], y[o % NR][:]).then_inc(y_out[o % NR], 16)
                            sp.wait_ge(prod, n + 3)
                            sp.sem_inc(stood, 1)
                            sp.dma_start(h_dram[o, :, ds(g * GT, GT)], h[o % NR][:]).then_inc(h_out[o % NR], 16)
                        if not last:
                            sp.wait_ge(summed, g * FT + FT)
                            load_x(g + 2, v)

                with sp.Fori(0, NG // 2 - 1) as i:
                    step(i, False)
                step(NG // 2 - 1, True)
                for j in range(NR):
                    sp.wait_ge(y_out[j], 16 * NG * sum(1 for o in range(RES, FT) if o % NR == j))
                    sp.wait_ge(h_out[j], 16 * NG * FT // NR)

            @block.tensor
            def _(pe):
                with pe.Fori(0, NG // 2) as i:
                    for v in range(2):
                        g = i * 2 + v
                        pe.wait_ge(x_in[v], i * 32 + 32)
                        part = lambda t, k: t[v][:, k * GT:(k + 1) * GT]
                        for o in range(FT):
                            pe.wait_ge(evicted, g * FT + o + 1)
                            split_matmuls(nc, acc[o % 4][:], [(a[:, o, k, :], part(b, k)) for k in range(KT)
                                                              for a, b in ((hi, xh), (hi, xl), (lo, xh))]).then_inc(summed, 1)

            @block.scalar
            def _(act):
                act.sem_inc(evicted, 4)

                def front(n, o, i, v):
                    count = (i * 2 + v) * (16 * FT // NR) + o // NR * 16 + 16
                    act.wait_ge(g_in[o % NR], count)
                    act.wait_ge(deq, n + 1)
                    nc.scalar.activation(ra[o % 2][:], ga[o % NR][:], ACT.Identity, scale=isg[:, 0:1], bias=magic[:, 0:1]).then_inc(added, 1)

                act.wait_ge(ready, 3)
                front(0, 0, 0, 0)
                with act.Fori(0, NG // 2) as i:
                    for v in range(2):
                        g = i * 2 + v
                        for o in range(FT):
                            n = g * FT + o
                            front(n + 1, o + 1, i, v)
                            act.wait_ge(deq, n + 3)
                            act.wait_ge(inc, n + 1)
                            nc.scalar.activation(sa[o % 2][:], qa[o % NR][:], ACT.Sigmoid, scale=65536.0).then_inc(sig, 1)
                            act.wait_ge(summed, n + 1)
                            if o < RES:
                                out = res[:, ds(g * GT + o * T, GT)]
                            else:
                                act.wait_ge(ymaxed, n + 1)
                                act.wait_ge(y_out[o % NR], g * (16 * y_stores(FT + o % NR)) + 16 * y_stores(o))
                                out = y[o % NR][:]
                            nc.scalar.activation(out, acc[o % 4][:], ACT.Copy, scale=yscale[:, 0:1]).then_inc(evicted, 1)

            @block.gpsimd
            def _(pool):
                pool.sem_inc(inc, 2)
                pool.sem_inc(prod, 2)

                def product(g, o):
                    n = g * FT + o
                    pool.wait_ge(clipped, n + 1)
                    pool.wait_ge(h_out[o % NR], g * (16 * FT // NR) + o // NR * 16)
                    pool.wait_ge(hmaxed, n + 1)
                    nc.gpsimd.tensor_tensor(h[o % NR][:], sq[o % 2][:], qa[o % NR][:], ALU.mult).then_inc(prod, 1)

                with pool.Fori(0, NG // 2) as i:
                    for v in range(2):
                        g = i * 2 + v
                        for o in range(FT):
                            n = g * FT + o
                            pool.wait_ge(sig, n + 1)
                            pool.wait_ge(prod, n + 1)
                            pool.sem_inc(stood, 1)
                            nc.gpsimd.tensor_scalar(sq[o % 2][:], sa[o % 2][:], 65536.0, MAGIC, ALU.mult, ALU.add).then_inc(inc, 1)
                            if v or o:
                                product(*((g, o - 1) if o else (i * 2, FT - 1)))
                    product(i * 2 + 1, FT - 1)

            @block.vector
            def _(dve):
                dve.sem_inc(deq, 2)
                dve.sem_inc(ymaxed, 4)
                dve.sem_inc(hmaxed, 4)
                nc.vector.memset(magic[:], MAGIC).then_inc(ready, 1)
                nc.vector.tensor_scalar(yscale[:], scale[:], 1.0 / FSCALE, None, ALU.mult).then_inc(ready, 1)
                nc.vector.tensor_scalar(gscale[:], sg[:], 1.0 / 65536.0, None, ALU.mult).then_inc(ready, 1)
                dve.wait_ge(ready, 3)

                def front(n, o):
                    dve.wait_ge(added, n + 1)
                    nc.vector.tensor_scalar(qa[o % NR][:], ra[o % 2][:], -MAGIC, gscale[:, 0:1], ALU.add, ALU.mult).then_inc(deq, 1)

                def hreduce(n, o):
                    dve.wait_ge(prod, n + 3)
                    nc.vector.tensor_reduce(htmax[:, ds(n, 1)], h[o % NR][:], AX.X, ALU.max, apply_absolute_value=True).then_inc(hmaxed, 1)

                front(0, 0)
                with dve.Fori(0, NG // 2) as i:
                    for v in range(2):
                        g = i * 2 + v
                        for o in range(FT):
                            n = g * FT + o
                            front(n + 1, o + 1)
                            dve.wait_ge(inc, n + 3)
                            nc.vector.tensor_scalar(sq[o % 2][:], sq[o % 2][:], -MAGIC, 65535.0, ALU.add, ALU.min).then_inc(clipped, 1)
                            dve.wait_ge(evicted, n + 5)
                            out = res[:, ds(g * GT + o * T, GT)] if o < RES else y[o % NR][:]
                            nc.vector.tensor_reduce(ytmax[:, ds(n, 1)], out, AX.X, ALU.max, apply_absolute_value=True).then_inc(ymaxed, 1)
                            m = v * FT + o - 2
                            if m >= 0:
                                hreduce(i * (2 * FT) + m, m % FT)
                    for m in (2 * FT - 2, 2 * FT - 1):
                        hreduce(i * (2 * FT) + m, m % FT)
                dve.wait_ge(ymaxed, FT * NG + 4)
                nc.vector.tensor_reduce(ymax[:], ytmax[:], AX.X, ALU.max).then_inc(done, 1)
                dve.wait_ge(hmaxed, FT * NG + 4)
                nc.vector.tensor_reduce(hmax[:], htmax[:], AX.X, ALU.max).then_inc(done, 1)
                dve.wait_ge(done, 2)


def product_phase(nc, h_dram, y_dram, res, ish, isu, o_dram, omax):
    W, NR = 1024, 4
    TR = T // W
    flat = lambda t: t.rearrange("f p t -> (f p) t")
    with ExitStack() as ctx:
        kit = Kit(nc, ctx)
        h = [kit.sb(f"j_h{j}", [P, W], F32) for j in range(NR)]
        u = [kit.sb(f"j_u{j}", [P, W], F32) for j in range(NR)]
        o = [kit.sb(f"j_o{j}", [P, W], F32) for j in range(NR)]
        magic = kit.sb("j_magic", [P, 1], F32)
        tmax = kit.sb("j_tmax", [P, FT * TR], F32)
        h_in, u_in, stored = ([kit.sem(f"j_{n}{j}") for j in range(NR)] for n in ("h_in", "u_in", "out"))
        ready, added, cut, prod, maxed, done, stood = (kit.sem(f"j_{n}") for n in ("ready", "added", "cut", "prod", "maxed", "done", "stood"))
        with nc.Block() as block:
            @block.sync
            def _(sp):
                def load(f, j, up):
                    sp.dma_start(h[j][:], flat(h_dram)[ds(f * P, P), j * W:(j + 1) * W]).then_inc(h_in[j], 16)
                    if up:
                        sp.dma_start(u[j][:], flat(y_dram)[ds(f * P, P), j * W:(j + 1) * W]).then_inc(u_in[j], 16)

                for j in range(NR):
                    load(0, j, False)
                for f in range(RES):
                    for j in range(NR):
                        sp.wait_ge(prod, f * NR + j + 1)
                        load(f + 1, j, f + 1 >= RES)

                def store(f, last):
                    for j in range(NR):
                        sp.wait_ge(prod, f * NR + (j + 1))
                        if not last:
                            load(f + 1, j, True)
                        sp.dma_start(flat(o_dram)[ds(f * P, P), j * W:(j + 1) * W], o[j][:]).then_inc(stored[j], 16)

                with sp.Fori(RES, FT - 1) as f:
                    store(f, False)
                store(FT - 1, True)
                for j in range(NR):
                    sp.wait_ge(stored[j], 16 * (FT - RES))

            def over_rows(eng, body):
                for f in range(RES):
                    for j in range(TR):
                        body(f, j, True)
                with eng.Fori(RES, FT) as f:
                    for j in range(TR):
                        body(f, j, False)

            def up_tile(f, j, resident):
                return res[:, f * T + j * W:f * T + (j + 1) * W] if resident else u[j][:]

            @block.scalar
            def _(act):
                act.wait_ge(ready, 1)

                def body(f, j, resident):
                    act.wait_ge(h_in[j], f * 16 + 16)
                    nc.scalar.activation(h[j][:], h[j][:], ACT.Identity, scale=ish[:, 0:1], bias=magic[:, 0:1]).then_inc(added, 1)
                    if not resident:
                        act.wait_ge(u_in[j], (f - RES) * 16 + 16)
                    nc.scalar.activation(up_tile(f, j, resident), up_tile(f, j, resident), ACT.Identity,
                                         scale=isu[:, 0:1], bias=magic[:, 0:1]).then_inc(added, 1)
                over_rows(act, body)

            @block.gpsimd
            def _(pool):
                def body(f, j, resident):
                    pool.wait_ge(added, (f * TR + j) * 2 + 2)
                    pool.sem_inc(stood, 1)
                    nc.gpsimd.tensor_scalar(up_tile(f, j, resident), up_tile(f, j, resident), 1.0, -MAGIC, ALU.mult, ALU.add).then_inc(cut, 1)
                over_rows(pool, body)

            @block.vector
            def _(dve):
                nc.vector.memset(magic[:], MAGIC).then_inc(ready, 1)

                def body(f, j, resident):
                    n = f * TR + j
                    dve.wait_ge(cut, n + 1)
                    if resident:
                        out = up_tile(f, j, True)
                    else:
                        out = o[j][:]
                        dve.wait_ge(stored[j], (f - RES) * 16)
                    nc.vector.scalar_tensor_tensor(out=out, in0=h[j][:], scalar=-MAGIC, in1=up_tile(f, j, resident),
                                                   op0=ALU.add, op1=ALU.mult).then_inc(prod, 1)
                    dve.wait_ge(prod, n + 1)
                    nc.vector.tensor_reduce(tmax[:, ds(n, 1)], out, AX.X, ALU.max, apply_absolute_value=True).then_inc(maxed, 1)

                over_rows(dve, body)
                dve.wait_ge(maxed, FT * TR)
                nc.vector.tensor_reduce(omax[:], tmax[:], AX.X, ALU.max).then_inc(done, 1)
                dve.wait_ge(done, 1)


def product_quantiser(nc, omax, sh, su, so, iso):
    with ExitStack() as ctx:
        kit = Kit(nc, ctx)
        amax, unit, inv = (kit.sb(f"qo_{n}", [P, 1], F32) for n in ("amax", "unit", "inv"))
        reduced, steps = kit.sem("qo_reduced"), kit.sem("qo_steps")
        with nc.Block() as block:
            @block.gpsimd
            def _(pool):
                nc.gpsimd.partition_all_reduce(amax[:], omax[:], P, RMAX).then_inc(reduced, 1)

            @block.vector
            def _(dve):
                nc.vector.tensor_tensor(unit[:], sh[:], su[:], ALU.mult).then_inc(steps, 1)
                dve.wait_ge(reduced, 1)
                dve.wait_ge(steps, 1)
                nc.vector.tensor_tensor(amax[:], amax[:], unit[:], ALU.mult).then_inc(steps, 1)
                dve.wait_ge(steps, 2)
                nc.vector.tensor_scalar(so[:], amax[:], 1.0 / QMAX, 1e-12, ALU.mult, ALU.max).then_inc(steps, 1)
                dve.wait_ge(steps, 3)
                nc.vector.reciprocal(inv[:], so[:]).then_inc(steps, 1)
                dve.wait_ge(steps, 4)
                nc.vector.tensor_tensor(iso[:], inv[:], unit[:], ALU.mult).then_inc(steps, 1)
                dve.wait_ge(steps, 5)


def down_phase(nc, o_dram, res, so, iso, wd, x2_dram, out):
    with ExitStack() as ctx:
        kit = Kit(nc, ctx)
        o32 = [kit.sb(f"d_o{v}", [P, FT - RES, GT], F32) for v in range(2)]
        r32 = [kit.sb(f"d_t{j}", [P, GT], F32) for j in range(3)]
        oh = [kit.sb(f"d_oh{v}", [P, FT, GT], F16) for v in range(2)]
        ol = [kit.sb(f"d_ol{v}", [P, FT, GT], F16) for v in range(2)]
        xt = [kit.sb(f"d_x{j}", [P, D], F32) for j in range(2)]
        rs = [kit.sb(f"d_r{j}", [P, D], F32) for j in range(2)]
        magic, ysc = kit.sb("d_magic", [P, 1], F32), kit.sb("d_ysc", [P, 1], F32)
        norm = Norm(kit, "n3")
        acc = [kit.ps(f"d_acc{j}", [P, D]) for j in range(2)]
        o_in = [kit.sem(f"d_in{v}") for v in range(2)]
        x_in = [kit.sem(f"d_x_in{j}") for j in range(2)]
        f_out = [kit.sem(f"d_out{j}") for j in range(2)]
        ready, rounded, hi_done, lo_done, summed, added, normed = (kit.sem(f"d_{n}") for n in (
            "ready", "rounded", "hi", "lo", "summed", "added", "normed"))
        wh, wl = wd
        with nc.Block() as block:
            @block.sync
            def _(sp):
                def load_o(g, v):
                    sp.dma_start(o32[v][:], o_dram[RES:FT, :, ds(g * GT, GT)].rearrange("f p t -> p f t")).then_inc(o_in[v], 16)

                for v in range(2):
                    load_o(v, v)
                for j in range(2):
                    sp.dma_start(xt[j][:], x2_dram[j * P:(j + 1) * P, :]).then_inc(x_in[j], 16)
                def step(i, last):
                    for v in range(2):
                        g = i * 2 + v
                        sp.wait_ge(rounded, g * FT + FT)
                        if not last or v == 0:
                            load_o((g + 2) % NG, v)
                        for tt in range(TG):
                            n = g * TG + tt
                            sp.wait_ge(added, n + 3)
                            if not (last and v == 1 and tt >= TG - 2):
                                sp.dma_start(xt[tt % 2][:], x2_dram[ds((n + 2) * P, P), :]).then_inc(x_in[tt % 2], 16)
                            sp.wait_ge(normed, n + 1)
                            sp.dma_start(out[ds(n * P, P), :], rs[tt % 2][:]).then_inc(f_out[tt % 2], 16)

                with sp.Fori(0, NG // 2 - 1) as i:
                    step(i, False)
                step(NG // 2 - 1, True)
                for v in range(2):
                    sp.wait_ge(f_out[v], 16 * T // P // 2)

            @block.tensor
            def _(pe):
                with pe.Fori(0, NG // 2) as i:
                    for v in range(2):
                        g = i * 2 + v
                        for tt in range(TG):
                            pe.wait_ge(added, g * TG + tt + 1)
                            t = slice(tt * P, (tt + 1) * P)
                            n = 0
                            for k in range(FT):
                                if tt == 0:
                                    pe.wait_ge(lo_done, g * FT + k + 1)
                                for a, b in ((oh[v], wh), (oh[v], wl), (ol[v], wh)):
                                    mm = nc.tensor.matmul(acc[tt % 2][:], a[:, k, t], b[:, k, :], start=(n == 0), stop=(n == 3 * FT - 1))
                                    n += 1
                            mm.then_inc(summed, 1)

            @block.scalar
            def _(act):
                act.wait_ge(ready, 2)

                def round_row(g, v, f):
                    act.wait_ge(lo_done, g * FT + max(f - 2, 0))
                    src = res[:, ds(g % NG * GT + f * T, GT)] if f < RES else o32[v][:, f - RES]
                    nc.scalar.activation(r32[f % 3][:], src, ACT.Identity, scale=iso[:, 0:1], bias=magic[:, 0:1]).then_inc(rounded, 1)

                act.wait_ge(o_in[0], 16)
                for f in range(FT):
                    round_row(0, 0, f)
                with act.Fori(0, NG // 2) as i:
                    for v in range(2):
                        g = i * 2 + v
                        act.wait_ge(o_in[1 - v], (i + v) * 16 + 16)
                        for tt in range(TG):
                            for f in range(tt * 3, tt * 3 + 3):
                                round_row(g + 1, 1 - v, f)
                            norm.square_root(nc, act, g * TG + tt, tt % 2)

            @block.vector
            def _(dve):
                dve.sem_inc(added, 2)
                nc.vector.memset(magic[:], MAGIC).then_inc(ready, 1)
                nc.vector.tensor_scalar(ysc[:], so[:], 1.0 / FSCALE, None, ALU.mult).then_inc(ready, 1)
                dve.wait_ge(ready, 2)

                def split(n0, v, f):
                    dve.wait_ge(rounded, n0 + f + 1)
                    nc.vector.tensor_scalar(oh[v][:, f], r32[f % 3][:], -MAGIC, None, ALU.add).then_inc(hi_done, 1)
                    dve.wait_ge(hi_done, n0 + f + 1)
                    nc.vector.scalar_tensor_tensor(out=ol[v][:, f], in0=r32[f % 3][:], scalar=-MAGIC, in1=oh[v][:, f],
                                                   op0=ALU.add, op1=ALU.subtract).then_inc(lo_done, 1)

                for f in range(FT):
                    split(0, 0, f)
                with dve.Fori(0, NG // 2) as i:
                    for v in range(2):
                        g = i * 2 + v
                        dve.wait_ge(summed, g * TG)
                        for tt in range(TG):
                            n, j = g * TG + tt, tt % 2
                            for f in range(tt * 3, tt * 3 + 3):
                                split((g + 1) * FT, 1 - v, f)
                            dve.wait_ge(summed, n + 1)
                            dve.wait_ge(f_out[j], g * 32 + tt // 2 * 16)
                            dve.wait_ge(x_in[j], g * (16 * TG // 2) + (tt // 2 * 16 + 16))
                            nc.vector.scalar_tensor_tensor(out=rs[j][:], in0=acc[j][:], scalar=ysc[:, 0:1], in1=xt[j][:],
                                                           op0=ALU.mult, op1=ALU.add).then_inc(added, 1)
                            dve.wait_ge(added, n + 3)
                            norm.statistics(nc, dve, n, j, rs[j][:])
                            norm.scale(nc, dve, n, j, rs[j][:], rs[j][:]).then_inc(normed, 1)


def feed_forward(nc, c, attn2, x1_dram, w_dram, scratch, out):
    x2_dram = scratch("scr_x2", [T, D], F32)
    x_dram = [scratch(f"scr_xq_{n}", [NG, P, KT * GT], F16) for n in ("hi", "lo")]
    gate_dram, up_dram, h_dram, o_dram = (scratch(f"scr_{n}", [FT, P, T], F32) for n in ("gate", "up", "h", "o"))
    with ExitStack() as ctx:
        kit = Kit(nc, ctx)
        names = ("x", "gate", "up", "h", "o")
        pmax, scale, inverse = ({n: kit.sb(f"{k}_{n}", [P, 1], F32) for n in names} for k in ("pmax", "scale", "inverse"))
        of = lambda n: (pmax[n], scale[n], inverse[n])
        wd = [kit.sb(f"wd_{n}", [P, FT, D], F16) for n in ("hi", "lo")]
        res = kit.sb("rows", [P, RES * T], F32)
        x2 = res[:, 0:T // P * D]
        with ExitStack() as up_scope:
            wu = [Kit(nc, up_scope).sb(f"wu_{n}", [P, FT, KT, P], F16) for n in ("hi", "lo")]
            with ExitStack() as gate_scope:
                wg = [Kit(nc, gate_scope).sb(f"wg_{n}", [P, FT, KT, P], F16) for n in ("hi", "lo")]
                tiles = lambda w, m: [(w[j][:].rearrange("p t k n -> p t (k n)"), w_dram[j][m * FT:(m + 1) * FT].rearrange("t p n -> p t n"))
                                      for j in range(2)]
                down_tiles = [(wd[j][:, k * KT:(k + 1) * KT, r * P:(r + 1) * P], w_dram[j][2 * FT + r * 3 + k].rearrange("p (q n) -> p q n", n=P))
                              for j in range(2) for r in range(KT) for k in range(3)]
                second_norm_phase(nc, attn2, x1_dram, x2, x2_dram, pmax["x"], tiles(wg, 0))
                quantisers(nc, "qx", [of("x")])
                gate_phase(nc, c, x2, scale["x"], inverse["x"], wg, gate_dram, x_dram, pmax["gate"], tiles(wu, 1) + down_tiles)
            quantisers(nc, "qg", [of("gate")])
            up_phase(nc, x_dram, scale["x"], wu, gate_dram, scale["gate"], inverse["gate"], up_dram, res, h_dram,
                     pmax["up"], pmax["h"])
        quantisers(nc, "quh", [of("up"), of("h")])
        product_phase(nc, h_dram, up_dram, res, inverse["h"], inverse["up"], o_dram, pmax["o"])
        product_quantiser(nc, pmax["o"], scale["h"], scale["up"], scale["o"], inverse["o"])
        down_phase(nc, o_dram, res, scale["o"], inverse["o"], wd, x2_dram, out)


def decoder_layer(nc, x, context, mask, Wq, bq, Wk, bk, Wv, bv, Wf, bf, w_gate, w_up, w_down, out):
    x = x.rearrange("b s d -> (b s) d")
    context = context.rearrange("b s d -> (b s) d")
    mask = mask.rearrange("b o q k -> (b o q) k")
    out = out.rearrange("b s d -> (b s) d")

    def scratch(name, shape, dt):
        return nc.dram_tensor(name, shape, dt).ap()

    qk_dram = [scratch(f"scr_{n}", [B, D, S], F16) for n in ("q_hi", "q_lo", "k_hi", "k_lo")]
    q2_dram = [scratch(f"scr_q2_{n}", [B, D, S], F16) for n in ("hi", "lo")]
    k2_dram = [scratch(f"scr_k2_{n}", [B, D, S], F16) for n in ("hi", "lo")]
    v_dram, v2_dram = scratch("scr_v", [B * H, P, ST, VW], F16), scratch("scr_v2", [B * H, P, ST, VW], F16)
    mb_dram, nm_dram = scratch("scr_mb", [T, S], BF16), scratch("scr_nm", [B, S, S], F16)
    w_dram = [scratch(f"scr_w_{n}", [3 * FT, P, KT * P], F16) for n in ("hi", "lo")]
    attn, attn2, x1_dram = (scratch(n, [T, D], F32) for n in ("scr_attn", "scr_attn2", "scr_x1"))

    with ExitStack() as ctx:
        c = make_identities(nc, Kit(nc, ctx))
        preparation_phase(nc, c, x, Wq, bq, Wk, bk, Wv, bv, qk_dram, v_dram, context, k2_dram, v2_dram,
                          mask, mb_dram, nm_dram, (w_gate, w_up, w_down), w_dram)
        attention_phase(nc, c, "self", True, qk_dram[0:2], qk_dram[2:4], v_dram, attn)
        projection_phase(nc, c, attn, x, Wf, bf, x1_dram, q2_dram)
        attention_phase(nc, c, "cross", False, q2_dram, k2_dram, v2_dram, attn2, mb_dram, nm_dram)
        feed_forward(nc, c, attn2, x1_dram, w_dram, scratch, out)


_INS = ["x", "ctx_1024", "mask_Bx1xSxS2_ik1", "L0_attn_Wq", "L0_attn_bq", "L0_attn_Wk", "L0_attn_bk", "L0_attn_Wv",
        "L0_attn_bv", "L0_attn_Wf", "L0_attn_bf", "L0_ffn_w_gate", "L0_ffn_w_up", "L0_ffn_w_down"]


def kernel(**inputs):
    import concourse.bacc as bacc
    from concourse.bass_utils import run_bass_kernel_spmd

    nc = bacc.Bacc("TRN2", target_bir_lowering=False, num_devices=1)
    arrays, args = {}, []
    for name in _INS:
        a = np.ascontiguousarray(inputs[name])
        arrays[f"in_{name}"] = a
        args.append(nc.dram_tensor(f"in_{name}", a.shape, mybir.dt.from_np(a.dtype), kind="ExternalInput").ap())
    args.append(nc.dram_tensor("out_0", (B, S, D), F32, kind="ExternalOutput").ap())
    decoder_layer(nc, *args)
    r = run_bass_kernel_spmd(nc, [arrays], core_ids=[0])
    return r.results[0]["out_0"]
```
